# Optimizing a Trainium2 kernel written in Bass

```python
import numpy as np
import jax
import jax.numpy as jnp

def _softmax(x, axis=-1):
    return jax.nn.softmax(x, axis=axis)

def _gelu(x):
    return jax.nn.gelu(x, approximate=True)

def _silu(x):
    return jax.nn.silu(x)

def _sigmoid(x):
    return jax.nn.sigmoid(x)

def _layernorm(x, axis=-1, eps=1e-05):
    m = jnp.mean(x, axis=axis, keepdims=True)
    v = jnp.var(x, axis=axis, keepdims=True)
    return (x - m) / jnp.sqrt(v + eps)

def _scatter_add(tgt, idx, src, axis=0):
    return tgt.at[idx].add(src)

def _segment_sum(src, seg, n):
    return jax.ops.segment_sum(src, seg, n)
kernel_name = 'mk_flamingo_gated_d1_seqx_r4_0f3247'

def setup_inputs(seed: int=0):
    np.random.seed(seed)
    _w = jnp.asarray

    def _rec_inputs():
        import jax
        import jax.numpy as jnp
        _rk = jax.random.key(seed)
        x = -0.0003929 + 0.9999 * jax.random.normal(jax.random.fold_in(_rk, 1), (16, 112, 256), jnp.float32)
        _lenS = 112 - jax.random.randint(jax.random.fold_in(_rk, 7), (16,), 0, max(1, 112 // 4) + 1, jnp.int32)
        _lenS2 = 375 - jax.random.randint(jax.random.fold_in(_rk, 8), (16,), 0, max(1, 375 // 4) + 1, jnp.int32)
        _ctx_768P = jax.random.normal(jax.random.fold_in(_rk, 11), (16, 16, 192), jnp.float32)
        _ctx_768c = jax.random.dirichlet(jax.random.fold_in(_rk, 511), 0.3 * jnp.ones((16,), jnp.float32), (16, 375))
        _ctx_768t = jnp.einsum('bsk,bkd->bsd', _ctx_768c, _ctx_768P)
        _ctx_768t = _ctx_768t * jax.lax.rsqrt(jnp.mean(jnp.square(_ctx_768t)) + 1e-12) * 0.953939
        ctx_768 = 0.00095986 + 0.999812 * (_ctx_768t + 0.3 * jax.random.normal(jax.random.fold_in(_rk, 611), (16, 375, 192), jnp.float32))
        _validS = jnp.arange(112)[None, :] < _lenS[:, None]
        _validS2 = jnp.arange(375)[None, :] < _lenS2[:, None]
        _causal = jnp.tril(jnp.ones((112, 112), dtype=bool))
        mask_BxS2_bf1 = jnp.ones((16, 375), dtype=bool)
        _g = jax.random.normal(jax.random.fold_in(_rk, 9001), (2, 1), jnp.float32)
        _g = jnp.sign(_g) * jnp.maximum(jnp.abs(_g), 1.0) + (_g == 0) * 1.0
        g_xattn = _g[0]
        g_ffn = _g[1]
        return (x, ctx_768, mask_BxS2_bf1, g_xattn, g_ffn)
    x, ctx_768, mask_BxS2_bf1, g_xattn, g_ffn = _rec_inputs()

    def _L0_xattn_setup():
        import jax, jax.numpy as jnp
        import numpy as np
        DIM = 256
        CTX_DIM = 192
        HEADS = 16
        key = jax.random.key(seed)
        ks = jax.random.split(key, 7)
        B, N, M = (4, 1024, 64)
        x = jax.random.normal(ks[0], (B, N, DIM), dtype=jnp.float32)
        context = jax.random.normal(ks[1], (B, M, CTX_DIM), dtype=jnp.float32)
        context_mask = jnp.ones((B, M), dtype=bool)
        s_d = 1.0 / np.sqrt(DIM)
        s_c = 1.0 / np.sqrt(CTX_DIM)
        Wq = jax.random.normal(ks[2], (DIM, DIM), dtype=jnp.float32) * s_d
        Wk = jax.random.normal(ks[3], (CTX_DIM, DIM), dtype=jnp.float32) * s_c
        Wv = jax.random.normal(ks[4], (CTX_DIM, DIM), dtype=jnp.float32) * s_c
        Wo = jax.random.normal(ks[5], (DIM, DIM), dtype=jnp.float32) * s_d
        return {'x': x, 'context': context, 'context_mask': context_mask, 'Wq': Wq, 'Wk': Wk, 'Wv': Wv, 'Wo': Wo}
    _L0_xattn_all = _L0_xattn_setup()
    _L0_xattn_in = {k: v for k, v in _L0_xattn_all.items() if k in ('Wq', 'Wk', 'Wv', 'Wo')}
    del _L0_xattn_all

    def _L0_ffn_setup():
        import jax, jax.numpy as jnp
        import numpy as np
        D_MODEL, D_FF, N_EXPERTS, TOP_K = (256, 512, 8, 2)
        B, S = (2, 512)
        key = jax.random.key(seed)
        ks = jax.random.split(key, 6)
        sd = 1.0 / np.sqrt(D_MODEL)
        sf = 1.0 / np.sqrt(D_FF)
        return {'x': jax.random.normal(ks[0], (B, S, D_MODEL), jnp.float32), 'router_w': jax.random.normal(ks[1], (N_EXPERTS, D_MODEL), jnp.float32) * sd, 'gate_w': jax.random.normal(ks[2], (N_EXPERTS, D_MODEL, D_FF), jnp.float32) * sd, 'gate_b': jnp.zeros((N_EXPERTS, D_FF), jnp.float32), 'up_w': jax.random.normal(ks[3], (N_EXPERTS, D_MODEL, D_FF), jnp.float32) * sd, 'up_b': jnp.zeros((N_EXPERTS, D_FF), jnp.float32), 'down_w': jax.random.normal(ks[4], (N_EXPERTS, D_FF, D_MODEL), jnp.float32) * sf, 'down_b': jnp.zeros((N_EXPERTS, D_MODEL), jnp.float32)}
    _L0_ffn_all = _L0_ffn_setup()
    _L0_ffn_in = {k: v for k, v in _L0_ffn_all.items() if k in ('router_w', 'gate_w', 'gate_b', 'up_w', 'up_b', 'down_w', 'down_b')}
    del _L0_ffn_all
    return {'x': x, 'ctx_768': ctx_768, 'mask_BxS2_bf1': mask_BxS2_bf1, 'g_xattn': g_xattn, 'g_ffn': g_ffn, 'L0_xattn_Wq': _L0_xattn_in['Wq'], 'L0_xattn_Wk': _L0_xattn_in['Wk'], 'L0_xattn_Wv': _L0_xattn_in['Wv'], 'L0_xattn_Wo': _L0_xattn_in['Wo'], 'L0_ffn_router_w': _L0_ffn_in['router_w'], 'L0_ffn_gate_w': _L0_ffn_in['gate_w'], 'L0_ffn_gate_b': _L0_ffn_in['gate_b'], 'L0_ffn_up_w': _L0_ffn_in['up_w'], 'L0_ffn_up_b': _L0_ffn_in['up_b'], 'L0_ffn_down_w': _L0_ffn_in['down_w'], 'L0_ffn_down_b': _L0_ffn_in['down_b']}

def reference(x, ctx_768, mask_BxS2_bf1, g_xattn, g_ffn, L0_xattn_Wq, L0_xattn_Wk, L0_xattn_Wv, L0_xattn_Wo, L0_ffn_router_w, L0_ffn_gate_w, L0_ffn_gate_b, L0_ffn_up_w, L0_ffn_up_b, L0_ffn_down_w, L0_ffn_down_b):
    import jax
    import jax.numpy as jnp

    def _L0_xattn_ref(x, context, context_mask, Wq, Wk, Wv, Wo):
        import jax, jax.numpy as jnp
        import numpy as np
        DIM = 256
        CTX_DIM = 192
        HEADS = 16
        B, N, _ = x.shape
        M = context.shape[1]
        hd = DIM // HEADS
        scale = hd ** (-0.5)
        q = (x @ Wq).reshape(B, N, HEADS, hd).transpose(0, 2, 1, 3)
        k = (context @ Wk).reshape(B, M, HEADS, hd).transpose(0, 2, 1, 3)
        v = (context @ Wv).reshape(B, M, HEADS, hd).transpose(0, 2, 1, 3)
        scores = jnp.einsum('bhid,bhjd->bhij', q, k) * scale
        max_neg = -jnp.finfo(scores.dtype).max
        scores = jnp.where(context_mask[:, None, None, :], scores, max_neg)
        attn = jax.nn.softmax(scores, axis=-1)
        out = jnp.einsum('bhij,bhjd->bhid', attn, v)
        out = out.transpose(0, 2, 1, 3).reshape(B, N, DIM)
        return out @ Wo

    def _L0_ffn_ref(x, router_w, gate_w, gate_b, up_w, up_b, down_w, down_b):
        import jax, jax.numpy as jnp
        import numpy as np
        D_MODEL, D_FF, N_EXPERTS, TOP_K = (256, 512, 8, 2)
        B, S = (2, 512)
        b, s, d = x.shape
        xf = x.reshape(b * s, d)
        n = xf.shape[0]
        router_logits = xf @ router_w.T
        probs = jax.nn.softmax(router_logits, axis=-1)
        topv, topi = jax.lax.top_k(probs, TOP_K)
        mask = jnp.zeros_like(probs).at[jnp.arange(n)[:, None], topi].set(1.0)
        probs = probs * mask
        probs = probs / (probs.sum(axis=-1, keepdims=True) + 1e-09)
        g = jnp.einsum('nd,edf->nef', xf, gate_w) + gate_b
        u = jnp.einsum('nd,edf->nef', xf, up_w) + up_b
        h = jax.nn.silu(g) * u
        expert_out = jnp.einsum('nef,efd->ned', h, down_w) + down_b
        y = jnp.einsum('ne,ned->nd', probs, expert_out)
        return y.reshape(b, s, d)
    x = x + jnp.tanh(g_xattn[0]) * _L0_xattn_ref(_layernorm(x, axis=-1), ctx_768, mask_BxS2_bf1, L0_xattn_Wq, L0_xattn_Wk, L0_xattn_Wv, L0_xattn_Wo)
    x = x + jnp.tanh(g_ffn[0]) * _L0_ffn_ref(_layernorm(x, axis=-1), L0_ffn_router_w, L0_ffn_gate_w, L0_ffn_gate_b, L0_ffn_up_w, L0_ffn_up_b, L0_ffn_down_w, L0_ffn_down_b)
    return x

_drawn_inputs = setup_inputs


def setup_inputs(seed=0):
    import zlib

    import numpy as np

    out = dict(_drawn_inputs(seed))
    spreads = {'L0_ffn_gate_b': (0.0, 0.1), 'L0_ffn_up_b': (0.0, 0.1), 'L0_ffn_down_b': (0.0, 0.1)}
    factors = {}
    for name, (base, spread) in spreads.items():
        noise = np.random.default_rng([zlib.crc32(name.encode()), seed]).standard_normal(out[name].shape)
        drawn = base * np.exp(spread * noise) if base else spread * noise
        out[name] = jnp.asarray(drawn.astype(out[name].dtype))
    for name, factor in factors.items():
        out[name] = (out[name] * factor).astype(out[name].dtype)
    return out
```

```python
from contextlib import ExitStack

import concourse.bass as bass
from concourse import mybir

F32 = mybir.dt.float32
F32R = mybir.dt.float32r
BF16 = mybir.dt.bfloat16
F16 = mybir.dt.float16
U8 = mybir.dt.uint8
ALU = mybir.AluOpType
ACT = mybir.ActivationFunctionType
AX = mybir.AxisListType

HEADS = 16
PAIRS = HEADS // 2
LN_EPS = 1e-5
HIDDEN = float(2.0 ** 126)


def f32(ap):
    return ap.bitcast(F32)


def build(nc, x, ctx_768, mask, g_xattn, g_ffn, Wq, Wk, Wv, Wo, router_w, gate_w, gate_b, up_w, up_b,
          down_w, down_b, out):
    B, N, DIM = x.shape
    M, CTX = ctx_768.shape[1], ctx_768.shape[2]
    HD = DIM // HEADS
    JT = 3
    JP = M // JT
    MP = M + M % 2
    CK = CTX // 2
    GB = 4
    GROUPS = B // GB
    NI = 128
    VW = 3 * HD + 1
    RB, RM = 96, 97
    SCALE = HD ** -0.5

    q_scr = nc.dram_tensor("q_scr", [2, B, DIM, N], F32, kind="Internal").ap()
    k_scr = nc.dram_tensor("k_scr", [2, 2, DIM, MP], F32, kind="Internal").ap()
    bias_scr = nc.dram_tensor("bias_scr", [B, MP], F32, kind="Internal").ap()

    E = gate_w.shape[0]
    TOP_K = 2
    NT = TOP_K * B * N // 128 + E - 1
    ROWW = DIM + 1
    xs_scr = nc.dram_tensor("xs_scr", [NT * 128, ROWW], F32, kind="Internal").ap()
    y_scr = nc.dram_tensor("y_scr", [TOP_K * B * N + NT * 128, DIM], F32, kind="Internal").ap()

    with ExitStack() as whole:
        def keep(name, shape, dt):
            return whole.enter_context(nc.sbuf_tensor(name, shape, dt))

        def sem(name):
            return whole.enter_context(nc.semaphore(name))

        X = keep("X", [N, B, DIM], F32)
        ident = keep("ident", [128, 128], F32)
        gates = keep("gates", [128, 2], F32)
        tg = keep("tg", [128, 2], F32)
        banks = [whole.enter_context(nc.psum_tensor(f"bank{i}", [128, 512], F32)) for i in range(6)]
        misc = whole.enter_context(nc.psum_tensor("misc", [128, 1024], F32))
        psS, psST, psO = banks[0:2], banks[2:4], banks[4:6]

        attention(nc, locals())
        experts(nc, locals())


def attention(nc, v):
    (x, ctx_768, mask, Wq, Wk, Wv, Wo, X, ident, gates, tg, psS, psST, psO, misc) = (
        v[k] for k in "x ctx_768 mask Wq Wk Wv Wo X ident gates tg psS psST psO misc".split())
    (B, N, DIM, M, HD, JT, JP, MP, CK, GB, GROUPS, NI, VW, RB, RM, SCALE) = (
        v[k] for k in "B N DIM M HD JT JP MP CK GB GROUPS NI VW RB RM SCALE".split())
    q_scr, k_scr, bias_scr = v["q_scr"], v["k_scr"], v["bias_scr"]
    CTX = 2 * CK

    with ExitStack() as stack:
        def sb(name, shape, dt):
            return stack.enter_context(nc.sbuf_tensor(name, shape, dt))

        def sem(name):
            return stack.enter_context(nc.semaphore(name))

        shapes = {"q": (Wq, 128), "k": (Wk, CK), "v": (Wv, CK), "o": (Wo, 128)}
        Wf = {k: sb(f"w{k}_f", [p, 2, DIM], F32) for k, (_, p) in shapes.items()}
        WH = {k: sb(f"w{k}_h", [p, 2, DIM], F32R) for k, (_, p) in shapes.items()}
        WL = {k: sb(f"w{k}_l", [p, 2, DIM], F32R) for k, (_, p) in shapes.items()}
        mask_sb = sb("mask_sb", [B, M], U8)
        bias_sb = sb("bias_sb", [B, MP], F32)
        stats = sb("stats", [N, B, 6], F32)
        mv = sb("mv", [N, B, 2], F32)
        rstd = sb("rstd", [N, B], F32)
        veps = sb("veps", [N, B], F32)
        xn = sb("xn", [N, GB, DIM], F32)
        xTH = sb("xTH", [128, 2, GB * N], F32R)
        xTL = sb("xTL", [128, 2, GB * N], F32R)
        qH = sb("qH", [128, 2, GB * N], F32R)
        qL = sb("qL", [128, 2, GB * N], F32R)
        ctx_sb = sb("ctx_sb", [JP, 2, JT, CTX], F32)
        cTH = sb("cTH", [CK, 2, MP], F32R)
        cTL = sb("cTL", [CK, 2, MP], F32R)
        kH = sb("kH", [128, 2, 2, MP], F32R)
        kL = sb("kL", [128, 2, 2, MP], F32R)
        KS = [sb(f"KS{u}", [128, PAIRS, MP], F32R) for u in range(2)]
        QS = [sb(f"QS{u}", [128, PAIRS, 2, NI], F32R) for u in range(2)]
        vf = sb("vf", [JP, 2, JT, DIM], F32)
        vr = sb("vr", [JP, JT, DIM], F32)
        VS = sb("VS", [JP, 2, JT, HEADS, VW], BF16)
        zero = sb("zero", [JP, 1], F32)
        mx = sb("mx", [N, HEADS], F32)
        nm = sb("nm", [HEADS, N], F32R)
        UN = PAIRS * JT
        PT = sb("PT", [JP, UN, 2, NI], F32)
        PL = sb("PL", [JP, UN, 2, NI], F16)
        PH = PT[:].rearrange("p u e i -> p (u e i)").bitcast(BF16).rearrange(
            "p (u e i two) -> p u e i two", u=UN, e=2, two=2)[:, :, :, :, 1]
        osum = sb("osum", [N, HEADS, HD], F32)
        rden = sb("rden", [N, HEADS], F32)
        on = sb("on", [N, HEADS, HD], F32)
        oTH = sb("oTH", [128, 2, N], F32R)
        oTL = sb("oTL", [128, 2, N], F32R)

        s_w, s_x, s_g, s_m = sem("weights_in"), sem("x_in"), sem("gates_in"), sem("mask_in")
        s_id0, s_id = sem("ident_zero"), sem("ident_ready")
        s_clear, s_wh, s_wl, s_bias = sem("cleared"), sem("w_high"), sem("w_low"), sem("bias_ready")
        s_st, s_mv, s_ve, s_sq, s_rs = (sem(n) for n in ("ln_stats", "ln_mv", "ln_veps", "ln_sqrt", "ln_rstd"))
        s_xn, s_xt, s_xh, s_xl = sem("xn_ready"), sem("xT_ready"), sem("xT_high"), sem("xT_low")
        s_qp, s_qh, s_ql, s_qw = sem("q_psum"), sem("q_high"), sem("q_low"), sem("q_written")
        FT = 5
        fill = sb("fill", [128, FT, v["ROWW"]], F32)
        s_f0, s_f1, s_fw = sem("fill_zero"), sem("fill_ids"), sem("fill_written")
        s_bw, s_tg = sem("bias_written"), sem("tanh_ready")

        def groups(eng, group):
            group(0)
            with eng.Fori(1, GROUPS) as g:
                group(g)

        later = lambda g: not isinstance(g, int) or g > 0

        with nc.Block() as block:
            @block.sync
            def _(sp):
                sp.dma_start(X[:], x.rearrange("b i d -> i b d")).then_inc(s_x, 16)
                for k, (w, p) in shapes.items():
                    sp.dma_start(Wf[k][:], w.rearrange("(c p) n -> p c n", p=p)).then_inc(s_w, 16)
                sp.dma_start(mask_sb[:], mask).then_inc(s_m, 16)
                for j, g in enumerate((v["g_xattn"], v["g_ffn"])):
                    sp.dma_start(gates[:, j:j + 1], g.rearrange("(o a) -> o a", o=1).to_broadcast([128, 1])
                                 ).then_inc(s_g, 16)
                sp.wait_ge(s_bias, 1)
                sp.wait_ge(s_clear, 3)
                sp.dma_start(bias_scr, bias_sb[:]).then_inc(s_bw, 16)
                def group(g):
                    sp.wait_ge(s_ql, g + 1)
                    for part, t in ((0, qH), (1, qL)):
                        for c in range(2):
                            sp.dma_start(
                                q_scr[part, bass.ds(g * GB, GB), c * 128:(c + 1) * 128, :].rearrange("b p i -> p b i"),
                                f32(t[:, c, :]).rearrange("p (b i) -> p b i", b=GB)).then_inc(s_qw, 16)
                groups(sp, group)
                sp.wait_ge(s_qw, 64 * GROUPS)
                sp.wait_ge(s_bw, 16)

            @block.gpsimd
            def _(pool):
                pool.memset(ident[:], 0.0).then_inc(s_id0, 1)
                pool.wait_ge(s_id0, 1)
                pool.affine_select(out=ident[:], in_=ident[:], compare_op=ALU.not_equal, fill=1.0, base=0,
                                   pattern=[[-1, 128]], channel_multiplier=1).then_inc(s_id, 1)
                pool.wait_ge(s_id, 1)
                parts = [(f32(cTH[:, :, M:MP]), 0.0), (f32(cTL[:, :, M:MP]), 0.0), (bias_sb[:, M:MP], 0.0), (zero[:], 0.0),
                         (PT[:, :, :, N:NI], 0.0), (PL[:, :, :, N:NI], 0.0),
                         (VS[:, :, :, :, VW - 1:VW].rearrange("p u t h o -> p (u t) h o"), 1.0)]
                for u in range(2):
                    parts += [(f32(QS[u][0:96]), 0.0), (f32(QS[u][96:128]), 1.0), (f32(KS[u][96:128]), 1.0)]
                for n, (part, value) in enumerate(parts):
                    pool.memset(part, value).then_inc(s_clear, 1)
                    pool.wait_ge(s_clear, n + 1)

                pool.memset(fill[:], 0.0).then_inc(s_f0, 1)
                pool.wait_ge(s_f0, 1)
                for n in range(v["NT"] // FT):
                    if n:
                        pool.wait_ge(s_fw, 16 * n)
                    pool.iota(fill[:, :, DIM:DIM + 1].rearrange("p t o -> p (t o)").bitcast(mybir.dt.int32),
                              pattern=[[128, FT]], base=2 * B * N + 128 * FT * n, channel_multiplier=1).then_inc(s_f1, 1)
                    pool.wait_ge(s_f1, n + 1)
                    pool.dma_start(v["xs_scr"][128 * FT * n:128 * FT * (n + 1), :].rearrange("(t p) w -> p t w", p=128),
                                   fill[:]).then_inc(s_fw, 16)
                pool.wait_ge(s_fw, 16 * (v["NT"] // FT))

            @block.scalar
            def _(act):
                act.wait_ge(s_g, 32)
                act.activation(tg[:], gates[:], ACT.Tanh).then_inc(s_tg, 1)
                act.wait_ge(s_w, 64)
                for k in shapes:
                    act.activation(WH[k][:], Wf[k][:], ACT.Copy, scale=SCALE if k == "q" else 1.0
                                   ).then_inc(s_wh, 1)
                act.wait_ge(s_ve, 1)
                act.activation(rstd[:], veps[:], ACT.Sqrt).then_inc(s_sq, 1)
                def group(g):
                    act.wait_ge(s_xt, g + 1)
                    act.activation(xTH[:], misc[:].rearrange("p (c n) -> p c n", c=2)[:, :, 0:GB * N], ACT.Copy
                                   ).then_inc(s_xh, 1)
                    act.wait_ge(s_qp, g + 1)
                    if later(g):
                        act.wait_ge(s_qw, 64 * g)
                    for c in range(2):
                        act.activation(qH[:, c, :], psS[c][:, 0:GB * N], ACT.Copy).then_inc(s_qh, 1)

                groups(act, group)

            @block.tensor
            def _(pe):
                pe.wait_ge(s_id, 1)
                pe.wait_ge(s_wl, 4)
                def group(g):
                    pe.wait_ge(s_xn, g + 1)
                    if later(g):
                        pe.wait_ge(s_xl, g)
                    for c in range(2):
                        for b in range(GB):
                            mm = pe.transpose(misc[:, c * 512 + b * N:c * 512 + (b + 1) * N],
                                              xn[:, b, c * 128:(c + 1) * 128], ident[0:N, 0:N])
                    mm.then_inc(s_xt, 1)
                    pe.wait_ge(s_xl, g + 1)
                    if later(g):
                        pe.wait_ge(s_ql, g)
                    for m in range(2):
                        for n, (w, r) in enumerate(((WH, xTH), (WL, xTH), (WH, xTL))):
                            for c in range(2):
                                mm = pe.matmul(psS[m][:, 0:GB * N], w["q"][:, c, m * 128:(m + 1) * 128], r[:, c, :],
                                               start=(n == 0 and c == 0), stop=(n == 2 and c == 1))
                    mm.then_inc(s_qp, 1)

                groups(pe, group)

            @block.vector
            def _(dve):
                for n, k in enumerate(shapes):
                    dve.wait_ge(s_wh, n + 1)
                    dve.scalar_tensor_tensor(out=WL[k][:], in0=Wf[k][:], scalar=SCALE if k == "q" else 1.0,
                                             in1=f32(WH[k][:]), op0=ALU.mult, op1=ALU.subtract).then_inc(s_wl, 1)
                dve.wait_ge(s_m, 16)
                dve.tensor_scalar(bias_sb[:, 0:M].rearrange("b (t p) -> b t p", t=JT),
                                  mask_sb[:].rearrange("b (p t) -> b t p", t=JT),
                                  -1.0, HIDDEN, ALU.add, ALU.mult).then_inc(s_bias, 1)
                dve.wait_ge(s_x, 16)
                layer_norm_stats(dve, X, stats, mv, veps, rstd, B, s_st, s_mv, s_ve, s_sq, s_rs)
                def group(g):
                    if later(g):
                        dve.wait_ge(s_xt, g)
                    for b in range(GB):
                        nb = g * GB + b
                        ins = dve.tensor_scalar(xn[:, b, :], X[:, bass.ds(nb, 1), :],
                                                mv[:, bass.ds(nb, 1), 0:1], rstd[:, bass.ds(nb, 1)],
                                                ALU.subtract, ALU.mult)
                    ins.then_inc(s_xn, 1)
                    dve.wait_ge(s_xh, g + 1)
                    dve.tensor_tensor(xTL[:], misc[:].rearrange("p (c n) -> p c n", c=2)[:, :, 0:GB * N],
                                      f32(xTH[:]), ALU.subtract).then_inc(s_xl, 1)
                    dve.wait_ge(s_qh, 2 * g + 2)
                    for c in range(2):
                        ins = dve.tensor_tensor(qL[:, c, :], psS[c][:, 0:GB * N], f32(qH[:, c, :]), ALU.subtract)
                    ins.then_inc(s_ql, 1)

                groups(dve, group)

        two = lambda name: [sem(f"{name}{u}") for u in range(2)]
        d_ctx, d_kw, d_ks, d_qs, d_m = two("ctx_in"), two("k_out"), two("ks_in"), two("qs_in"), two("m_in")
        p_T, p_K, p_V, p_S, p_mT = (sem(n) for n in ("pe_ctxT", "pe_k", "pe_v", "pe_scores", "pe_maxT"))
        p_ST, p_PV, p_OT, p_Wo = (sem(n) for n in ("pe_scoresT", "pe_pv", "pe_oT", "pe_wo"))
        a_T, a_K, a_V, a_V1, a_E, a_O = (sem(n) for n in ("act_ctxT", "act_k", "act_v", "act_v1", "act_exp", "act_oT"))
        v_T, v_K, v_L, v_max, v_nm = (sem(n) for n in ("dve_ctxT", "dve_k", "dve_plow", "dve_max", "dve_negmax"))
        v_os, v_rd, v_on, v_O, v_x1 = (sem(n) for n in ("dve_osum", "dve_rden", "dve_on", "dve_oT", "dve_x1"))
        g_1, g_r, g_V, g_L = (sem(n) for n in ("pool_v1", "pool_rest", "pool_v", "pool_plow"))

        SB = UN // 2
        POOL = [k for k in (1, 4, 6, 9, 11) if k < SB]
        vec = lambda k: sum(j not in POOL for j in range(k + 1))
        pol = lambda k: sum(j in POOL for j in range(k + 1))
        last_bank = lambda p: (JT * p + JT - 1) // 2
        pv_at = {last_bank(p) + 3: p for p in range(PAIRS)}
        SLOTS = max(pv_at) + 1
        heads_at = {2: (0, 1), 3: (2, 3), 4: (4, 5), 5: (6, 7), 6: (8, 9), 7: (10, 11), 8: (12, 13), 9: (14,), 10: (15,)}
        MT, CT, VP, OP = 11, 10, 4, 7

        def at(i, c):
            return 2 * i + c, i + c // 2, c % 2

        def steps(eng, step):
            first, last = 4, B - 3
            for n in range(first):
                step(0, n)
            with eng.Fori(first // 2, (last + 1) // 2) as i:
                step(i, 0)
                step(i, 1)
            for n in range(last + 1, B + 3):
                step(0, n)

        def live(i, c, back):
            return not isinstance(i, int) or 0 <= 2 * i + c - back < B

        def wait(eng, s, value):
            if not isinstance(value, int) or value > 0:
                eng.wait_ge(s, value)

        with nc.Block() as block:
            @block.sync
            def _(sp):
                def load_ctx(i, c):
                    b, h, u = at(i, c)
                    wait(sp, p_T, b - 1)
                    sp.dma_start(ctx_sb[:, u, :, :], ctx_768[bass.ds(b, 1), :, :].rearrange("o (p t) d -> p (o t) d", t=JT)
                                 ).then_inc(d_ctx[u], 16)

                def step(i, c):
                    if live(i, c, -2):
                        load_ctx(i, c + 2)
                    if live(i, c, 0):
                        b, h, u = at(i, c)
                        sp.wait_ge(v_K, b + 1)
                        for part, t in ((0, kH), (1, kL)):
                            sp.dma_start(k_scr[u, part].rearrange("(m p) j -> p m j", p=128), f32(t[:, u])
                                         ).then_inc(d_kw[u], 16)
                    if live(i, c, 1):
                        b, h, u = at(i, c - 1)
                        sp.wait_ge(v_nm, b + 1)
                        sp.dma_start(f32(QS[u][RM:RM + 1, :, :, 0:N]).rearrange("o q e i -> o (q e) i"),
                                     f32(nm[:])).then_inc(d_m[u], 16)
                    if live(i, c, 0):
                        b, h, u = at(i, c)
                        wait(sp, p_ST, SB * (b - 1))
                        for s, part in enumerate((0, 1, 0)):
                            for e in range(2):
                                sp.dma_start(
                                    f32(QS[u][32 * s + HD * e:32 * s + HD * e + HD, :, e, 0:N]),
                                    q_scr[part, bass.ds(b, 1)].rearrange("o (q e r) i -> e r (o q) i", e=2, r=HD)[e]
                                ).then_inc(d_qs[u], 16)
                        sp.dma_start(f32(KS[u][RB:RB + 1, :, :]),
                                     bias_scr[bass.ds(b, 1), :].unsqueeze(1).to_broadcast([1, PAIRS, MP])
                                     ).then_inc(d_ks[u], 16)
                        sp.wait_ge(d_kw[u], 32 * (h + 1))
                        for s, part in enumerate((0, 0, 1)):
                            sp.dma_start(f32(KS[u][32 * s:32 * s + 32, :, :]),
                                         k_scr[u, part].rearrange("(q r) j -> r q j", r=32)).then_inc(d_ks[u], 16)

                load_ctx(0, 0)
                load_ctx(0, 1)
                steps(sp, step)

            @block.gpsimd
            def _(pool):
                def low(i, c, k):
                    b, h, u = at(i, c - 2)
                    pool.wait_ge(a_E, SB * b + k + 1)
                    pool.tensor_tensor(PL[:, 2 * k:2 * k + 2, :, 0:N], PT[:, 2 * k:2 * k + 2, :, 0:N],
                                       PH[:, 2 * k:2 * k + 2, :, 0:N], ALU.subtract).then_inc(g_L, 1)

                def values(i, c):
                    b, h, u = at(i, c - 1)
                    part = lambda k: VS[:, u, :, :, HD * k:HD * (k + 1)]
                    head = lambda t: t[:].rearrange("p t (h d) -> p t h d", d=HD)
                    pool.wait_ge(a_V1, b + 1)
                    wait(pool, g_V, b)
                    pool.tensor_tensor(head(vr), vf[:, u].rearrange("p t (h d) -> p t h d", d=HD), part(0), ALU.subtract).then_inc(g_r, 1)
                    pool.wait_ge(g_r, b + 1)
                    pool.tensor_tensor(part(1), head(vr), zero[:].unsqueeze(2).unsqueeze(3).to_broadcast([JP, JT, HEADS, HD]),
                                       ALU.add).then_inc(g_1, 1)
                    pool.wait_ge(g_1, b + 1)
                    pool.tensor_tensor(part(2), head(vr), part(1), ALU.subtract).then_inc(g_V, 1)

                def step(i, c):
                    for k in POOL:
                        if live(i, c, 2):
                            low(i, c, k)
                    if live(i, c, 1):
                        values(i, c)

                steps(pool, step)

            @block.scalar
            def _(act):
                def transposed(i, c):
                        b, h, u = at(i, c)
                        act.wait_ge(p_T, b + 1)
                        wait(act, p_V, b)
                        act.activation(cTH[:, :, 0:M], misc[0:CK].rearrange("p (c n) -> p c n", c=2)[:, :, 0:M],
                                       ACT.Copy).then_inc(a_T, 1)

                def step(i, c):
                    if live(i, c, 3):
                        b, h, u = at(i, c - 3)
                        act.wait_ge(p_OT, b + 1)
                        wait(act, p_Wo, b)
                        act.activation(oTH[:], psS[0][:, 0:2 * N].rearrange("p (c i) -> p c i", c=2),
                                       ACT.Copy).then_inc(a_O, 1)
                    for k in range(SLOTS):
                        if k == CT + 1 and live(i, c, -1):
                            transposed(i, c + 1)
                        if k < SB and live(i, c, 2):
                            b, h, u = at(i, c - 2)
                            act.wait_ge(p_ST, SB * b + k + 1)
                            wait(act, p_PV, PAIRS * (b - 1) + (2 * k + 1) // JT + 1)
                            act.activation(PT[:, 2 * k:2 * k + 2, :, 0:N].rearrange("p a e i -> p (a e) i"),
                                           psST[k % 2][0:JP].rearrange("p (a i) -> p a i", i=NI)[:, :, 0:N],
                                           ACT.Exp).then_inc(a_E, 1)
                        if k == 7 and live(i, c, 1):
                            b, h, u = at(i, c - 1)
                            act.wait_ge(a_V, b + 1)
                            wait(act, p_PV, PAIRS * (b - 1))
                            act.activation(VS[:, u, :, :, 0:HD].rearrange("p t h d -> p (t h) d"),
                                           vf[:, u].rearrange("p t (h d) -> p (t h) d", d=HD), ACT.Copy).then_inc(a_V1, 1)
                        if k == 1 and live(i, c, 0):
                            b, h, u = at(i, c)
                            act.wait_ge(p_K, b + 1)
                            wait(act, d_kw[u], 32 * h)
                            act.activation(kH[:, u], misc[:].rearrange("p (m n) -> p m n", m=2)[:, :, 0:MP],
                                           ACT.Copy).then_inc(a_K, 1)
                        if k == VP + 1 and live(i, c, 0):
                            b, h, u = at(i, c)
                            act.wait_ge(p_V, b + 1)
                            wait(act, g_r, b - 1)
                            act.activation(vf[:, u].rearrange("p t n -> p (t n)"), misc[0:JP, 0:JT * DIM], ACT.Copy
                                           ).then_inc(a_V, 1)

                transposed(0, 0)
                steps(act, step)

            @block.tensor
            def _(pe):
                def ctx_T(i, c):
                    b, h, u = at(i, c)
                    pe.wait_ge(d_ctx[u], 16 * (h + 1))
                    wait(pe, a_V, b)
                    wait(pe, v_x1, b - 3)
                    for k in range(2):
                        for t in range(JT):
                            mm = pe.transpose(misc[0:CK, 512 * k + JP * t:512 * k + JP * (t + 1)],
                                              ctx_sb[:, u, t, CK * k:CK * (k + 1)], ident[0:JP, 0:JP])
                    mm.then_inc(p_T, 1)

                def project_k(i, c):
                    b, h, u = at(i, c)
                    pe.wait_ge(v_T, b + 1)
                    for m in range(2):
                        for n, (w, r) in enumerate(((WH, cTH), (WL, cTH), (WH, cTL))):
                            for k in range(2):
                                mm = pe.matmul(misc[:, 512 * m:512 * m + MP], w["k"][:, k, m * 128:(m + 1) * 128],
                                               r[:, k, :], start=(n == 0 and k == 0), stop=(n == 2 and k == 1))
                    mm.then_inc(p_K, 1)

                def project_v(i, c):
                    b, h, u = at(i, c)
                    pe.wait_ge(v_K, b + 1)
                    for t in range(JT):
                        for n, (w, r) in enumerate(((WH, cTH), (WL, cTH), (WH, cTL))):
                            for k in range(2):
                                mm = pe.matmul(misc[0:JP, DIM * t:DIM * (t + 1)], r[:, k, JP * t:JP * (t + 1)],
                                               w["v"][:, k, :], start=(n == 0 and k == 0), stop=(n == 2 and k == 1))
                    mm.then_inc(p_V, 1)

                def scores(i, c, hd):
                    b, h, u = at(i, c - 1)
                    if hd == 0:
                        pe.wait_ge(d_ks[u], 64 * (h + 1))
                        pe.wait_ge(d_qs[u], 96 * (h + 1))
                        wait(pe, v_O, b - 1)
                    if hd == 1:
                        wait(pe, v_nm, b)
                    wait(pe, v_max, HEADS * b + hd - 1)
                    pe.matmul(psS[hd % 2][0:N, 0:MP], QS[u][0:RM, hd // 2, hd % 2, 0:N], KS[u][0:RM, hd // 2, :],
                              start=True, stop=True).then_inc(p_S, 1)

                def max_T(i, c):
                    b, h, u = at(i, c - 1)
                    pe.wait_ge(v_max, HEADS * (b + 1))
                    pe.transpose(psS[1][0:HEADS, 0:N], mx[:], ident[0:N, 0:N]).then_inc(p_mT, 1)

                def scores_T(i, c, k):
                    b, h, u = at(i, c - 2)
                    if k == 0:
                        pe.wait_ge(d_m[u], 16 * (h + 1))
                    wait(pe, a_E, SB * b + k - 1)
                    for a in range(2):
                        p, t = divmod(2 * k + a, JT)
                        mm = pe.matmul(psST[k % 2][0:JP, 2 * NI * a:2 * NI * (a + 1)],
                                       KS[u][0:RM + 1, p, JP * t:JP * (t + 1)],
                                       QS[u][0:RM + 1, p, :, :].rearrange("r e i -> r (e i)"), start=True, stop=True)
                    mm.then_inc(p_ST, 1)

                def sums(i, c, p):
                    b, h, u = at(i, c - 2)
                    if p == 0:
                        pe.wait_ge(g_V, b + 1)
                    if p % 4 == 0:
                        wait(pe, v_os, 2 * (b - 1) + p // 4 + 1)
                    k = last_bank(p)
                    pe.wait_ge(v_L, vec(SB - 1) * b + vec(k))
                    pe.wait_ge(g_L, pol(SB - 1) * b + pol(k))
                    for e in range(2):
                        hd = 2 * p + e
                        for part, P in enumerate((PH, PL)):
                            for t in range(JT):
                                mm = pe.matmul(psO[hd // 8][:, VW * (hd % 8):VW * (hd % 8 + 1)], P[:, JT * p + t, e, :],
                                               VS[:, u, t, hd, :], start=(part == 0 and t == 0),
                                               stop=(part == 1 and t == JT - 1))
                    mm.then_inc(p_PV, 1)

                def out_T(i, c):
                    b, h, u = at(i, c - 3)
                    pe.wait_ge(v_on, 2 * b + 2)
                    pe.wait_ge(v_max, HEADS * min(b + 2, B) if isinstance(b, int) else HEADS * (b + 2))
                    for k in range(2):
                        mm = pe.transpose(psS[0][:, N * k:N * (k + 1)],
                                          on[:, 8 * k:8 * k + 8, :].rearrange("i h d -> i (h d)"), ident[0:N, 0:N])
                    mm.then_inc(p_OT, 1)

                def project_o(i, c):
                    b, h, u = at(i, c - 3)
                    pe.wait_ge(v_O, b + 1)
                    if live(i, c, 0):
                        pe.wait_ge(a_V, b + 4)
                    for n, (w, r) in enumerate(((WH, oTH), (WL, oTH), (WH, oTL))):
                        for k in range(2):
                            mm = pe.matmul(misc[0:N, 0:DIM], r[:, k, :], w["o"][:, k, :],
                                           start=(n == 0 and k == 0), stop=(n == 2 and k == 1))
                    mm.then_inc(p_Wo, 1)

                def step(i, c):
                    if live(i, c, 3):
                        out_T(i, c)
                    for s in range(SLOTS):
                        heads = heads_at.get(s, ()) if live(i, c, 1) else ()
                        if s < SB and live(i, c, 2):
                            scores_T(i, c, s)
                        if s == 1 and live(i, c, 0):
                            project_k(i, c)
                        for hd in heads[0:1]:
                            scores(i, c, hd)
                        if s in pv_at and live(i, c, 2):
                            sums(i, c, pv_at[s])
                        if s == VP and live(i, c, 0):
                            project_v(i, c)
                        if s == OP and live(i, c, 3):
                            project_o(i, c)
                        for hd in heads[1:2]:
                            scores(i, c, hd)
                        if s == MT and live(i, c, 1):
                            max_T(i, c)
                        if s == CT and live(i, c, -1):
                            ctx_T(i, c + 1)

                ctx_T(0, 0)
                steps(pe, step)

            @block.vector
            def _(dve):
                def low(i, c, k):
                    b, h, u = at(i, c - 2)
                    dve.wait_ge(a_E, SB * b + k + 1)
                    dve.tensor_tensor(PL[:, 2 * k:2 * k + 2, :, 0:N].rearrange("p a e i -> p (a e) i"),
                                      PT[:, 2 * k:2 * k + 2, :, 0:N].rearrange("p a e i -> p (a e) i"),
                                      PH[:, 2 * k:2 * k + 2, :, 0:N].rearrange("p a e i -> p (a e) i"),
                                      ALU.subtract).then_inc(v_L, 1)

                def maximum(i, c, hd):
                    b, h, u = at(i, c - 1)
                    dve.wait_ge(p_S, HEADS * b + hd + 1)
                    if hd == 0:
                        wait(dve, p_mT, b)
                    dve.tensor_reduce(mx[:, hd:hd + 1], psS[hd % 2][0:N, 0:M], AX.X, ALU.max).then_inc(v_max, 1)

                def normalise(i, c, half):
                    b, h, u = at(i, c - 2)
                    dve.wait_ge(p_PV, PAIRS * b + 4 * half + 4)
                    hs = slice(8 * half, 8 * half + 8)
                    o = psO[half][0:N, 0:8 * VW].rearrange("i (h w) -> i h w", w=VW)
                    dve.reciprocal(rden[:, hs], o[:, :, VW - 1]).then_inc(v_rd, 1)
                    dve.tensor_reduce(osum[:, hs, :], o[:, :, 0:3 * HD].rearrange("i h (k d) -> i h d k", k=3),
                                      AX.X, ALU.add).then_inc(v_os, 1)
                    dve.wait_ge(v_rd, 2 * b + half + 1)
                    dve.wait_ge(v_os, 2 * b + half + 1)
                    wait(dve, p_OT, b)
                    dve.tensor_tensor(on[:, hs, :], osum[:, hs, :],
                                      rden[:, hs].unsqueeze(2).to_broadcast([N, 8, HD]),
                                      ALU.mult).then_inc(v_on, 1)

                def transposed(i, c):
                    b, h, u = at(i, c)
                    dve.wait_ge(a_T, b + 1)
                    dve.tensor_tensor(cTL[:, :, 0:M], misc[0:CK].rearrange("p (c n) -> p c n", c=2)[:, :, 0:M],
                                      f32(cTH[:, :, 0:M]), ALU.subtract).then_inc(v_T, 1)

                def step(i, c):
                    if live(i, c, 3):
                        b, h, u = at(i, c - 3)
                        dve.wait_ge(a_O, b + 1)
                        dve.tensor_tensor(oTL[:], psS[0][:, 0:2 * N].rearrange("p (c i) -> p c i", c=2),
                                          f32(oTH[:]), ALU.subtract).then_inc(v_O, 1)
                    for s in range(SLOTS):
                        heads = heads_at.get(s, ()) if live(i, c, 1) else ()
                        for hd in heads[0:1]:
                            maximum(i, c, hd)
                        if 0 < s <= SB and s - 1 not in POOL and live(i, c, 2):
                            low(i, c, s - 1)
                        if s == 2 and live(i, c, 0):
                            b, h, u = at(i, c)
                            dve.wait_ge(a_K, b + 1)
                            dve.tensor_tensor(kL[:, u], misc[:].rearrange("p (m n) -> p m n", m=2)[:, :, 0:MP],
                                              f32(kH[:, u]), ALU.subtract).then_inc(v_K, 1)
                        for hd in heads[1:2]:
                            maximum(i, c, hd)
                        if s == MT and live(i, c, 1):
                            b, h, u = at(i, c - 1)
                            dve.wait_ge(p_mT, b + 1)
                            if not isinstance(i, int) or b > 0:
                                b1, h1, u1 = at(i, c - 2)
                                dve.wait_ge(d_m[u1], 16 * (h1 + 1))
                            dve.tensor_scalar(nm[:], psS[1][0:HEADS, 0:N], -1.0, None, ALU.mult
                                              ).then_inc(v_nm, 1)
                        if s == OP + 1 and live(i, c, 3):
                            b, h, u = at(i, c - 3)
                            dve.wait_ge(p_Wo, b + 1)
                            dve.scalar_tensor_tensor(out=X[:, bass.ds(b, 1), :], in0=misc[0:N, 0:DIM].unsqueeze(1),
                                                     scalar=tg[0:N, 0:1],
                                                     in1=X[:, bass.ds(b, 1), :], op0=ALU.mult, op1=ALU.add
                                                     ).then_inc(v_x1, 1)
                        if s == pv_slot(3) + 1 and live(i, c, 2):
                            normalise(i, c, 0)
                        if s == CT + 1 and live(i, c, -1):
                            transposed(i, c + 1)
                    if live(i, c, 2):
                        normalise(i, c, 1)

                pv_slot = lambda p: last_bank(p) + 3
                transposed(0, 0)
                steps(dve, step)


def experts(nc, v):
    (B, N, DIM, X, ident, tg, banks, misc, out) = (v[k] for k in "B N DIM X ident tg banks misc out".split())
    router_w, gate_w, gate_b, up_w, up_b, down_w, down_b = (
        v[k] for k in "router_w gate_w gate_b up_w up_b down_w down_b".split())
    xs_scr, y_scr, NT, ROWW = v["xs_scr"], v["y_scr"], v["NT"], v["ROWW"]
    E, FF = gate_w.shape[0], gate_w.shape[2]
    FC, DC = FF // 128, DIM // 128
    I32 = mybir.dt.int32
    XS = 2.0 ** 10
    WS = 2.0 ** 14

    with ExitStack() as stack:
        def sb(name, shape, dt):
            return stack.enter_context(nc.sbuf_tensor(name, shape, dt))

        def sem(name):
            return stack.enter_context(nc.semaphore(name))

        GH = sb("GH", [128, E, 2, DC, FF], F16)
        GL = sb("GL", [128, E, 2, DC, FF], F16)
        DH = sb("DH", [128, E, FC, DIM], F32R)
        DL = sb("DL", [128, E, FC, DIM], F32R)
        inv = sb("inv", [128, E], F32)
        gb = sb("gb", [128, E * FC], F32)
        ub = sb("ub", [128, E * FC], F32)
        tw = sb("tw", [N, 2, B], F32)
        tile_e = sb("tile_e", [1, NT], I32)
        db = sb("db", [E, DIM], F32)

        with ExitStack() as inner:
            def tmp(name, shape, dt):
                return inner.enter_context(nc.sbuf_tensor(name, shape, dt))

            def isem(name):
                return inner.enter_context(nc.semaphore(name))

            xn = tmp("xn2", [N, B, ROWW], F32)
            stats = tmp("stats2", [N, B, 6], F32)
            mv = tmp("mv2", [N, B, 2], F32)
            rstd, veps = tmp("rstd2", [N, B], F32), tmp("veps2", [N, B], F32)
            rw, rwT = tmp("rw", [E, DIM], F32), tmp("rwT", [128, DC, E], F32)
            braw = tmp("braw", [E * FC, 2, 128], F32)
            xT = tmp("xT2", [128, 2, DC, N], F32)
            raw = tmp("w_raw", [128, 2, 2, DC, FF], F32)
            draw = tmp("d_raw", [128, 2, FC, DIM], F32)
            am, amax = tmp("am", [128, 2], F32), tmp("amax", [128, 2], F32)
            pw, sc = tmp("pw", [128, 4], F32), tmp("sc", [128, 2], F32)
            upper, ones = tmp("upper", [N, N], F32), tmp("ones2", [N, N], F32)
            R = {n: tmp("r_" + n, [N, B, E], F32) for n in
                 "low exp eq score sel1 rest sel2 both a0 a1 pos tie pick1 pick2 wsel".split()}
            r = {n: tmp("s_" + n, [N, B], F32) for n in
                 "m sum m1 t1 m2 t2 p1 p2 den rden rsum w1 w2 f1 f2".split()}
            pos = [tmp(f"pos{k}", [N, B], I32) for k in range(2)]
            c = {n: tmp("c_" + n, [N, E], F32) for n in "cnt pad e0 e1 base".split()}
            ci, ca = tmp("c_int", [N, E], I32), tmp("c_and", [N, E], I32)
            tie_i, start_i = tmp("tie_i", [N, B, E], I32), tmp("start_i", [1, NT, E], I32)
            start, past, nexp = tmp("start", [1, NT, E], F32), tmp("past", [1, NT, E], F32), tmp("nexp", [1, NT], F32)
            wselT = raw[0:E, 0].rearrange("p j c f -> p (j c f)")[:, 0:B * N].rearrange("p (b i) -> p b i", b=B)

            i_sm, i_w = isem("small_in"), [isem(f"w_in{u}") for u in range(2)]
            q_c, q_tri, q_iota, q_id, q_amax = (isem(n) for n in ("pool_clear", "tri", "iota", "ids", "amax_all"))
            q_sc = [isem(f"rows_out{k}") for k in range(2)]
            t_rw, t_x, t_lg, t_rank, t_w, t_wb = (isem(n) for n in
                                                  ("pe_rw", "pe_xT2", "pe_logits", "pe_rank", "pe_wselT", "pe_bias"))
            s_x, s_exp, s_h, s_sq = (isem(n) for n in ("act_xT2", "act_exp2", "act_high", "act_sqrt2"))
            e_rw, e_st, e_mv, e_ve, e_rs, e_xn = (isem(n) for n in
                                                  ("dve_rw", "dve_st2", "dve_mv2", "dve_ve2", "dve_rs2", "dve_xn2"))
            e_r, e_low, e_sel, e_pos, e_wt, e_am, e_sc, e_l, e_dl, e_X = (isem(n) for n in (
                "dve_chain", "dve_low", "dve_sel", "dve_pos", "dve_wselT", "dve_amax", "dve_scale", "dve_wlow",
                "dve_dlow", "dve_xbias"))
            e_ch = isem("dve_scale_chain")
            bX, bL, bR, bC = banks[0:2], banks[2], banks[3], banks[4]

            with nc.Block() as block:
                @block.sync
                def _(sp):
                    sp.dma_start(rw[:], router_w).then_inc(i_sm, 16)
                    for j, t in enumerate((gate_b, up_b)):
                        sp.dma_start(braw[:, j, :], t.rearrange("e (f p) -> (e f) p", p=128)).then_inc(i_sm, 16)
                    sp.dma_start(db[:], down_b).then_inc(i_sm, 16)

                    def load(i, u):
                        e = 2 * i + u
                        for j, w in enumerate((gate_w, up_w)):
                            sp.dma_start(raw[:, u, j], w[bass.ds(e, 1)].rearrange("o (c p) f -> p (o c) f", p=128)
                                         ).then_inc(i_w[u], 16)
                        sp.dma_start(draw[:, u], down_w[bass.ds(e, 1)].rearrange("o (f p) d -> p (o f) d", p=128)
                                     ).then_inc(i_w[u], 16)

                    load(0, 0)
                    load(0, 1)
                    with sp.Fori(1, E // 2) as i:
                        for u in range(2):
                            sp.wait_ge(e_l, 2 * i + u - 1)
                            sp.wait_ge(e_dl, 2 * i + u - 1)
                            load(i, u)

                @block.gpsimd
                def _(pool):
                    pool.memset(upper[:], 0.0).then_inc(q_c, 1)
                    pool.wait_ge(q_c, 1)
                    pool.affine_select(out=upper[:], in_=upper[:], compare_op=ALU.is_ge, fill=1.0, base=0,
                                       pattern=[[-1, N]], channel_multiplier=1).then_inc(q_tri, 1)
                    pool.wait_ge(q_tri, 1)
                    pool.memset(ones[:], 1.0).then_inc(q_tri, 1)
                    pool.wait_ge(q_tri, 2)
                    pool.iota(tie_i[:], pattern=[[0, B], [-1, E]], base=E, channel_multiplier=0).then_inc(q_iota, 1)
                    pool.wait_ge(q_iota, 1)
                    pool.iota(start_i[:], pattern=[[128, NT], [0, E]], base=0, channel_multiplier=0
                              ).then_inc(q_iota, 1)
                    pool.wait_ge(q_iota, 2)
                    for k in range(2):
                        if k:
                            pool.wait_ge(q_sc[0], 16 * B)
                        pool.iota(xn[:, :, DIM:ROWW].rearrange("i b o -> i (b o)").bitcast(I32),
                                  pattern=[[2 * N, B]], base=k, channel_multiplier=2).then_inc(q_id, 1)
                        pool.wait_ge(q_id, k + 1)
                        if k == 0:
                            pool.wait_ge(e_xn, 1)
                            pool.wait_ge(e_pos, 2)
                        for b in range(B):
                            pool.indirect_dma_start(
                                xs_scr, bass.IndirectOffsetOnAxis(ap=pos[k][:, b:b + 1].bitcast(mybir.dt.uint32), axis=0),
                                xn[:, b, :], None).then_inc(q_sc[k], 16)
                    for e in range(E):
                        u = e % 2
                        pool.wait_ge(e_am, e + 1)
                        pool.partition_all_reduce(amax[:, u:u + 1], am[:, u:u + 1], 128,
                                                  bass.bass_isa.ReduceOp.max).then_inc(q_amax, 1)
                    pool.wait_ge(q_sc[1], 16 * B)

                @block.scalar
                def _(act):
                    act.wait_ge(e_ve, 1)
                    act.activation(rstd[:], veps[:], ACT.Sqrt).then_inc(s_sq, 1)
                    for b in range(B):
                        u = b % 2
                        act.wait_ge(t_x, b + 1)
                        if b >= 2:
                            act.wait_ge(t_lg, b - 1)
                        act.activation(xT[:, u], bX[u][:, 0:DC * N].rearrange("p (c i) -> p c i", c=DC), ACT.Copy
                                       ).then_inc(s_x, 1)
                    act.wait_ge(e_low, 1)
                    act.activation(R["exp"][:], R["low"][:], ACT.Exp).then_inc(s_exp, 1)
                    with act.Fori(0, E // 2) as i:
                        for u in range(2):
                            e = 2 * i + u
                            act.wait_ge(e_sc, e + 1)
                            act.activation(GH[:, bass.ds(e, 1)].rearrange("p e j c f -> p (e j c f)"),
                                           raw[:, u].rearrange("p j c f -> p (j c f)"), ACT.Copy,
                                           scale=sc[:, u:u + 1]).then_inc(s_h, 1)
                            act.activation(DH[:, bass.ds(e, 1)].rearrange("p e f d -> p (e f d)"),
                                           draw[:, u].rearrange("p f d -> p (f d)"), ACT.Copy).then_inc(s_h, 1)

                @block.tensor
                def _(pe):
                    pe.wait_ge(i_sm, 64)
                    for k in range(DC):
                        pe.transpose(bC[:, E * k:E * (k + 1)], rw[:, 128 * k:128 * (k + 1)], ident[0:E, 0:E])
                    for j in range(2):
                        mm = pe.transpose(bC[:, 64 + 32 * j:64 + 32 * j + E * FC], braw[:, j, :],
                                          ident[0:E * FC, 0:E * FC])
                    mm.then_inc(t_rw, 1)
                    pe.wait_ge(e_rw, 3)
                    pe.wait_ge(e_xn, 1)

                    def turn(b):
                        if b >= 2:
                            pe.wait_ge(s_x, b - 1)
                        for k in range(DC):
                            mm = pe.transpose(bX[b % 2][:, N * k:N * (k + 1)], xn[:, b, 128 * k:128 * (k + 1)],
                                              ident[0:N, 0:N])
                        mm.then_inc(t_x, 1)

                    turn(0)
                    for b in range(B):
                        if b + 1 < B:
                            turn(b + 1)
                        pe.wait_ge(s_x, b + 1)
                        for k in range(DC):
                            mm = pe.matmul(bL[0:N, b * E:(b + 1) * E], xT[:, b % 2, k, :], rwT[:, k, :],
                                           start=(k == 0), stop=(k == DC - 1))
                        mm.then_inc(t_lg, 1)
                    pe.wait_ge(e_sel, 1)
                    pe.wait_ge(q_tri, 2)
                    flat = R["both"][:].rearrange("i b e -> i (b e)")
                    pe.matmul(bR[0:N, 0:B * E], upper[:], flat, start=True, stop=True)
                    pe.matmul(bR[0:N, 256:256 + B * E], ones[:], flat, start=True, stop=True).then_inc(t_rank, 1)
                    pe.wait_ge(e_pos, 3)
                    for g in range(B // 4):
                        if g >= 2:
                            pe.wait_ge(e_wt, g - 1)
                        for b in range(4):
                            mm = pe.transpose(bX[g % 2][0:E, N * b:N * (b + 1)], R["wsel"][:, 4 * g + b, :],
                                              ident[0:N, 0:N])
                        mm.then_inc(t_w, 1)
                    for b in range(B):
                        pe.wait_ge(e_wt, b // 4 + 1)
                        if b >= 2:
                            pe.wait_ge(e_X, b - 1)
                        else:
                            pe.wait_ge(e_wt, 4)
                        pe.matmul(bX[b % 2][0:N, 0:DIM], wselT[:, b, :], db[:], start=True, stop=True
                                  ).then_inc(t_wb, 1)

                @block.vector
                def _(dve):
                    n_chain = [0]

                    def link(ins):
                        n_chain[0] += 1
                        ins.then_inc(e_r, 1)
                        dve.wait_ge(e_r, n_chain[0])

                    dve.wait_ge(t_rw, 1)
                    dve.tensor_copy(rwT[:], bC[:, 0:DC * E].rearrange("p (c e) -> p c e", c=DC)).then_inc(e_rw, 1)
                    dve.tensor_copy(gb[:], bC[:, 64:64 + E * FC]).then_inc(e_rw, 1)
                    dve.tensor_copy(ub[:], bC[:, 96:96 + E * FC]).then_inc(e_rw, 1)
                    layer_norm_stats(dve, X, stats, mv, veps, rstd, B, e_st, e_mv, e_ve, s_sq, e_rs)
                    for b in range(B):
                        ins = dve.tensor_scalar(xn[:, b, 0:DIM], X[:, b, :], mv[:, b, 0:1], rstd[:, b:b + 1],
                                                ALU.subtract, ALU.mult)
                    ins.then_inc(e_xn, 1)
                    dve.wait_ge(q_iota, 2)
                    link(dve.tensor_copy(R["tie"][:], tie_i[:]))
                    link(dve.tensor_copy(start[:], start_i[:]))
                    dve.wait_ge(t_lg, B)
                    logits = bL[0:N, 0:B * E].rearrange("i (b e) -> i b e", e=E)
                    wide = lambda t: t[:].unsqueeze(2).to_broadcast([N, B, E])
                    link(dve.tensor_reduce(r["m"][:], logits, AX.X, ALU.max))
                    dve.tensor_tensor(R["low"][:], logits, wide(r["m"]), ALU.subtract).then_inc(e_low, 1)
                    dve.wait_ge(s_exp, 1)
                    link(dve.tensor_reduce(r["sum"][:], R["exp"][:], AX.X, ALU.add))
                    for k, src in ((1, R["exp"]), (2, R["rest"])):
                        mk, tk, sel = r[f"m{k}"], r[f"t{k}"], R[f"sel{k}"]
                        link(dve.tensor_reduce(mk[:], src[:], AX.X, ALU.max))
                        link(dve.tensor_tensor(R["eq"][:], src[:], wide(mk), ALU.is_equal))
                        link(dve.tensor_tensor(R["score"][:], R["eq"][:], R["tie"][:], ALU.mult))
                        link(dve.tensor_reduce(tk[:], R["score"][:], AX.X, ALU.max))
                        link(dve.tensor_tensor(sel[:], R["score"][:], wide(tk), ALU.is_equal))
                        if k == 1:
                            link(dve.scalar_tensor_tensor(out=R["rest"][:], in0=sel[:], scalar=-4.0, in1=src[:],
                                                          op0=ALU.mult, op1=ALU.add))
                    dve.tensor_tensor(R["both"][:], R["sel1"][:], R["sel2"][:], ALU.add).then_inc(e_sel, 1)
                    dve.wait_ge(t_rank, 1)
                    rank = bR[0:N, 0:B * E].rearrange("i (b e) -> i b e", e=E)
                    total = bR[0:N, 256:256 + B * E].rearrange("i (b e) -> i b e", e=E)
                    link(dve.tensor_copy(R["a0"][:], total))
                    a, b_ = R["a0"], R["a1"]
                    sh = 1
                    while sh < B:
                        link(dve.tensor_tensor(b_[:, sh:B, :], a[:, sh:B, :], a[:, 0:B - sh, :], ALU.add))
                        link(dve.tensor_copy(b_[:, 0:sh, :], a[:, 0:sh, :]))
                        a, b_, sh = b_, a, 2 * sh
                    link(dve.tensor_scalar(ci[:], a[:, B - 1, :], 127.0, None, ALU.add))
                    link(dve.tensor_scalar(ca[:], ci[:], -128, None, ALU.bitwise_and))
                    link(dve.tensor_copy(c["pad"][:], ca[:]))
                    link(dve.tensor_copy(c["e0"][:], c["pad"][:]))
                    x0, x1, sh = c["e0"], c["e1"], 1
                    while sh < E:
                        link(dve.tensor_tensor(x1[:, sh:E], x0[:, sh:E], x0[:, 0:E - sh], ALU.add))
                        link(dve.tensor_copy(x1[:, 0:sh], x0[:, 0:sh]))
                        x0, x1, sh = x1, x0, 2 * sh
                    link(dve.tensor_tensor(c["base"][:], x0[:], c["pad"][:], ALU.subtract))
                    link(dve.tensor_tensor(b_[:], a[:], total, ALU.subtract))
                    link(dve.tensor_tensor(a[:], b_[:], rank, ALU.add))
                    link(dve.tensor_tensor(R["pos"][:], a[:], c["base"][:].unsqueeze(1).to_broadcast([N, B, E]),
                                           ALU.add))
                    for k in range(2):
                        link(dve.tensor_tensor(R[f"pick{k + 1}"][:], R["pos"][:], R[f"sel{k + 1}"][:], ALU.mult))
                        link(dve.tensor_reduce(r[f"f{k + 1}"][:], R[f"pick{k + 1}"][:], AX.X, ALU.add))
                        dve.tensor_copy(pos[k][:], r[f"f{k + 1}"][:]).then_inc(e_pos, 1)
                    link(dve.tensor_tensor(past[:], start[:], x0[0:1, :].unsqueeze(1).to_broadcast([1, NT, E]),
                                           ALU.is_ge))
                    link(dve.tensor_reduce(nexp[:], past[:], AX.X, ALU.add))
                    link(dve.tensor_scalar(tile_e[:], nexp[:], float(E - 1), None, ALU.min))
                    link(dve.reciprocal(r["rsum"][:], r["sum"][:]))
                    link(dve.tensor_tensor(r["p1"][:], r["m1"][:], r["rsum"][:], ALU.mult))
                    link(dve.tensor_tensor(r["p2"][:], r["m2"][:], r["rsum"][:], ALU.mult))
                    link(dve.scalar_tensor_tensor(out=r["den"][:], in0=r["p1"][:], scalar=1e-9, in1=r["p2"][:],
                                                  op0=ALU.add, op1=ALU.add))
                    link(dve.reciprocal(r["rden"][:], r["den"][:]))
                    for k in range(2):
                        link(dve.scalar_tensor_tensor(out=tw[:, k, :], in0=r[f"p{k + 1}"][:], scalar=tg[0:N, 1:2],
                                                      in1=r["rden"][:], op0=ALU.mult, op1=ALU.mult))
                        link(dve.tensor_tensor(R[f"pick{k + 1}"][:], R[f"sel{k + 1}"][:],
                                               tw[:, k, :].unsqueeze(2).to_broadcast([N, B, E]), ALU.mult))
                    dve.tensor_tensor(R["wsel"][:], R["pick1"][:], R["pick2"][:], ALU.add).then_inc(e_pos, 1)
                    with dve.Fori(0, E // 2) as i:
                        for u in range(2):
                            e = 2 * i + u
                            dve.wait_ge(i_w[u], 48 * (i + 1))
                            dve.tensor_reduce(am[:, u:u + 1], raw[:, u].rearrange("p j c f -> p (j c f)"), AX.X,
                                              ALU.max, apply_absolute_value=True).then_inc(e_am, 1)
                            dve.wait_ge(q_amax, e + 1)
                            dve.tensor_scalar(pw[:, u:u + 1].bitcast(I32), amax[:, u:u + 1].bitcast(I32), 0x7F800000,
                                              None, ALU.bitwise_and).then_inc(e_ch, 1)
                            dve.wait_ge(e_ch, 4 * e + 1)
                            dve.tensor_scalar(pw[:, 2 + u:3 + u], pw[:, u:u + 1], 2.0 ** -100, 1.0 / WS, ALU.max,
                                              ALU.mult).then_inc(e_ch, 1)
                            dve.wait_ge(e_ch, 4 * e + 2)
                            dve.reciprocal(sc[:, u:u + 1], pw[:, 2 + u:3 + u]).then_inc(e_sc, 1)
                            dve.tensor_scalar(inv[:, bass.ds(e, 1)], pw[:, 2 + u:3 + u], 1.0 / XS, None, ALU.mult
                                              ).then_inc(e_ch, 1)
                            dve.wait_ge(e_sc, e + 1)
                            dve.tensor_scalar(ub[:, bass.ds(e * FC, FC)], ub[:, bass.ds(e * FC, FC)], sc[:, u:u + 1],
                                              XS, ALU.mult, ALU.mult).then_inc(e_ch, 1)
                            dve.wait_ge(s_h, 2 * e + 2)
                            dve.scalar_tensor_tensor(
                                out=GL[:, bass.ds(e, 1)].rearrange("p e j c f -> p (e j c f)"),
                                in0=raw[:, u].rearrange("p j c f -> p (j c f)"), scalar=sc[:, u:u + 1],
                                in1=GH[:, bass.ds(e, 1)].rearrange("p e j c f -> p (e j c f)"),
                                op0=ALU.mult, op1=ALU.subtract).then_inc(e_l, 1)
                            dve.tensor_tensor(DL[:, bass.ds(e, 1)].rearrange("p e f d -> p (e f d)"),
                                              draw[:, u].rearrange("p f d -> p (f d)"),
                                              f32(DH[:, bass.ds(e, 1)].rearrange("p e f d -> p (e f d)")),
                                              ALU.subtract).then_inc(e_dl, 1)
                    for g in range(B // 4):
                        dve.wait_ge(t_w, g + 1)
                        dve.tensor_copy(wselT[:, 4 * g:4 * g + 4, :],
                                        bX[g % 2][0:E, 0:4 * N].rearrange("e (b i) -> e b i", b=4)).then_inc(e_wt, 1)
                    for b in range(B):
                        dve.wait_ge(t_wb, b + 1)
                        dve.tensor_tensor(X[:, b, :], X[:, b, :], bX[b % 2][0:N, 0:DIM], ALU.add).then_inc(e_X, 1)

        UN = 4
        xt = sb("xt", [128, UN, ROWW], F32)
        xH, xL = sb("xH", [128, 2, DC, 128], F16), sb("xL", [128, 2, DC, 128], F16)
        sg, hf = sb("sg", [128, FC, 128], F32), sb("hf", [128, FC, 128], F32)
        hH, hL = sb("hH", [128, 2, FC, 128], F32R), sb("hL", [128, 2, FC, 128], F32R)
        where = sb("where", [128, UN], I32)
        v_id = sem("dve_where")
        ys = sb("ys", [128, UN, DIM], F32)
        l_x = [sem(f"tile_in{u}") for u in range(UN)]
        y_out = [sem(f"tile_out{u}") for u in range(UN)]
        k_T, k_GU, k_D = sem("pe_tileT"), sem("pe_gate_up"), sem("pe_down")
        a_x, a_s, a_h = sem("act_tile_x"), sem("act_silu"), sem("act_h")
        v_x, v_h, v_l, v_y = sem("dve_tile_x"), sem("dve_h"), sem("dve_hlow"), sem("dve_y")
        bT, bG, bU, bY = [banks[0], banks[5]], banks[1:3], banks[3:5], [misc[:, 0:512], misc[:, 512:1024]]

        def tiles(eng, step):
            first = UN + 2
            count = (NT - first) // UN
            for n in range(first):
                step(0, n)
            with eng.Fori(1, 1 + count) as i:
                for c in range(2, UN + 2):
                    step(i, c)
            for n in range(first + UN * count, NT + 2):
                step(0, n)

        def has(i, c, back):
            return not isinstance(i, int) or 0 <= UN * i + c - back < NT

        def at(i, c):
            return UN * i + c, i + c // UN, c % UN, c % 2

        def wait(eng, s, value):
            if not isinstance(value, int) or value > 0:
                eng.wait_ge(s, value)

        def expert(eng, t):
            return eng.value_load(tile_e[0:1, bass.ds(t, 1)], min_val=0, max_val=E - 1)

        def two_experts(eng, i, c, kept):
            one = expert(eng, UN * i + c - 1) if has(i, c, 1) else None
            two = kept.get((id(i) if not isinstance(i, int) else 0, c - 2))
            if two is None and has(i, c, 2):
                two = expert(eng, UN * i + c - 2)
            kept[(id(i) if not isinstance(i, int) else 0, c - 1)] = one
            return one, two

        with nc.Block() as block:
            @block.sync
            def _(sp):
                def step(i, c):
                    if has(i, c, 0):
                        t, h, s, u = at(i, c)
                        wait(sp, k_T, t - UN + 1)
                        wait(sp, v_id, t - UN + 1)
                        sp.dma_start(xt[:, s, :], xs_scr[bass.ds(128 * t, 128), :]).then_inc(l_x[s], 16)

                tiles(sp, step)

            @block.gpsimd
            def _(pool):
                for t in range(NT):
                    s = t % UN
                    pool.wait_ge(v_y, t + 1)
                    pool.indirect_dma_start(
                        y_scr, bass.IndirectOffsetOnAxis(ap=where[:, s:s + 1].bitcast(mybir.dt.uint32), axis=0),
                        ys[:, s, :], None).then_inc(y_out[s], 16)
                for s in range(UN):
                    pool.wait_ge(y_out[s], 16 * ((NT + UN - 1 - s) // UN))

            @block.scalar
            def _(act):
                def step(i, c):
                    if has(i, c, 1):
                        e = expert(act, UN * i + c - 1)
                    if has(i, c, 0):
                        t, h, s, u = at(i, c)
                        act.wait_ge(k_T, t + 1)
                        wait(act, k_GU, t - 1)
                        act.activation(xH[:, u], bT[u][:, 0:DC * 128].rearrange("p (c s) -> p c s", c=DC), ACT.Copy,
                                       scale=XS).then_inc(a_x, 1)
                    if has(i, c, 1):
                        t, h, s, u = at(i, c - 1)
                        act.wait_ge(k_GU, t + 1)
                        for f in range(FC):
                            wait(act, v_h, FC * (t - 1) + f + 1)
                            act.activation(sg[:, f, :], bG[u][:, 128 * f:128 * (f + 1)], ACT.Silu,
                                           bias=gb[:, bass.ds(e * FC + f, 1)], scale=inv[:, bass.ds(e, 1)]
                                           ).then_inc(a_s, 1)
                        act.wait_ge(v_h, FC * (t + 1))
                        wait(act, k_D, t - 1)
                        act.activation(hH[:, u], hf[:], ACT.Copy).then_inc(a_h, 1)

                tiles(act, step)

            @block.tensor
            def _(pe):
                kept = {}

                def step(i, c):
                    e1, e2 = two_experts(pe, i, c, kept)
                    if has(i, c, 0):
                        t, h, s, u = at(i, c)
                        pe.wait_ge(l_x[s], 16 * (h + 1))
                        wait(pe, v_x, t - 1)
                        for k in range(DC):
                            mm = pe.transpose(bT[u][:, 128 * k:128 * (k + 1)], xt[:, s, 128 * k:128 * (k + 1)],
                                              ident[:])
                        mm.then_inc(k_T, 1)
                    if has(i, c, 1):
                        t, h, s, u = at(i, c - 1)
                        pe.wait_ge(v_x, t + 1)
                        wait(pe, a_s, FC * (t - 1))
                        wait(pe, v_h, FC * (t - 1))
                        for j, bank in enumerate((bG[u], bU[u])):
                            for f in range(FC):
                                for n, (W, x) in enumerate(((GH, xH), (GH, xL), (GL, xH))):
                                    for k in range(DC):
                                        w = W[:, bass.ds(e1, 1), j, k, 128 * f:128 * (f + 1)]
                                        mm = pe.matmul(bank[:, 128 * f:128 * (f + 1)], w.rearrange("p o f -> p (o f)"),
                                                       x[:, u, k, :], start=(n == 0 and k == 0),
                                                       stop=(n == 2 and k == DC - 1))
                        mm.then_inc(k_GU, 1)
                    if has(i, c, 2):
                        t, h, s, u = at(i, c - 2)
                        pe.wait_ge(v_l, t + 1)
                        wait(pe, v_y, t - 1)
                        for n, (W, x) in enumerate(((DH, hH), (DL, hH), (DH, hL))):
                            for f in range(FC):
                                mm = pe.matmul(bY[u][:, 0:DIM], x[:, u, f, :],
                                               W[:, bass.ds(e2, 1), f, :].rearrange("p o d -> p (o d)"),
                                               start=(n == 0 and f == 0), stop=(n == 2 and f == FC - 1))
                        mm.then_inc(k_D, 1)

                tiles(pe, step)

            @block.vector
            def _(dve):
                kept = {}

                def step(i, c):
                    e1, e2 = two_experts(dve, i, c, kept)
                    if has(i, c, 0):
                        t, h, s, u = at(i, c)
                        dve.wait_ge(a_x, t + 1)
                        dve.scalar_tensor_tensor(out=xL[:, u], in0=bT[u][:, 0:DC * 128].rearrange("p (c s) -> p c s", c=DC),
                                                 scalar=XS, in1=xH[:, u], op0=ALU.mult, op1=ALU.subtract
                                                 ).then_inc(v_x, 1)
                        dve.wait_ge(l_x[s], 16 * (h + 1))
                        wait(dve, y_out[s], 16 * h)
                        dve.tensor_copy(where[:, s:s + 1], xt[:, s, DIM:ROWW].bitcast(I32)).then_inc(v_id, 1)
                    if has(i, c, 1):
                        t, h, s, u = at(i, c - 1)
                        wait(dve, v_l, t)
                        for f in range(FC):
                            dve.wait_ge(a_s, FC * t + f + 1)
                            dve.scalar_tensor_tensor(out=hf[:, f, :], in0=bU[u][:, 128 * f:128 * (f + 1)],
                                                     scalar=ub[:, bass.ds(e1 * FC + f, 1)], in1=sg[:, f, :],
                                                     op0=ALU.add, op1=ALU.mult).then_inc(v_h, 1)
                        dve.wait_ge(a_h, t + 1)
                        dve.tensor_tensor(hL[:, u], hf[:], f32(hH[:, u]), ALU.subtract).then_inc(v_l, 1)
                    if has(i, c, 2):
                        t, h, s, u = at(i, c - 2)
                        dve.wait_ge(k_D, t + 1)
                        wait(dve, y_out[s], 16 * h)
                        dve.wait_ge(v_id, t + 1)
                        dve.tensor_scalar(ys[:, s, :], bY[u][:, 0:DIM], inv[:, bass.ds(e2, 1)], None, ALU.mult
                                          ).then_inc(v_y, 1)

                tiles(dve, step)

        QB = 4
        yt = sb("yt", [N, 2, QB, 2, DIM], F32)
        y_in = [sem(f"y_in{u}") for u in range(2)]
        y_add, s_out = sem("y_added"), sem("out_written")
        y_rows = y_scr[0:2 * B * N, :].rearrange("(b i k) d -> i b k d", i=N, k=2)
        out_rows = out.rearrange("b i d -> i b d")
        with nc.Block() as block:
            @block.sync
            def _(sp):
                for g in range(B // QB):
                    if g >= 2:
                        sp.wait_ge(y_add, 2 * QB * (g - 1))
                    sp.dma_start(yt[:, g % 2], y_rows[:, QB * g:QB * (g + 1)]).then_inc(y_in[g % 2], 16)

            @block.scalar
            def _(act):
                for g in range(B // QB):
                    act.wait_ge(y_add, 2 * QB * (g + 1))
                    act.dma_start(out_rows[:, QB * g:QB * (g + 1), :], X[:, QB * g:QB * (g + 1), :]).then_inc(s_out, 16)
                act.wait_ge(s_out, 16 * (B // QB))

            @block.vector
            def _(dve):
                for g in range(B // QB):
                    dve.wait_ge(y_in[g % 2], 16 * (g // 2 + 1))
                    for k in range(2):
                        for q in range(QB):
                            b = QB * g + q
                            if k:
                                dve.wait_ge(y_add, 2 * QB * g + q + 1)
                            dve.scalar_tensor_tensor(out=X[:, b, :], in0=yt[:, g % 2, q, k, :], scalar=tw[:, k, b:b + 1],
                                                     in1=X[:, b, :], op0=ALU.mult, op1=ALU.add).then_inc(y_add, 1)


def layer_norm_stats(dve, X, stats, mv, veps, rstd, B, s_st, s_mv, s_ve, s_sq, s_rs):
    for b in range(B):
        dve.bn_stats(stats[:, b, :], X[:, b, :]).then_inc(s_st, 1)
    dve.wait_ge(s_st, B)
    for b in range(B):
        dve.bn_aggr(mv[:, b, :], stats[:, b, :]).then_inc(s_mv, 1)
    dve.wait_ge(s_mv, B)
    dve.tensor_scalar(veps[:], mv[:, :, 1], LN_EPS, None, ALU.add).then_inc(s_ve, 1)
    dve.wait_ge(s_sq, 1)
    dve.reciprocal(rstd[:], rstd[:]).then_inc(s_rs, 1)
    dve.wait_ge(s_rs, 1)


_INS = ["x", "ctx_768", "mask_BxS2_bf1", "g_xattn", "g_ffn", "L0_xattn_Wq", "L0_xattn_Wk", "L0_xattn_Wv",
        "L0_xattn_Wo", "L0_ffn_router_w", "L0_ffn_gate_w", "L0_ffn_gate_b", "L0_ffn_up_w", "L0_ffn_up_b",
        "L0_ffn_down_w", "L0_ffn_down_b"]


def kernel(**inputs):
    import numpy as _np
    import concourse.bacc as _bacc
    from concourse.bass_utils import run_bass_kernel_spmd as _run

    nc = _bacc.Bacc("TRN2", target_bir_lowering=False, num_devices=1)
    arrays, args = {}, []
    for name in _INS:
        a = _np.ascontiguousarray(inputs[name])
        if a.dtype == _np.bool_:
            a = a.view(_np.uint8)
        arrays[f"in_{name}"] = a
        args.append(nc.dram_tensor(f"in_{name}", a.shape, mybir.dt.from_np(a.dtype), kind="ExternalInput").ap())
    out = nc.dram_tensor("out", inputs["x"].shape, F32, kind="ExternalOutput").ap()
    build(nc, *args, out)
    return _run(nc, [arrays], core_ids=[0]).results[0]["out"]
```

```python
from contextlib import ExitStack

import concourse.bass as bass
from concourse import mybir

F32 = mybir.dt.float32
F32R = mybir.dt.float32r
BF16 = mybir.dt.bfloat16
F16 = mybir.dt.float16
U8 = mybir.dt.uint8
ALU = mybir.AluOpType
ACT = mybir.ActivationFunctionType
AX = mybir.AxisListType

HEADS = 16
PAIRS = HEADS // 2
LN_EPS = 1e-5
HIDDEN = float(2.0 ** 126)


def f32(ap):
    return ap.bitcast(F32)


def build(nc, x, ctx_768, mask, g_xattn, g_ffn, Wq, Wk, Wv, Wo, router_w, gate_w, gate_b, up_w, up_b,
          down_w, down_b, out):
    B, N, DIM = x.shape
    M, CTX = ctx_768.shape[1], ctx_768.shape[2]
    HD = DIM // HEADS
    JT = 3
    JP = M // JT
    MP = M + M % 2
    CK = CTX // 2
    GB = 4
    GROUPS = B // GB
    NI = 128
    VW = 3 * HD + 1
    RB, RM = 96, 97
    SCALE = HD ** -0.5
    NB = 3

    q_scr = nc.dram_tensor("q_scr", [2, B, DIM, N], F32, kind="Internal").ap()
    k_scr = nc.dram_tensor("k_scr", [NB, 2, DIM, MP], F32, kind="Internal").ap()
    bias_scr = nc.dram_tensor("bias_scr", [B, MP], F32, kind="Internal").ap()

    E = gate_w.shape[0]
    TOP_K = 2
    NT = TOP_K * B * N // 128 + E - 1
    ROWW = DIM + 1
    xs_scr = nc.dram_tensor("xs_scr", [NT * 128, ROWW], F32, kind="Internal").ap()
    y_scr = nc.dram_tensor("y_scr", [TOP_K * B * N + NT * 128, DIM], F32, kind="Internal").ap()

    with ExitStack() as whole:
        def keep(name, shape, dt):
            return whole.enter_context(nc.sbuf_tensor(name, shape, dt))

        def sem(name):
            return whole.enter_context(nc.semaphore(name))

        X = keep("X", [N, B, DIM], F32)
        ident = keep("ident", [128, 128], F32)
        gates = keep("gates", [128, 2], F32)
        tg = keep("tg", [128, 2], F32)
        banks = [whole.enter_context(nc.psum_tensor(f"bank{i}", [128, 512], F32)) for i in range(6)]
        misc = whole.enter_context(nc.psum_tensor("misc", [128, 1024], F32))
        psS, psST, psO = banks[0:2], banks[2:4], banks[4:6]

        attention(nc, locals())
        experts(nc, locals())


def attention(nc, v):
    (x, ctx_768, mask, Wq, Wk, Wv, Wo, X, ident, gates, tg, psS, psST, psO, misc) = (
        v[k] for k in "x ctx_768 mask Wq Wk Wv Wo X ident gates tg psS psST psO misc".split())
    (B, N, DIM, M, HD, JT, JP, MP, CK, GB, GROUPS, NI, VW, RB, RM, SCALE, NB) = (
        v[k] for k in "B N DIM M HD JT JP MP CK GB GROUPS NI VW RB RM SCALE NB".split())
    q_scr, k_scr, bias_scr = v["q_scr"], v["k_scr"], v["bias_scr"]
    CTX = 2 * CK

    with ExitStack() as stack:
        def sb(name, shape, dt):
            return stack.enter_context(nc.sbuf_tensor(name, shape, dt))

        def sem(name):
            return stack.enter_context(nc.semaphore(name))

        shapes = {"q": (Wq, 128), "k": (Wk, CK), "v": (Wv, CK), "o": (Wo, 128)}
        WH = {k: sb(f"w{k}_h", [p, 2, DIM], F32R) for k, (_, p) in shapes.items()}
        WL = {k: sb(f"w{k}_l", [p, 2, DIM], F32R) for k, (_, p) in shapes.items()}
        cTH = sb("cTH", [CK, 2, MP], F32R)
        cTL = sb("cTL", [CK, 2, MP], F32R)
        KS = [sb(f"KS{u}", [128, PAIRS, MP], F32R) for u in range(NB)]
        QS = [sb(f"QS{u}", [128, PAIRS, 2, NI], F32R) for u in range(NB)]
        VS = sb("VS", [JP, NB, JT, HEADS, VW], BF16)
        zero = sb("zero", [JP, 1], F32)
        UN = PAIRS * JT
        PT = sb("PT", [JP, UN, 2, NI], F32)
        PL = sb("PL", [JP, UN, 2, NI], F16)
        PH = PT[:].rearrange("p u e i -> p (u e i)").bitcast(BF16).rearrange(
            "p (u e i two) -> p u e i two", u=UN, e=2, two=2)[:, :, :, :, 1]
        early = stack.enter_context(ExitStack())
        first = lambda name, shape, dt: early.enter_context(nc.sbuf_tensor(name, shape, dt))
        Wf = {k: first(f"w{k}_f", [p, 2, DIM], F32) for k, (_, p) in shapes.items()}
        mask_sb = first("mask_sb", [B, M], U8)
        bias_sb = first("bias_sb", [B, MP], F32)
        stats = first("stats", [N, B, 6], F32)
        mv = first("mv", [N, B, 2], F32)
        rstd = first("rstd", [N, B], F32)
        veps = first("veps", [N, B], F32)
        xn = first("xn", [N, GB, DIM], F32)
        xTH = first("xTH", [128, 2, GB * N], F32R)
        xTL = first("xTL", [128, 2, GB * N], F32R)
        qH = first("qH", [128, 2, GB * N], F32R)
        qL = first("qL", [128, 2, GB * N], F32R)

        s_w, s_x, s_g, s_m = sem("weights_in"), sem("x_in"), sem("gates_in"), sem("mask_in")
        s_id0, s_id = sem("ident_zero"), sem("ident_ready")
        s_clear, s_wh, s_wl, s_bias = sem("cleared"), sem("w_high"), sem("w_low"), sem("bias_ready")
        s_st, s_mv, s_ve, s_sq, s_rs = (sem(n) for n in ("ln_stats", "ln_mv", "ln_veps", "ln_sqrt", "ln_rstd"))
        s_xn, s_xt, s_xh, s_xl = sem("xn_ready"), sem("xT_ready"), sem("xT_high"), sem("xT_low")
        s_qp, s_qh, s_ql, s_qw = sem("q_psum"), sem("q_high"), sem("q_low"), sem("q_written")
        FT = 5
        fill = first("fill", [128, FT, v["ROWW"]], F32)
        s_f0, s_f1, s_fw = sem("fill_zero"), sem("fill_ids"), sem("fill_written")
        s_bw, s_tg = sem("bias_written"), sem("tanh_ready")

        def groups(eng, group):
            group(0)
            with eng.Fori(1, GROUPS) as g:
                group(g)

        later = lambda g: not isinstance(g, int) or g > 0

        with nc.Block() as block:
            @block.sync
            def _(sp):
                sp.dma_start(X[:], x.rearrange("b i d -> i b d")).then_inc(s_x, 16)
                for k, (w, p) in shapes.items():
                    sp.dma_start(Wf[k][:], w.rearrange("(c p) n -> p c n", p=p)).then_inc(s_w, 16)
                sp.dma_start(mask_sb[:], mask).then_inc(s_m, 16)
                for j, g in enumerate((v["g_xattn"], v["g_ffn"])):
                    sp.dma_start(gates[:, j:j + 1], g.rearrange("(o a) -> o a", o=1).to_broadcast([128, 1])
                                 ).then_inc(s_g, 16)
                sp.wait_ge(s_bias, 1)
                sp.wait_ge(s_clear, 3)
                sp.dma_start(bias_scr, bias_sb[:]).then_inc(s_bw, 16)
                def group(g):
                    sp.wait_ge(s_ql, g + 1)
                    for part, t in ((0, qH), (1, qL)):
                        for c in range(2):
                            sp.dma_start(
                                q_scr[part, bass.ds(g * GB, GB), c * 128:(c + 1) * 128, :].rearrange("b p i -> p b i"),
                                f32(t[:, c, :]).rearrange("p (b i) -> p b i", b=GB)).then_inc(s_qw, 16)
                groups(sp, group)
                sp.wait_ge(s_qw, 64 * GROUPS)
                sp.wait_ge(s_bw, 16)

            @block.gpsimd
            def _(pool):
                pool.memset(ident[:], 0.0).then_inc(s_id0, 1)
                pool.wait_ge(s_id0, 1)
                pool.affine_select(out=ident[:], in_=ident[:], compare_op=ALU.not_equal, fill=1.0, base=0,
                                   pattern=[[-1, 128]], channel_multiplier=1).then_inc(s_id, 1)
                pool.wait_ge(s_id, 1)
                parts = [(f32(cTH[:, :, M:MP]), 0.0), (f32(cTL[:, :, M:MP]), 0.0), (bias_sb[:, M:MP], 0.0), (zero[:], 0.0),
                         (PT[:, :, :, N:NI], 0.0), (PL[:, :, :, N:NI], 0.0),
                         (VS[:, :, :, :, VW - 1:VW].rearrange("p u t h o -> p (u t) h o"), 1.0)]
                for u in range(NB):
                    parts += [(f32(QS[u][0:96]), 0.0), (f32(QS[u][96:128]), 1.0), (f32(KS[u][96:128]), 1.0)]
                for n, (part, value) in enumerate(parts):
                    pool.memset(part, value).then_inc(s_clear, 1)
                    pool.wait_ge(s_clear, n + 1)

                pool.memset(fill[:], 0.0).then_inc(s_f0, 1)
                pool.wait_ge(s_f0, 1)
                for n in range(v["NT"] // FT):
                    if n:
                        pool.wait_ge(s_fw, 16 * n)
                    pool.iota(fill[:, :, DIM:DIM + 1].rearrange("p t o -> p (t o)").bitcast(mybir.dt.int32),
                              pattern=[[128, FT]], base=2 * B * N + 128 * FT * n, channel_multiplier=1).then_inc(s_f1, 1)
                    pool.wait_ge(s_f1, n + 1)
                    pool.dma_start(v["xs_scr"][128 * FT * n:128 * FT * (n + 1), :].rearrange("(t p) w -> p t w", p=128),
                                   fill[:]).then_inc(s_fw, 16)
                pool.wait_ge(s_fw, 16 * (v["NT"] // FT))

            @block.scalar
            def _(act):
                act.wait_ge(s_g, 32)
                act.activation(tg[:], gates[:], ACT.Tanh).then_inc(s_tg, 1)
                act.wait_ge(s_w, 64)
                for k in shapes:
                    act.activation(WH[k][:], Wf[k][:], ACT.Copy, scale=SCALE if k == "q" else 1.0
                                   ).then_inc(s_wh, 1)
                act.wait_ge(s_ve, 1)
                act.activation(rstd[:], veps[:], ACT.Sqrt).then_inc(s_sq, 1)
                def group(g):
                    act.wait_ge(s_xt, g + 1)
                    act.activation(xTH[:], misc[:].rearrange("p (c n) -> p c n", c=2)[:, :, 0:GB * N], ACT.Copy
                                   ).then_inc(s_xh, 1)
                    act.wait_ge(s_qp, g + 1)
                    if later(g):
                        act.wait_ge(s_qw, 64 * g)
                    for c in range(2):
                        act.activation(qH[:, c, :], psS[c][:, 0:GB * N], ACT.Copy).then_inc(s_qh, 1)

                groups(act, group)

            @block.tensor
            def _(pe):
                pe.wait_ge(s_id, 1)
                pe.wait_ge(s_wl, 4)
                def group(g):
                    pe.wait_ge(s_xn, g + 1)
                    if later(g):
                        pe.wait_ge(s_xl, g)
                    for c in range(2):
                        for b in range(GB):
                            mm = pe.transpose(misc[:, c * 512 + b * N:c * 512 + (b + 1) * N],
                                              xn[:, b, c * 128:(c + 1) * 128], ident[0:N, 0:N])
                    mm.then_inc(s_xt, 1)
                    pe.wait_ge(s_xl, g + 1)
                    if later(g):
                        pe.wait_ge(s_ql, g)
                    for m in range(2):
                        for n, (w, r) in enumerate(((WH, xTH), (WL, xTH), (WH, xTL))):
                            for c in range(2):
                                mm = pe.matmul(psS[m][:, 0:GB * N], w["q"][:, c, m * 128:(m + 1) * 128], r[:, c, :],
                                               start=(n == 0 and c == 0), stop=(n == 2 and c == 1))
                    mm.then_inc(s_qp, 1)

                groups(pe, group)

            @block.vector
            def _(dve):
                for n, k in enumerate(shapes):
                    dve.wait_ge(s_wh, n + 1)
                    dve.scalar_tensor_tensor(out=WL[k][:], in0=Wf[k][:], scalar=SCALE if k == "q" else 1.0,
                                             in1=f32(WH[k][:]), op0=ALU.mult, op1=ALU.subtract).then_inc(s_wl, 1)
                dve.wait_ge(s_m, 16)
                dve.tensor_scalar(bias_sb[:, 0:M].rearrange("b (t p) -> b t p", t=JT),
                                  mask_sb[:].rearrange("b (p t) -> b t p", t=JT),
                                  -1.0, HIDDEN, ALU.add, ALU.mult).then_inc(s_bias, 1)
                dve.wait_ge(s_x, 16)
                layer_norm_stats(dve, X, stats, mv, veps, rstd, B, s_st, s_mv, s_ve, s_sq, s_rs)
                def group(g):
                    if later(g):
                        dve.wait_ge(s_xt, g)
                    for b in range(GB):
                        nb = g * GB + b
                        ins = dve.tensor_scalar(xn[:, b, :], X[:, bass.ds(nb, 1), :],
                                                mv[:, bass.ds(nb, 1), 0:1], rstd[:, bass.ds(nb, 1)],
                                                ALU.subtract, ALU.mult)
                    ins.then_inc(s_xn, 1)
                    dve.wait_ge(s_xh, g + 1)
                    dve.tensor_tensor(xTL[:], misc[:].rearrange("p (c n) -> p c n", c=2)[:, :, 0:GB * N],
                                      f32(xTH[:]), ALU.subtract).then_inc(s_xl, 1)
                    dve.wait_ge(s_qh, 2 * g + 2)
                    for c in range(2):
                        ins = dve.tensor_tensor(qL[:, c, :], psS[c][:, 0:GB * N], f32(qH[:, c, :]), ALU.subtract)
                    ins.then_inc(s_ql, 1)

                groups(dve, group)

        early.close()
        ctx_sb = sb("ctx_sb", [JP, NB, JT, CTX], F32)
        kH = sb("kH", [128, NB, 2, MP], F32R)
        kL = sb("kL", [128, NB, 2, MP], F32R)
        vf = sb("vf", [JP, NB, JT, DIM], F32)
        vr = sb("vr", [JP, JT, DIM], F32)
        mx = sb("mx", [N, HEADS], F32)
        nm = sb("nm", [HEADS, N], F32R)
        osum = sb("osum", [N, HEADS, HD], F32)
        rden = sb("rden", [N, HEADS], F32)
        on = sb("on", [N, HEADS, HD], F32)
        oTH = sb("oTH", [128, 2, N], F32R)
        oTL = sb("oTL", [128, 2, N], F32R)

        each = lambda name: [sem(f"{name}{u}") for u in range(NB)]
        d_ctx, d_kw, d_ks, d_qs, d_m = each("ctx_in"), each("k_out"), each("ks_in"), each("qs_in"), each("m_in")
        p_T, p_K, p_V, p_S, p_mT = (sem(n) for n in ("pe_ctxT", "pe_k", "pe_v", "pe_scores", "pe_maxT"))
        p_ST, p_PV, p_OT, p_Wo = (sem(n) for n in ("pe_scoresT", "pe_pv", "pe_oT", "pe_wo"))
        a_T, a_K, a_V, a_V1, a_E, a_O = (sem(n) for n in ("act_ctxT", "act_k", "act_v", "act_v1", "act_exp", "act_oT"))
        v_T, v_K, v_L, v_max, v_nm = (sem(n) for n in ("dve_ctxT", "dve_k", "dve_plow", "dve_max", "dve_negmax"))
        v_os, v_rd, v_on, v_O, v_x1 = (sem(n) for n in ("dve_osum", "dve_rden", "dve_on", "dve_oT", "dve_x1"))
        g_1, g_r, g_V, g_L = (sem(n) for n in ("pool_v1", "pool_rest", "pool_v", "pool_plow"))

        SB = UN // 2
        POOL = [k for k in (1, 2, 5, 7, 8) if k < SB]
        vec = lambda k: sum(j not in POOL for j in range(k + 1))
        pol = lambda k: sum(j in POOL for j in range(k + 1))
        last_bank = lambda p: (JT * p + JT - 1) // 2
        pv_at = {last_bank(p) + 3: p for p in range(PAIRS)}
        SLOTS = max(pv_at) + 1
        heads_at = {0: (0, 1), 1: (2, 3), 2: (4,), 3: (5, 6), 4: (7, 8), 5: (9, 10), 6: (11, 12), 7: (13, 14), 8: (15,)}
        KP = (1, 2)
        VP = (4, 5, 6)
        MT, OT, OP, CT = 10, 10, 11, 10

        def at(i, c):
            return NB * i + c, i + c // NB, c % NB

        def steps(eng, step):
            first = NB + 1
            count = (B - 2 - first) // NB
            for n in range(first):
                step(0, n)
            with eng.Fori(1, 1 + count) as i:
                for c in range(1, NB + 1):
                    step(i, c)
            for n in range(first + NB * count, B + 3):
                step(0, n)

        def live(i, c, back):
            return not isinstance(i, int) or 0 <= NB * i + c - back < B

        def wait(eng, s, value):
            if not isinstance(value, int) or value > 0:
                eng.wait_ge(s, value)

        with nc.Block() as block:
            @block.sync
            def _(sp):
                def load_ctx(i, c):
                    b, h, u = at(i, c)
                    wait(sp, p_T, b - NB + 1)
                    sp.dma_start(ctx_sb[:, u, :, :], ctx_768[bass.ds(b, 1), :, :].rearrange("o (p t) d -> p (o t) d", t=JT)
                                 ).then_inc(d_ctx[u], 16)

                def step(i, c):
                    if live(i, c, -2):
                        load_ctx(i, c + 2)
                    if live(i, c, 0):
                        b, h, u = at(i, c)
                        wait(sp, p_ST, SB * (b - NB + 1))
                        for s, part in enumerate((0, 1, 0)):
                            for e in range(2):
                                sp.dma_start(
                                    f32(QS[u][32 * s + HD * e:32 * s + HD * e + HD, :, e, 0:N]),
                                    q_scr[part, bass.ds(b, 1)].rearrange("o (q e r) i -> e r (o q) i", e=2, r=HD)[e]
                                ).then_inc(d_qs[u], 16)
                        sp.dma_start(f32(KS[u][RB:RB + 1, :, :]),
                                     bias_scr[bass.ds(b, 1), :].unsqueeze(1).to_broadcast([1, PAIRS, MP])
                                     ).then_inc(d_ks[u], 16)
                        sp.wait_ge(v_K, b + 1)
                        for part, t in ((0, kH), (1, kL)):
                            sp.dma_start(k_scr[u, part].rearrange("(m p) j -> p m j", p=128), f32(t[:, u])
                                         ).then_inc(d_kw[u], 16)
                        sp.wait_ge(d_kw[u], 32 * (h + 1))
                        for s, part in enumerate((0, 0, 1)):
                            sp.dma_start(f32(KS[u][32 * s:32 * s + 32, :, :]),
                                         k_scr[u, part].rearrange("(q r) j -> r q j", r=32)).then_inc(d_ks[u], 16)
                    if live(i, c, 1):
                        b, h, u = at(i, c - 1)
                        sp.wait_ge(v_nm, b + 1)
                        sp.dma_start(f32(QS[u][RM:RM + 1, :, :, 0:N]).rearrange("o q e i -> o (q e) i"),
                                     f32(nm[:])).then_inc(d_m[u], 16)

                load_ctx(0, 0)
                load_ctx(0, 1)
                steps(sp, step)

            @block.gpsimd
            def _(pool):
                def low(i, c, k):
                    b, h, u = at(i, c - 2)
                    pool.wait_ge(a_E, SB * b + k + 1)
                    pool.tensor_tensor(PL[:, 2 * k:2 * k + 2, :, 0:N], PT[:, 2 * k:2 * k + 2, :, 0:N],
                                       PH[:, 2 * k:2 * k + 2, :, 0:N], ALU.subtract).then_inc(g_L, 1)

                def values(i, c):
                    b, h, u = at(i, c - 1)
                    part = lambda k: VS[:, u, :, :, HD * k:HD * (k + 1)]
                    head = lambda t: t[:].rearrange("p t (h d) -> p t h d", d=HD)
                    pool.wait_ge(a_V1, b + 1)
                    wait(pool, g_V, b)
                    pool.tensor_tensor(head(vr), vf[:, u].rearrange("p t (h d) -> p t h d", d=HD), part(0), ALU.subtract).then_inc(g_r, 1)
                    pool.wait_ge(g_r, b + 1)
                    pool.tensor_tensor(part(1), head(vr), zero[:].unsqueeze(2).unsqueeze(3).to_broadcast([JP, JT, HEADS, HD]),
                                       ALU.add).then_inc(g_1, 1)
                    pool.wait_ge(g_1, b + 1)
                    pool.tensor_tensor(part(2), head(vr), part(1), ALU.subtract).then_inc(g_V, 1)

                def step(i, c):
                    for k in POOL:
                        if live(i, c, 2):
                            low(i, c, k)
                    if live(i, c, 1):
                        values(i, c)

                steps(pool, step)

            @block.scalar
            def _(act):
                def transposed(i, c):
                        b, h, u = at(i, c)
                        act.wait_ge(p_T, b + 1)
                        wait(act, p_V, JT * b)
                        act.activation(cTH[:, :, 0:M], misc[0:CK].rearrange("p (c n) -> p c n", c=2)[:, :, 0:M],
                                       ACT.Copy).then_inc(a_T, 1)

                def step(i, c):
                    for k in range(SLOTS):
                        if k == OT + 1 and live(i, c, 3):
                            b, h, u = at(i, c - 3)
                            act.wait_ge(p_OT, b + 1)
                            wait(act, p_Wo, b)
                            act.activation(oTH[:], psS[0][:, 0:2 * N].rearrange("p (c i) -> p c i", c=2),
                                           ACT.Copy).then_inc(a_O, 1)
                        if k == CT + 1 and live(i, c, -1):
                            transposed(i, c + 1)
                        if k < SB and live(i, c, 2):
                            b, h, u = at(i, c - 2)
                            act.wait_ge(p_ST, SB * b + k + 1)
                            wait(act, p_PV, PAIRS * (b - 1) + (2 * k + 1) // JT + 1)
                            act.activation(PT[:, 2 * k:2 * k + 2, :, 0:N].rearrange("p a e i -> p (a e) i"),
                                           psST[k % 2][0:JP].rearrange("p (a i) -> p a i", i=NI)[:, :, 0:N],
                                           ACT.Exp).then_inc(a_E, 1)
                        if k == 7 and live(i, c, 1):
                            b, h, u = at(i, c - 1)
                            act.wait_ge(a_V, b + 1)
                            wait(act, p_PV, PAIRS * (b - NB + 1))
                            act.activation(VS[:, u, :, :, 0:HD].rearrange("p t h d -> p (t h) d"),
                                           vf[:, u].rearrange("p t (h d) -> p (t h) d", d=HD), ACT.Copy).then_inc(a_V1, 1)
                        if k == KP[-1] and live(i, c, 0):
                            b, h, u = at(i, c)
                            act.wait_ge(p_K, 2 * b + 2)
                            wait(act, d_kw[u], 32 * h)
                            act.activation(kH[:, u], misc[:].rearrange("p (m n) -> p m n", m=2)[:, :, 0:MP],
                                           ACT.Copy).then_inc(a_K, 1)
                        if k == VP[-1] + 1 and live(i, c, 0):
                            b, h, u = at(i, c)
                            act.wait_ge(p_V, JT * b + JT)
                            wait(act, g_r, b - NB + 1)
                            act.activation(vf[:, u].rearrange("p t n -> p (t n)"), misc[0:JP, 0:JT * DIM], ACT.Copy
                                           ).then_inc(a_V, 1)

                transposed(0, 0)
                steps(act, step)

            @block.tensor
            def _(pe):
                def ctx_T(i, c):
                    b, h, u = at(i, c)
                    pe.wait_ge(d_ctx[u], 16 * (h + 1))
                    wait(pe, a_V, b)
                    for k in range(2):
                        for t in range(JT):
                            mm = pe.transpose(misc[0:CK, 512 * k + JP * t:512 * k + JP * (t + 1)],
                                              ctx_sb[:, u, t, CK * k:CK * (k + 1)], ident[0:JP, 0:JP])
                    mm.then_inc(p_T, 1)

                def project_k(i, c, m):
                    b, h, u = at(i, c)
                    if m == 0:
                        pe.wait_ge(v_T, b + 1)
                    for n, (w, r) in enumerate(((WH, cTH), (WL, cTH), (WH, cTL))):
                        for k in range(2):
                            mm = pe.matmul(misc[:, 512 * m:512 * m + MP], w["k"][:, k, m * 128:(m + 1) * 128],
                                           r[:, k, :], start=(n == 0 and k == 0), stop=(n == 2 and k == 1))
                    mm.then_inc(p_K, 1)

                def project_v(i, c, t):
                    b, h, u = at(i, c)
                    if t == 0:
                        pe.wait_ge(v_K, b + 1)
                    for n, (w, r) in enumerate(((WH, cTH), (WL, cTH), (WH, cTL))):
                        for k in range(2):
                            mm = pe.matmul(misc[0:JP, DIM * t:DIM * (t + 1)], r[:, k, JP * t:JP * (t + 1)],
                                           w["v"][:, k, :], start=(n == 0 and k == 0), stop=(n == 2 and k == 1))
                    mm.then_inc(p_V, 1)

                def scores(i, c, hd):
                    b, h, u = at(i, c - 1)
                    if hd == 0:
                        pe.wait_ge(d_ks[u], 64 * (h + 1))
                        pe.wait_ge(d_qs[u], 96 * (h + 1))
                        wait(pe, v_x1, b - 2)
                    if hd == 1:
                        wait(pe, v_nm, b)
                    wait(pe, v_max, HEADS * b + hd - 1)
                    pe.matmul(psS[hd % 2][0:N, 0:MP], QS[u][0:RM, hd // 2, hd % 2, 0:N], KS[u][0:RM, hd // 2, :],
                              start=True, stop=True).then_inc(p_S, 1)

                def max_T(i, c):
                    b, h, u = at(i, c - 1)
                    pe.wait_ge(v_max, HEADS * (b + 1))
                    pe.transpose(psS[1][0:HEADS, 0:N], mx[:], ident[0:N, 0:N]).then_inc(p_mT, 1)

                def scores_T(i, c, k):
                    b, h, u = at(i, c - 2)
                    if k == 0:
                        pe.wait_ge(d_m[u], 16 * (h + 1))
                    wait(pe, a_E, SB * b + k - 1)
                    for a in range(2):
                        p, t = divmod(2 * k + a, JT)
                        mm = pe.matmul(psST[k % 2][0:JP, 2 * NI * a:2 * NI * (a + 1)],
                                       KS[u][0:RM + 1, p, JP * t:JP * (t + 1)],
                                       QS[u][0:RM + 1, p, :, :].rearrange("r e i -> r (e i)"), start=True, stop=True)
                    mm.then_inc(p_ST, 1)

                def sums(i, c, p):
                    b, h, u = at(i, c - 2)
                    if p == 0:
                        pe.wait_ge(g_V, b + 1)
                    if p % 4 == 0:
                        wait(pe, v_os, 2 * (b - 1) + p // 4 + 1)
                    k = last_bank(p)
                    pe.wait_ge(v_L, vec(SB - 1) * b + vec(k))
                    pe.wait_ge(g_L, pol(SB - 1) * b + pol(k))
                    for e in range(2):
                        hd = 2 * p + e
                        for part, P in enumerate((PH, PL)):
                            for t in range(JT):
                                mm = pe.matmul(psO[hd // 8][:, VW * (hd % 8):VW * (hd % 8 + 1)], P[:, JT * p + t, e, :],
                                               VS[:, u, t, hd, :], start=(part == 0 and t == 0),
                                               stop=(part == 1 and t == JT - 1))
                    mm.then_inc(p_PV, 1)

                def out_T(i, c):
                    b, h, u = at(i, c - 3)
                    pe.wait_ge(v_on, 2 * b + 2)
                    pe.wait_ge(v_max, HEADS * min(b + 2, B) if isinstance(b, int) else HEADS * (b + 2))
                    for k in range(2):
                        mm = pe.transpose(psS[0][:, N * k:N * (k + 1)],
                                          on[:, 8 * k:8 * k + 8, :].rearrange("i h d -> i (h d)"), ident[0:N, 0:N])
                    mm.then_inc(p_OT, 1)

                def project_o(i, c):
                    b, h, u = at(i, c - 3)
                    pe.wait_ge(v_O, b + 1)
                    for n, (w, r) in enumerate(((WH, oTH), (WL, oTH), (WH, oTL))):
                        for k in range(2):
                            mm = pe.matmul(psS[0][0:N, 0:DIM], r[:, k, :], w["o"][:, k, :],
                                           start=(n == 0 and k == 0), stop=(n == 2 and k == 1))
                    mm.then_inc(p_Wo, 1)

                def step(i, c):
                    for s in range(SLOTS):
                        heads = heads_at.get(s, ()) if live(i, c, 1) else ()
                        if s < SB and live(i, c, 2):
                            scores_T(i, c, s)
                        if s in KP and live(i, c, 0):
                            project_k(i, c, KP.index(s))
                        for hd in heads[0:1]:
                            scores(i, c, hd)
                        if s in pv_at and live(i, c, 2):
                            sums(i, c, pv_at[s])
                        if s in VP and live(i, c, 0):
                            project_v(i, c, VP.index(s))
                        for hd in heads[1:2]:
                            scores(i, c, hd)
                        if s == MT and live(i, c, 1):
                            max_T(i, c)
                        if s == OT and live(i, c, 3):
                            out_T(i, c)
                        if s == OP and live(i, c, 3):
                            project_o(i, c)
                        if s == CT and live(i, c, -1):
                            ctx_T(i, c + 1)

                ctx_T(0, 0)
                steps(pe, step)

            @block.vector
            def _(dve):
                def low(i, c, k):
                    b, h, u = at(i, c - 2)
                    dve.wait_ge(a_E, SB * b + k + 1)
                    dve.tensor_tensor(PL[:, 2 * k:2 * k + 2, :, 0:N].rearrange("p a e i -> p (a e) i"),
                                      PT[:, 2 * k:2 * k + 2, :, 0:N].rearrange("p a e i -> p (a e) i"),
                                      PH[:, 2 * k:2 * k + 2, :, 0:N].rearrange("p a e i -> p (a e) i"),
                                      ALU.subtract).then_inc(v_L, 1)

                def maximum(i, c, hd):
                    b, h, u = at(i, c - 1)
                    dve.wait_ge(p_S, HEADS * b + hd + 1)
                    if hd == 0:
                        wait(dve, p_mT, b)
                    dve.tensor_reduce(mx[:, hd:hd + 1], psS[hd % 2][0:N, 0:M], AX.X, ALU.max).then_inc(v_max, 1)

                def normalise(i, c, half):
                    b, h, u = at(i, c - 2)
                    dve.wait_ge(p_PV, PAIRS * b + 4 * half + 4)
                    hs = slice(8 * half, 8 * half + 8)
                    o = psO[half][0:N, 0:8 * VW].rearrange("i (h w) -> i h w", w=VW)
                    dve.reciprocal(rden[:, hs], o[:, :, VW - 1]).then_inc(v_rd, 1)
                    dve.tensor_reduce(osum[:, hs, :], o[:, :, 0:3 * HD].rearrange("i h (k d) -> i h d k", k=3),
                                      AX.X, ALU.add).then_inc(v_os, 1)
                    dve.wait_ge(v_rd, 2 * b + half + 1)
                    dve.wait_ge(v_os, 2 * b + half + 1)
                    wait(dve, p_OT, b)
                    dve.tensor_tensor(on[:, hs, :], osum[:, hs, :],
                                      rden[:, hs].unsqueeze(2).to_broadcast([N, 8, HD]),
                                      ALU.mult).then_inc(v_on, 1)

                def transposed(i, c):
                    b, h, u = at(i, c)
                    dve.wait_ge(a_T, b + 1)
                    dve.tensor_tensor(cTL[:, :, 0:M], misc[0:CK].rearrange("p (c n) -> p c n", c=2)[:, :, 0:M],
                                      f32(cTH[:, :, 0:M]), ALU.subtract).then_inc(v_T, 1)

                def step(i, c):
                    for s in range(SLOTS):
                        if s == OT + 1 and live(i, c, 3):
                            b, h, u = at(i, c - 3)
                            dve.wait_ge(a_O, b + 1)
                            dve.tensor_tensor(oTL[:], psS[0][:, 0:2 * N].rearrange("p (c i) -> p c i", c=2),
                                              f32(oTH[:]), ALU.subtract).then_inc(v_O, 1)
                        heads = heads_at.get(s, ()) if live(i, c, 1) else ()
                        for hd in heads[0:1]:
                            maximum(i, c, hd)
                        if 0 < s <= SB and s - 1 not in POOL and live(i, c, 2):
                            low(i, c, s - 1)
                        if s == KP[-1] + 1 and live(i, c, 0):
                            b, h, u = at(i, c)
                            dve.wait_ge(a_K, b + 1)
                            dve.tensor_tensor(kL[:, u], misc[:].rearrange("p (m n) -> p m n", m=2)[:, :, 0:MP],
                                              f32(kH[:, u]), ALU.subtract).then_inc(v_K, 1)
                        for hd in heads[1:2]:
                            maximum(i, c, hd)
                        if s == MT and live(i, c, 1):
                            b, h, u = at(i, c - 1)
                            dve.wait_ge(p_mT, b + 1)
                            if not isinstance(i, int) or b > 0:
                                b1, h1, u1 = at(i, c - 2)
                                dve.wait_ge(d_m[u1], 16 * (h1 + 1))
                            dve.tensor_scalar(nm[:], psS[1][0:HEADS, 0:N], -1.0, None, ALU.mult
                                              ).then_inc(v_nm, 1)
                        if s == OP + 1 and live(i, c, 3):
                            b, h, u = at(i, c - 3)
                            dve.wait_ge(p_Wo, b + 1)
                            dve.scalar_tensor_tensor(out=X[:, bass.ds(b, 1), :], in0=psS[0][0:N, 0:DIM].unsqueeze(1),
                                                     scalar=tg[0:N, 0:1],
                                                     in1=X[:, bass.ds(b, 1), :], op0=ALU.mult, op1=ALU.add
                                                     ).then_inc(v_x1, 1)
                        if s == pv_slot(3) + 1 and live(i, c, 2):
                            normalise(i, c, 0)
                        if s == CT + 1 and live(i, c, -1):
                            transposed(i, c + 1)
                    if live(i, c, 2):
                        normalise(i, c, 1)

                pv_slot = lambda p: last_bank(p) + 3
                transposed(0, 0)
                steps(dve, step)


def experts(nc, v):
    (B, N, DIM, X, ident, tg, banks, misc, out) = (v[k] for k in "B N DIM X ident tg banks misc out".split())
    router_w, gate_w, gate_b, up_w, up_b, down_w, down_b = (
        v[k] for k in "router_w gate_w gate_b up_w up_b down_w down_b".split())
    xs_scr, y_scr, NT, ROWW = v["xs_scr"], v["y_scr"], v["NT"], v["ROWW"]
    E, FF = gate_w.shape[0], gate_w.shape[2]
    FC, DC = FF // 128, DIM // 128
    I32 = mybir.dt.int32
    XS = 2.0 ** 10
    WS = 2.0 ** 14

    with ExitStack() as stack:
        def sb(name, shape, dt):
            return stack.enter_context(nc.sbuf_tensor(name, shape, dt))

        def sem(name):
            return stack.enter_context(nc.semaphore(name))

        GH = sb("GH", [128, E, 2, DC, FF], F16)
        GL = sb("GL", [128, E, 2, DC, FF], F16)
        DH = sb("DH", [128, E, FC, DIM], F32R)
        DL = sb("DL", [128, E, FC, DIM], F32R)
        inv = sb("inv", [128, E], F32)
        gb = sb("gb", [128, E * FC], F32)
        ub = sb("ub", [128, E * FC], F32)
        tw = sb("tw", [N, 2, B], F32)
        tile_e = sb("tile_e", [1, NT], I32)
        db = sb("db", [E, DIM], F32)

        with ExitStack() as inner:
            def tmp(name, shape, dt):
                return inner.enter_context(nc.sbuf_tensor(name, shape, dt))

            def isem(name):
                return inner.enter_context(nc.semaphore(name))

            xn = tmp("xn2", [N, B, ROWW], F32)
            stats = tmp("stats2", [N, B, 6], F32)
            mv = tmp("mv2", [N, B, 2], F32)
            rstd, veps = tmp("rstd2", [N, B], F32), tmp("veps2", [N, B], F32)
            rw, rwT = tmp("rw", [E, DIM], F32), tmp("rwT", [128, DC, E], F32)
            braw = tmp("braw", [E * FC, 2, 128], F32)
            xT = tmp("xT2", [128, 2, DC, N], F32)
            raw = tmp("w_raw", [128, 2, 2, DC, FF], F32)
            draw = tmp("d_raw", [128, 2, FC, DIM], F32)
            sq = tmp("sq", [128, E], F32)
            half, unit, sc = tmp("half", [128, E], F32), tmp("unit", [128, E], F32), tmp("sc", [128, E], F32)
            upper, ones = tmp("upper", [N, N], F32), tmp("ones2", [128, 128], F32)
            R = {n: tmp("r_" + n, [N, B, E], F32) for n in
                 "low exp eq score sel1 rest sel2 both a0 a1 pos tie pick1 pick2 wsel".split()}
            r = {n: tmp("s_" + n, [N, B], F32) for n in
                 "m sum m1 t1 m2 t2 p1 p2 den rden rsum w1 w2 f1 f2".split()}
            pos = [tmp(f"pos{k}", [N, B], I32) for k in range(2)]
            c = {n: tmp("c_" + n, [N, E], F32) for n in "cnt pad e0 e1 base".split()}
            ci, ca = tmp("c_int", [N, E], I32), tmp("c_and", [N, E], I32)
            tie_i, start_i = tmp("tie_i", [N, B, E], I32), tmp("start_i", [1, NT, E], I32)
            start, past, nexp = tmp("start", [1, NT, E], F32), tmp("past", [1, NT, E], F32), tmp("nexp", [1, NT], F32)
            wselT = tmp("wselT", [E, 4, N], F32)
            assert B // 4 == E - 4

            i_sm, i_w = isem("small_in"), [isem(f"w_in{u}") for u in range(2)]
            i_d = [isem(f"d_in{u}") for u in range(2)]
            q_c, q_tri, q_iota, q_id = (isem(n) for n in ("pool_clear", "tri", "iota", "ids"))
            q_sc = [isem(f"rows_out{k}") for k in range(2)]
            t_rw, t_x, t_lg, t_rank, t_w, t_wb, t_n = (isem(n) for n in (
                "pe_rw", "pe_xT2", "pe_logits", "pe_rank", "pe_wselT", "pe_bias", "pe_norm"))
            s_x, s_exp, s_h, s_sq, s_n = (isem(n) for n in ("act_xT2", "act_exp2", "act_high", "act_sqrt2", "act_norm"))
            e_rw, e_st, e_mv, e_ve, e_rs, e_xn = (isem(n) for n in
                                                  ("dve_rw", "dve_st2", "dve_mv2", "dve_ve2", "dve_rs2", "dve_xn2"))
            e_r, e_low, e_sel, e_pos, e_wt, e_sc, e_l, e_dl, e_X = (isem(n) for n in (
                "dve_chain", "dve_low", "dve_sel", "dve_pos", "dve_wselT", "dve_scale", "dve_wlow", "dve_dlow",
                "dve_xbias"))
            e_ch = isem("dve_scale_chain")
            bX, bL, bR, bC = banks[0:2], banks[2], banks[3], banks[4]
            bN = [bank[:, 256:257] for bank in banks[4:6]]

            with nc.Block() as block:
                @block.sync
                def _(sp):
                    sp.dma_start(rw[:], router_w).then_inc(i_sm, 16)
                    for j, t in enumerate((gate_b, up_b)):
                        sp.dma_start(braw[:, j, :], t.rearrange("e (f p) -> (e f) p", p=128)).then_inc(i_sm, 16)
                    sp.dma_start(db[:], down_b).then_inc(i_sm, 16)

                    def load(i, u, before):
                        e = 2 * i + u
                        if before:
                            sp.wait_ge(e_l, e - 1)
                        for j, w in enumerate((gate_w, up_w)):
                            sp.dma_start(raw[:, u, j], w[bass.ds(e, 1)].rearrange("o (c p) f -> p (o c) f", p=128)
                                         ).then_inc(i_w[u], 16)
                        if before:
                            sp.wait_ge(e_dl, e - 1)
                        sp.dma_start(draw[:, u], down_w[bass.ds(e, 1)].rearrange("o (f p) d -> p (o f) d", p=128)
                                     ).then_inc(i_d[u], 16)

                    load(0, 0, False)
                    load(0, 1, False)
                    with sp.Fori(1, E // 2) as i:
                        for u in range(2):
                            load(i, u, True)

                @block.gpsimd
                def _(pool):
                    pool.memset(upper[:], 0.0).then_inc(q_c, 1)
                    pool.wait_ge(q_c, 1)
                    pool.affine_select(out=upper[:], in_=upper[:], compare_op=ALU.is_ge, fill=1.0, base=0,
                                       pattern=[[-1, N]], channel_multiplier=1).then_inc(q_tri, 1)
                    pool.wait_ge(q_tri, 1)
                    pool.memset(ones[:], 1.0).then_inc(q_tri, 1)
                    pool.wait_ge(q_tri, 2)
                    pool.iota(tie_i[:], pattern=[[0, B], [-1, E]], base=E, channel_multiplier=0).then_inc(q_iota, 1)
                    pool.wait_ge(q_iota, 1)
                    pool.iota(start_i[:], pattern=[[128, NT], [0, E]], base=0, channel_multiplier=0
                              ).then_inc(q_iota, 1)
                    pool.wait_ge(q_iota, 2)
                    for k in range(2):
                        if k:
                            pool.wait_ge(q_sc[0], 16 * B)
                        pool.iota(xn[:, :, DIM:ROWW].rearrange("i b o -> i (b o)").bitcast(I32),
                                  pattern=[[2 * N, B]], base=k, channel_multiplier=2).then_inc(q_id, 1)
                        pool.wait_ge(q_id, k + 1)
                        if k == 0:
                            pool.wait_ge(e_xn, B)
                            pool.wait_ge(e_pos, 2)
                        for b in range(B):
                            pool.indirect_dma_start(
                                xs_scr, bass.IndirectOffsetOnAxis(ap=pos[k][:, b:b + 1].bitcast(mybir.dt.uint32), axis=0),
                                xn[:, b, :], None).then_inc(q_sc[k], 16)
                    pool.wait_ge(q_sc[1], 16 * B)

                @block.scalar
                def _(act):
                    def norm(e, i, u):
                        act.wait_ge(i_w[u], 32 * (i + 1))
                        act.activation(GL[:, bass.ds(e, 1)].rearrange("p e j c f -> p (e j c f)"),
                                       raw[:, u].rearrange("p j c f -> p (j c f)"), ACT.Square,
                                       accum_out=sq[:, bass.ds(e, 1)]).then_inc(s_n, 1)

                    def high(e, i, u):
                        act.wait_ge(e_sc, e + 1)
                        act.activation(GH[:, bass.ds(e, 1)].rearrange("p e j c f -> p (e j c f)"),
                                       raw[:, u].rearrange("p j c f -> p (j c f)"), ACT.Copy,
                                       scale=sc[:, bass.ds(e, 1)]).then_inc(s_h, 1)
                        act.wait_ge(i_d[u], 16 * (i + 1))
                        act.activation(DH[:, bass.ds(e, 1)].rearrange("p e f d -> p (e f d)"),
                                       draw[:, u].rearrange("p f d -> p (f d)"), ACT.Copy).then_inc(s_h, 1)

                    norm(0, 0, 0)
                    norm(1, 0, 1)
                    act.wait_ge(e_ve, 1)
                    act.activation(rstd[:], veps[:], ACT.Sqrt).then_inc(s_sq, 1)
                    for b in range(B):
                        u = b % 2
                        act.wait_ge(t_x, b + 1)
                        if b >= 2:
                            act.wait_ge(t_lg, b - 1)
                        act.activation(xT[:, u], bX[u][:, 0:DC * N].rearrange("p (c i) -> p c i", c=DC), ACT.Copy
                                       ).then_inc(s_x, 1)
                        if b == B // 4 - 1:
                            high(0, 0, 0)
                        if b == B // 2 - 1:
                            high(1, 0, 1)
                    norm(2, 1, 0)
                    act.wait_ge(e_low, 1)
                    act.activation(R["exp"][:], R["low"][:], ACT.Exp).then_inc(s_exp, 1)
                    high(2, 1, 0)
                    with act.Fori(1, E // 2 - 1) as i:
                        for e, k, u in ((2 * i + 1, i, 1), (2 * i + 2, i + 1, 0)):
                            norm(e, k, u)
                            high(e, k, u)
                    norm(E - 1, E // 2 - 1, 1)
                    high(E - 1, E // 2 - 1, 1)

                @block.tensor
                def _(pe):
                    pe.wait_ge(i_sm, 64)
                    for k in range(DC):
                        pe.transpose(bC[:, E * k:E * (k + 1)], rw[:, 128 * k:128 * (k + 1)], ident[0:E, 0:E])
                    for j in range(2):
                        mm = pe.transpose(bC[:, 64 + 32 * j:64 + 32 * j + E * FC], braw[:, j, :],
                                          ident[0:E * FC, 0:E * FC])
                    mm.then_inc(t_rw, 1)
                    pe.wait_ge(q_tri, 2)

                    def norm(e):
                        pe.wait_ge(s_n, e + 1)
                        if e >= 2:
                            pe.wait_ge(e_sc, e - 1)
                        pe.matmul(bN[e % 2], ones[:], sq[:, e:e + 1], start=True, stop=True
                                  ).then_inc(t_n, 1)

                    pe.wait_ge(e_rw, 3)
                    norm(0)
                    norm(1)

                    def turn(b):
                        pe.wait_ge(e_xn, b + 1)
                        if b >= 2:
                            pe.wait_ge(s_x, b - 1)
                        for k in range(DC):
                            mm = pe.transpose(bX[b % 2][:, N * k:N * (k + 1)], xn[:, b, 128 * k:128 * (k + 1)],
                                              ident[0:N, 0:N])
                        mm.then_inc(t_x, 1)

                    turn(0)
                    for b in range(B):
                        if b + 1 < B:
                            turn(b + 1)
                        pe.wait_ge(s_x, b + 1)
                        for k in range(DC):
                            mm = pe.matmul(bL[0:N, b * E:(b + 1) * E], xT[:, b % 2, k, :], rwT[:, k, :],
                                           start=(k == 0), stop=(k == DC - 1))
                        mm.then_inc(t_lg, 1)
                    norm(2)
                    pe.wait_ge(e_sel, 1)
                    flat = R["both"][:].rearrange("i b e -> i (b e)")
                    pe.matmul(bR[0:N, 0:B * E], upper[:], flat, start=True, stop=True)
                    pe.matmul(bR[0:N, 256:256 + B * E], ones[0:N, 0:N], flat, start=True, stop=True).then_inc(t_rank, 1)
                    pe.wait_ge(e_pos, 3)
                    for e in range(3, E):
                        norm(e)
                        g = e - 3
                        if g == B // 4:
                            break
                        if g >= 1:
                            pe.wait_ge(e_X, 2 * g)
                        for b in range(4):
                            mm = pe.transpose(bR[0:E, N * b:N * (b + 1)], R["wsel"][:, 4 * g + b, :],
                                              ident[0:N, 0:N])
                        mm.then_inc(t_w, 1)
                        pe.wait_ge(e_wt, g + 1)
                        for b in range(4):
                            mm = pe.matmul(bX[b // 2][0:N, DIM * (b % 2):DIM * (b % 2 + 1)], wselT[:, b, :],
                                           db[:], start=True, stop=True)
                        mm.then_inc(t_wb, 1)

                @block.vector
                def _(dve):
                    n_chain = [0]

                    def link(ins):
                        n_chain[0] += 1
                        ins.then_inc(e_r, 1)
                        dve.wait_ge(e_r, n_chain[0])

                    dve.wait_ge(t_rw, 1)
                    dve.tensor_copy(rwT[:], bC[:, 0:DC * E].rearrange("p (c e) -> p c e", c=DC)).then_inc(e_rw, 1)
                    dve.tensor_copy(gb[:], bC[:, 64:64 + E * FC]).then_inc(e_rw, 1)
                    dve.tensor_copy(ub[:], bC[:, 96:96 + E * FC]).then_inc(e_rw, 1)
                    layer_norm_stats(dve, X, stats, mv, veps, rstd, B, e_st, e_mv, e_ve, s_sq, e_rs)
                    for b in range(B):
                        dve.tensor_scalar(xn[:, b, 0:DIM], X[:, b, :], mv[:, b, 0:1], rstd[:, b:b + 1],
                                          ALU.subtract, ALU.mult).then_inc(e_xn, 1)

                    def scale(e, u):
                        one = lambda t: t[:, bass.ds(e, 1)]
                        dve.wait_ge(t_n, e + 1)
                        dve.tensor_scalar(one(half).bitcast(I32), bN[u].bitcast(I32), 0x7F000000, 1,
                                          ALU.bitwise_and, ALU.logical_shift_right).then_inc(e_ch, 1)
                        dve.wait_ge(e_ch, 4 * e + 1)
                        dve.tensor_scalar(one(unit), one(half), 2.0 ** -124, 2.0 ** 64 / WS, ALU.max, ALU.mult
                                          ).then_inc(e_ch, 1)
                        dve.wait_ge(e_ch, 4 * e + 2)
                        dve.reciprocal(one(sc), one(unit)).then_inc(e_sc, 1)
                        dve.tensor_scalar(one(inv), one(unit), 1.0 / XS, None, ALU.mult).then_inc(e_ch, 1)
                        dve.wait_ge(e_sc, e + 1)
                        dve.tensor_scalar(ub[:, bass.ds(e * FC, FC)], ub[:, bass.ds(e * FC, FC)], one(sc), XS,
                                          ALU.mult, ALU.mult).then_inc(e_ch, 1)

                    def low(e, u):
                        dve.wait_ge(s_h, 2 * e + 1)
                        dve.scalar_tensor_tensor(
                            out=GL[:, bass.ds(e, 1)].rearrange("p e j c f -> p (e j c f)"),
                            in0=raw[:, u].rearrange("p j c f -> p (j c f)"), scalar=sc[:, bass.ds(e, 1)],
                            in1=GH[:, bass.ds(e, 1)].rearrange("p e j c f -> p (e j c f)"),
                            op0=ALU.mult, op1=ALU.subtract).then_inc(e_l, 1)
                        dve.wait_ge(s_h, 2 * e + 2)
                        dve.tensor_tensor(DL[:, bass.ds(e, 1)].rearrange("p e f d -> p (e f d)"),
                                          draw[:, u].rearrange("p f d -> p (f d)"),
                                          f32(DH[:, bass.ds(e, 1)].rearrange("p e f d -> p (e f d)")),
                                          ALU.subtract).then_inc(e_dl, 1)

                    scale(0, 0)
                    scale(1, 1)
                    low(0, 0)
                    low(1, 1)
                    dve.wait_ge(q_iota, 2)
                    link(dve.tensor_copy(R["tie"][:], tie_i[:]))
                    link(dve.tensor_copy(start[:], start_i[:]))
                    dve.wait_ge(t_lg, B)
                    logits = bL[0:N, 0:B * E].rearrange("i (b e) -> i b e", e=E)
                    wide = lambda t: t[:].unsqueeze(2).to_broadcast([N, B, E])
                    link(dve.tensor_reduce(r["m"][:], logits, AX.X, ALU.max))
                    dve.tensor_tensor(R["low"][:], logits, wide(r["m"]), ALU.subtract).then_inc(e_low, 1)
                    dve.wait_ge(s_exp, 1)
                    link(dve.tensor_reduce(r["sum"][:], R["exp"][:], AX.X, ALU.add))
                    for k, src in ((1, R["exp"]), (2, R["rest"])):
                        mk, tk, sel = r[f"m{k}"], r[f"t{k}"], R[f"sel{k}"]
                        link(dve.tensor_reduce(mk[:], src[:], AX.X, ALU.max))
                        link(dve.tensor_tensor(R["eq"][:], src[:], wide(mk), ALU.is_equal))
                        link(dve.tensor_tensor(R["score"][:], R["eq"][:], R["tie"][:], ALU.mult))
                        link(dve.tensor_reduce(tk[:], R["score"][:], AX.X, ALU.max))
                        link(dve.tensor_tensor(sel[:], R["score"][:], wide(tk), ALU.is_equal))
                        if k == 1:
                            link(dve.scalar_tensor_tensor(out=R["rest"][:], in0=sel[:], scalar=-4.0, in1=src[:],
                                                          op0=ALU.mult, op1=ALU.add))
                    dve.tensor_tensor(R["both"][:], R["sel1"][:], R["sel2"][:], ALU.add).then_inc(e_sel, 1)
                    scale(2, 0)
                    dve.wait_ge(t_rank, 1)
                    rank = bR[0:N, 0:B * E].rearrange("i (b e) -> i b e", e=E)
                    total = bR[0:N, 256:256 + B * E].rearrange("i (b e) -> i b e", e=E)
                    link(dve.tensor_copy(R["a0"][:], total))
                    a, b_ = R["a0"], R["a1"]
                    sh = 1
                    while sh < B:
                        link(dve.tensor_tensor(b_[:, sh:B, :], a[:, sh:B, :], a[:, 0:B - sh, :], ALU.add))
                        link(dve.tensor_copy(b_[:, 0:sh, :], a[:, 0:sh, :]))
                        a, b_, sh = b_, a, 2 * sh
                    link(dve.tensor_scalar(ci[:], a[:, B - 1, :], 127.0, None, ALU.add))
                    link(dve.tensor_scalar(ca[:], ci[:], -128, None, ALU.bitwise_and))
                    link(dve.tensor_copy(c["pad"][:], ca[:]))
                    link(dve.tensor_copy(c["e0"][:], c["pad"][:]))
                    x0, x1, sh = c["e0"], c["e1"], 1
                    while sh < E:
                        link(dve.tensor_tensor(x1[:, sh:E], x0[:, sh:E], x0[:, 0:E - sh], ALU.add))
                        link(dve.tensor_copy(x1[:, 0:sh], x0[:, 0:sh]))
                        x0, x1, sh = x1, x0, 2 * sh
                    link(dve.tensor_tensor(c["base"][:], x0[:], c["pad"][:], ALU.subtract))
                    link(dve.tensor_tensor(b_[:], a[:], total, ALU.subtract))
                    link(dve.tensor_tensor(a[:], b_[:], rank, ALU.add))
                    link(dve.tensor_tensor(R["pos"][:], a[:], c["base"][:].unsqueeze(1).to_broadcast([N, B, E]),
                                           ALU.add))
                    for k in range(2):
                        link(dve.tensor_tensor(R[f"pick{k + 1}"][:], R["pos"][:], R[f"sel{k + 1}"][:], ALU.mult))
                        link(dve.tensor_reduce(r[f"f{k + 1}"][:], R[f"pick{k + 1}"][:], AX.X, ALU.add))
                        dve.tensor_copy(pos[k][:], r[f"f{k + 1}"][:]).then_inc(e_pos, 1)
                    link(dve.tensor_tensor(past[:], start[:], x0[0:1, :].unsqueeze(1).to_broadcast([1, NT, E]),
                                           ALU.is_ge))
                    link(dve.tensor_reduce(nexp[:], past[:], AX.X, ALU.add))
                    link(dve.tensor_scalar(tile_e[:], nexp[:], float(E - 1), None, ALU.min))
                    link(dve.reciprocal(r["rsum"][:], r["sum"][:]))
                    link(dve.tensor_tensor(r["p1"][:], r["m1"][:], r["rsum"][:], ALU.mult))
                    link(dve.tensor_tensor(r["p2"][:], r["m2"][:], r["rsum"][:], ALU.mult))
                    link(dve.scalar_tensor_tensor(out=r["den"][:], in0=r["p1"][:], scalar=1e-9, in1=r["p2"][:],
                                                  op0=ALU.add, op1=ALU.add))
                    link(dve.reciprocal(r["rden"][:], r["den"][:]))
                    for k in range(2):
                        link(dve.scalar_tensor_tensor(out=tw[:, k, :], in0=r[f"p{k + 1}"][:], scalar=tg[0:N, 1:2],
                                                      in1=r["rden"][:], op0=ALU.mult, op1=ALU.mult))
                        link(dve.tensor_tensor(R[f"pick{k + 1}"][:], R[f"sel{k + 1}"][:],
                                               tw[:, k, :].unsqueeze(2).to_broadcast([N, B, E]), ALU.mult))
                    dve.tensor_tensor(R["wsel"][:], R["pick1"][:], R["pick2"][:], ALU.add).then_inc(e_pos, 1)
                    low(2, 0)

                    with dve.Fori(1, E // 2 - 1) as i:
                        for e, u in ((2 * i + 1, 1), (2 * i + 2, 0)):
                            scale(e, u)
                            dve.wait_ge(t_w, e - 2)
                            dve.tensor_copy(wselT[:], bR[0:E, 0:4 * N].rearrange("e (b i) -> e b i", b=4)
                                            ).then_inc(e_wt, 1)
                            low(e, u)
                            dve.wait_ge(t_wb, e - 2)
                            for m in range(2):
                                rows = X[:, bass.ds(4 * (e - 3) + 2 * m, 2), :]
                                dve.tensor_tensor(rows, rows, bX[m][0:N, :].rearrange("i (b d) -> i b d", b=2),
                                                  ALU.add).then_inc(e_X, 1)
                    scale(E - 1, 1)
                    low(E - 1, 1)

        UN = 4
        xt = sb("xt", [128, UN, ROWW], F32)
        xH, xL = sb("xH", [128, 2, DC, 128], F16), sb("xL", [128, 2, DC, 128], F16)
        sg, hf = sb("sg", [128, FC, 128], F32), sb("hf", [128, FC, 128], F32)
        hH, hL = sb("hH", [128, 2, FC, 128], F32R), sb("hL", [128, 2, FC, 128], F32R)
        where = sb("where", [128, UN], I32)
        v_id = sem("dve_where")
        ys = sb("ys", [128, UN, DIM], F32)
        l_x = [sem(f"tile_in{u}") for u in range(UN)]
        y_out = [sem(f"tile_out{u}") for u in range(UN)]
        k_T, k_GU, k_D = sem("pe_tileT"), sem("pe_gate_up"), sem("pe_down")
        a_x, a_s, a_h = sem("act_tile_x"), sem("act_silu"), sem("act_h")
        v_x, v_h, v_l, v_y = sem("dve_tile_x"), sem("dve_h"), sem("dve_hlow"), sem("dve_y")
        bT, bG, bU, bY = [banks[0], banks[5]], banks[1:3], banks[3:5], [misc[:, 0:512], misc[:, 512:1024]]

        def tiles(eng, step):
            first = UN + 2
            count = (NT - first) // UN
            for n in range(first):
                step(0, n)
            with eng.Fori(1, 1 + count) as i:
                for c in range(2, UN + 2):
                    step(i, c)
            for n in range(first + UN * count, NT + 2):
                step(0, n)

        def has(i, c, back):
            return not isinstance(i, int) or 0 <= UN * i + c - back < NT

        def at(i, c):
            return UN * i + c, i + c // UN, c % UN, c % 2

        def wait(eng, s, value):
            if not isinstance(value, int) or value > 0:
                eng.wait_ge(s, value)

        def expert(eng, t):
            return eng.value_load(tile_e[0:1, bass.ds(t, 1)], min_val=0, max_val=E - 1)

        def two_experts(eng, i, c, kept):
            one = expert(eng, UN * i + c - 1) if has(i, c, 1) else None
            two = kept.get((id(i) if not isinstance(i, int) else 0, c - 2))
            if two is None and has(i, c, 2):
                two = expert(eng, UN * i + c - 2)
            kept[(id(i) if not isinstance(i, int) else 0, c - 1)] = one
            return one, two

        with nc.Block() as block:
            @block.sync
            def _(sp):
                def step(i, c):
                    if has(i, c, 0):
                        t, h, s, u = at(i, c)
                        wait(sp, k_T, t - UN + 1)
                        wait(sp, v_id, t - UN + 1)
                        sp.dma_start(xt[:, s, :], xs_scr[bass.ds(128 * t, 128), :]).then_inc(l_x[s], 16)

                tiles(sp, step)

            @block.gpsimd
            def _(pool):
                for t in range(NT):
                    s = t % UN
                    pool.wait_ge(v_y, t + 1)
                    pool.indirect_dma_start(
                        y_scr, bass.IndirectOffsetOnAxis(ap=where[:, s:s + 1].bitcast(mybir.dt.uint32), axis=0),
                        ys[:, s, :], None).then_inc(y_out[s], 16)
                for s in range(UN):
                    pool.wait_ge(y_out[s], 16 * ((NT + UN - 1 - s) // UN))

            @block.scalar
            def _(act):
                def step(i, c):
                    if has(i, c, 1):
                        e = expert(act, UN * i + c - 1)
                    if has(i, c, 0):
                        t, h, s, u = at(i, c)
                        act.wait_ge(k_T, t + 1)
                        wait(act, k_GU, t - 1)
                        act.activation(xH[:, u], bT[u][:, 0:DC * 128].rearrange("p (c s) -> p c s", c=DC), ACT.Copy,
                                       scale=XS).then_inc(a_x, 1)
                    if has(i, c, 1):
                        t, h, s, u = at(i, c - 1)
                        act.wait_ge(k_GU, t + 1)
                        for f in range(FC):
                            wait(act, v_h, FC * (t - 1) + f + 1)
                            act.activation(sg[:, f, :], bG[u][:, 128 * f:128 * (f + 1)], ACT.Silu,
                                           bias=gb[:, bass.ds(e * FC + f, 1)], scale=inv[:, bass.ds(e, 1)]
                                           ).then_inc(a_s, 1)
                        act.wait_ge(v_h, FC * (t + 1))
                        wait(act, k_D, t - 1)
                        act.activation(hH[:, u], hf[:], ACT.Copy).then_inc(a_h, 1)

                tiles(act, step)

            @block.tensor
            def _(pe):
                kept = {}

                def step(i, c):
                    e1, e2 = two_experts(pe, i, c, kept)
                    if has(i, c, 0):
                        t, h, s, u = at(i, c)
                        pe.wait_ge(l_x[s], 16 * (h + 1))
                        wait(pe, v_x, t - 1)
                        for k in range(DC):
                            mm = pe.transpose(bT[u][:, 128 * k:128 * (k + 1)], xt[:, s, 128 * k:128 * (k + 1)],
                                              ident[:])
                        mm.then_inc(k_T, 1)
                    if has(i, c, 1):
                        t, h, s, u = at(i, c - 1)
                        pe.wait_ge(v_x, t + 1)
                        wait(pe, a_s, FC * (t - 1))
                        wait(pe, v_h, FC * (t - 1))
                        for j, bank in enumerate((bG[u], bU[u])):
                            for f in range(FC):
                                for n, (W, x) in enumerate(((GH, xH), (GH, xL), (GL, xH))):
                                    for k in range(DC):
                                        w = W[:, bass.ds(e1, 1), j, k, 128 * f:128 * (f + 1)]
                                        mm = pe.matmul(bank[:, 128 * f:128 * (f + 1)], w.rearrange("p o f -> p (o f)"),
                                                       x[:, u, k, :], start=(n == 0 and k == 0),
                                                       stop=(n == 2 and k == DC - 1))
                        mm.then_inc(k_GU, 1)
                    if has(i, c, 2):
                        t, h, s, u = at(i, c - 2)
                        pe.wait_ge(v_l, t + 1)
                        wait(pe, v_y, t - 1)
                        for n, (W, x) in enumerate(((DH, hH), (DL, hH), (DH, hL))):
                            for f in range(FC):
                                mm = pe.matmul(bY[u][:, 0:DIM], x[:, u, f, :],
                                               W[:, bass.ds(e2, 1), f, :].rearrange("p o d -> p (o d)"),
                                               start=(n == 0 and f == 0), stop=(n == 2 and f == FC - 1))
                        mm.then_inc(k_D, 1)

                tiles(pe, step)

            @block.vector
            def _(dve):
                kept = {}

                def step(i, c):
                    e1, e2 = two_experts(dve, i, c, kept)
                    if has(i, c, 0):
                        t, h, s, u = at(i, c)
                        dve.wait_ge(a_x, t + 1)
                        dve.scalar_tensor_tensor(out=xL[:, u], in0=bT[u][:, 0:DC * 128].rearrange("p (c s) -> p c s", c=DC),
                                                 scalar=XS, in1=xH[:, u], op0=ALU.mult, op1=ALU.subtract
                                                 ).then_inc(v_x, 1)
                        dve.wait_ge(l_x[s], 16 * (h + 1))
                        wait(dve, y_out[s], 16 * h)
                        dve.tensor_copy(where[:, s:s + 1], xt[:, s, DIM:ROWW].bitcast(I32)).then_inc(v_id, 1)
                    if has(i, c, 1):
                        t, h, s, u = at(i, c - 1)
                        wait(dve, v_l, t)
                        for f in range(FC):
                            dve.wait_ge(a_s, FC * t + f + 1)
                            dve.scalar_tensor_tensor(out=hf[:, f, :], in0=bU[u][:, 128 * f:128 * (f + 1)],
                                                     scalar=ub[:, bass.ds(e1 * FC + f, 1)], in1=sg[:, f, :],
                                                     op0=ALU.add, op1=ALU.mult).then_inc(v_h, 1)
                        dve.wait_ge(a_h, t + 1)
                        dve.tensor_tensor(hL[:, u], hf[:], f32(hH[:, u]), ALU.subtract).then_inc(v_l, 1)
                    if has(i, c, 2):
                        t, h, s, u = at(i, c - 2)
                        dve.wait_ge(k_D, t + 1)
                        wait(dve, y_out[s], 16 * h)
                        dve.wait_ge(v_id, t + 1)
                        dve.tensor_scalar(ys[:, s, :], bY[u][:, 0:DIM], inv[:, bass.ds(e2, 1)], None, ALU.mult
                                          ).then_inc(v_y, 1)

                tiles(dve, step)

        QB = 4
        yt = sb("yt", [N, 2, QB, 2, DIM], F32)
        y_in = [sem(f"y_in{u}") for u in range(2)]
        y_add, s_out = sem("y_added"), sem("out_written")
        y_rows = y_scr[0:2 * B * N, :].rearrange("(b i k) d -> i b k d", i=N, k=2)
        out_rows = out.rearrange("b i d -> i b d")
        with nc.Block() as block:
            @block.sync
            def _(sp):
                for g in range(B // QB):
                    if g >= 2:
                        sp.wait_ge(y_add, 2 * QB * (g - 1))
                    sp.dma_start(yt[:, g % 2], y_rows[:, QB * g:QB * (g + 1)]).then_inc(y_in[g % 2], 16)

            @block.scalar
            def _(act):
                for g in range(B // QB):
                    act.wait_ge(y_add, 2 * QB * (g + 1))
                    act.dma_start(out_rows[:, QB * g:QB * (g + 1), :], X[:, QB * g:QB * (g + 1), :]).then_inc(s_out, 16)
                act.wait_ge(s_out, 16 * (B // QB))

            @block.vector
            def _(dve):
                for g in range(B // QB):
                    dve.wait_ge(y_in[g % 2], 16 * (g // 2 + 1))
                    for k in range(2):
                        for q in range(QB):
                            b = QB * g + q
                            if k:
                                dve.wait_ge(y_add, 2 * QB * g + q + 1)
                            dve.scalar_tensor_tensor(out=X[:, b, :], in0=yt[:, g % 2, q, k, :], scalar=tw[:, k, b:b + 1],
                                                     in1=X[:, b, :], op0=ALU.mult, op1=ALU.add).then_inc(y_add, 1)


def layer_norm_stats(dve, X, stats, mv, veps, rstd, B, s_st, s_mv, s_ve, s_sq, s_rs):
    for b in range(B):
        dve.bn_stats(stats[:, b, :], X[:, b, :]).then_inc(s_st, 1)
    dve.wait_ge(s_st, B)
    for b in range(B):
        dve.bn_aggr(mv[:, b, :], stats[:, b, :]).then_inc(s_mv, 1)
    dve.wait_ge(s_mv, B)
    dve.tensor_scalar(veps[:], mv[:, :, 1], LN_EPS, None, ALU.add).then_inc(s_ve, 1)
    dve.wait_ge(s_sq, 1)
    dve.reciprocal(rstd[:], rstd[:]).then_inc(s_rs, 1)
    dve.wait_ge(s_rs, 1)


_INS = ["x", "ctx_768", "mask_BxS2_bf1", "g_xattn", "g_ffn", "L0_xattn_Wq", "L0_xattn_Wk", "L0_xattn_Wv",
        "L0_xattn_Wo", "L0_ffn_router_w", "L0_ffn_gate_w", "L0_ffn_gate_b", "L0_ffn_up_w", "L0_ffn_up_b",
        "L0_ffn_down_w", "L0_ffn_down_b"]


def kernel(**inputs):
    import numpy as _np
    import concourse.bacc as _bacc
    from concourse.bass_utils import run_bass_kernel_spmd as _run

    nc = _bacc.Bacc("TRN2", target_bir_lowering=False, num_devices=1)
    arrays, args = {}, []
    for name in _INS:
        a = _np.ascontiguousarray(inputs[name])
        if a.dtype == _np.bool_:
            a = a.view(_np.uint8)
        arrays[f"in_{name}"] = a
        args.append(nc.dram_tensor(f"in_{name}", a.shape, mybir.dt.from_np(a.dtype), kind="ExternalInput").ap())
    out = nc.dram_tensor("out", inputs["x"].shape, F32, kind="ExternalOutput").ap()
    build(nc, *args, out)
    return _run(nc, [arrays], core_ids=[0]).results[0]["out"]
```

```python
from contextlib import ExitStack

import concourse.bass as bass
from concourse import mybir

F32 = mybir.dt.float32
F32R = mybir.dt.float32r
BF16 = mybir.dt.bfloat16
F16 = mybir.dt.float16
U8 = mybir.dt.uint8
ALU = mybir.AluOpType
ACT = mybir.ActivationFunctionType
AX = mybir.AxisListType

HEADS = 16
PAIRS = HEADS // 2
LN_EPS = 1e-5
HIDDEN = float(2.0 ** 126)


def f32(ap):
    return ap.bitcast(F32)


def build(nc, x, ctx_768, mask, g_xattn, g_ffn, Wq, Wk, Wv, Wo, router_w, gate_w, gate_b, up_w, up_b,
          down_w, down_b, out):
    B, N, DIM = x.shape
    M, CTX = ctx_768.shape[1], ctx_768.shape[2]
    HD = DIM // HEADS
    JT = 3
    JP = M // JT
    MP = M + M % 2
    CK = CTX // 2
    GB = 4
    GROUPS = B // GB
    NI = 128
    VW = 3 * HD + 1
    RB, RM = 96, 97
    SCALE = HD ** -0.5
    NB = 3

    q_scr = nc.dram_tensor("q_scr", [2, B, DIM, N], F32, kind="Internal").ap()
    k_scr = nc.dram_tensor("k_scr", [NB, 2, DIM, MP], F32, kind="Internal").ap()
    bias_scr = nc.dram_tensor("bias_scr", [B, MP], F32, kind="Internal").ap()

    E = gate_w.shape[0]
    TOP_K = 2
    TS = 256
    NT = TOP_K * B * N // TS + E - 1
    ROWW = DIM + 1
    EK = 5
    PARTS = -(-NT * TS // (128 * EK))
    xs_scr = nc.dram_tensor("xs_scr", [PARTS * EK * 128, ROWW], F32, kind="Internal").ap()
    y_scr = nc.dram_tensor("y_scr", [TOP_K * B * N + EK * 128, DIM], F32, kind="Internal").ap()

    with ExitStack() as whole:
        def keep(name, shape, dt):
            return whole.enter_context(nc.sbuf_tensor(name, shape, dt))

        def sem(name):
            return whole.enter_context(nc.semaphore(name))

        X = keep("X", [N, B, DIM], F32)
        ident = keep("ident", [128, 128], F32)
        gates = keep("gates", [128, 2], F32)
        tg = keep("tg", [128, 2], F32)
        mv2 = keep("mv2", [N, B, 2], F32)
        routed = keep("routed", [N, B, router_w.shape[0]], F32)
        sq = keep("sq", [128, router_w.shape[0]], F32)
        banks = [whole.enter_context(nc.psum_tensor(f"bank{i}", [128, 512], F32)) for i in range(6)]
        misc = whole.enter_context(nc.psum_tensor("misc", [128, 1024], F32))
        psS, psST, psO = banks[0:2], banks[2:4], banks[4:6]

        attention(nc, locals())
        experts(nc, locals())


def attention(nc, v):
    (x, ctx_768, mask, Wq, Wk, Wv, Wo, X, ident, gates, tg, psS, psST, psO, misc) = (
        v[k] for k in "x ctx_768 mask Wq Wk Wv Wo X ident gates tg psS psST psO misc".split())
    (B, N, DIM, M, HD, JT, JP, MP, CK, GB, GROUPS, NI, VW, RB, RM, SCALE, NB) = (
        v[k] for k in "B N DIM M HD JT JP MP CK GB GROUPS NI VW RB RM SCALE NB".split())
    router_w, gate_w, up_w, mv2, routed, sq = (v[k] for k in "router_w gate_w up_w mv2 routed sq".split())
    E = router_w.shape[0]
    q_scr, k_scr, bias_scr = v["q_scr"], v["k_scr"], v["bias_scr"]
    CTX = 2 * CK

    with ExitStack() as stack:
        def sb(name, shape, dt):
            return stack.enter_context(nc.sbuf_tensor(name, shape, dt))

        def sem(name):
            return stack.enter_context(nc.semaphore(name))

        shapes = {"q": (Wq, 128), "k": (Wk, CK), "v": (Wv, CK), "o": (Wo, 128)}
        WH = {k: sb(f"w{k}_h", [p, 2, DIM], F32R) for k, (_, p) in shapes.items()}
        WL = {k: sb(f"w{k}_l", [p, 2, DIM], F32R) for k, (_, p) in shapes.items()}
        rw, rwT = sb("rw", [E, DIM], F32), sb("rwT", [128, 2, E], F32)
        cTH = sb("cTH", [CK, 2, MP], F32R)
        cTL = sb("cTL", [CK, 2, MP], F32R)
        KS = [sb(f"KS{u}", [128, PAIRS, MP], F32R) for u in range(NB)]
        QS = [sb(f"QS{u}", [128, PAIRS, 2, NI], F32R) for u in range(NB)]
        VS = sb("VS", [JP, NB, JT, HEADS, VW], BF16)
        ctx_sb = sb("ctx_sb", [JP, NB, JT, CTX], F32)
        kH = sb("kH", [128, NB, 2, MP], F32R)
        kL = sb("kL", [128, NB, 2, MP], F32R)
        vf = sb("vf", [JP, NB, JT, DIM], F32)
        mx = sb("mx", [N, HEADS], F32)
        nm = sb("nm", [HEADS, N], F32R)
        rden = sb("rden", [N, HEADS], F32)
        early = stack.enter_context(ExitStack())
        first = lambda name, shape, dt: early.enter_context(nc.sbuf_tensor(name, shape, dt))
        Wf = {k: first(f"w{k}_f", [p, 2, DIM], F32) for k, (_, p) in shapes.items()}
        mask_sb = first("mask_sb", [B, M], U8)
        bias_sb = first("bias_sb", [B, MP], F32)
        stats = first("stats", [N, B, 6], F32)
        mv = first("mv", [N, B, 2], F32)
        rstd = first("rstd", [N, B], F32)
        veps = first("veps", [N, B], F32)
        xn = first("xn", [N, 2, GB, DIM], F32)
        xTH = first("xTH", [128, 2, 2, GB * N], F32R)
        xTL = first("xTL", [128, 2, 2, GB * N], F32R)
        qH = first("qH", [128, GROUPS, 2, GB * N], F32R)
        qL = first("qL", [128, GROUPS, 2, GB * N], F32R)
        early.close()
        UN = PAIRS * JT
        PT = sb("PT", [JP, UN, 2, NI], F32)
        PL = sb("PL", [JP, UN, 2, NI], F16)
        PH = PT[:].rearrange("p u e i -> p (u e i)").bitcast(BF16).rearrange(
            "p (u e i two) -> p u e i two", u=UN, e=2, two=2)[:, :, :, :, 1]
        vr = sb("vr", [JP, JT, DIM], F32)
        osum = sb("osum", [N, HEADS, HD], F32)
        on = sb("on", [N, HEADS, HD], F32)
        oTH = sb("oTH", [128, 2, N], F32R)
        oTL = sb("oTL", [128, 2, N], F32R)

        s_w = {k: sem(f"w{k}_in") for k in shapes}
        s_x, s_g, s_m = sem("x_in"), sem("gates_in"), sem("mask_in")
        s_id0, s_id = sem("ident_zero"), sem("ident_ready")
        s_clear, s_wh, s_wl, s_bias = sem("cleared"), sem("w_high"), sem("w_low"), sem("bias_ready")
        s_st, s_mv, s_ve, s_sq, s_rs = (sem(n) for n in ("ln_stats", "ln_mv", "ln_veps", "ln_sqrt", "ln_rstd"))
        s_xn, s_xt, s_xh, s_xl = sem("xn_ready"), sem("xT_ready"), sem("xT_high"), sem("xT_low")
        s_qp, s_qh, s_ql = sem("q_psum"), sem("q_high"), sem("q_low")
        s_qw = [sem(f"q_written{g}") for g in range(GROUPS)]
        s_e0, s_e1, s_ew = sem("empty_zero"), sem("empty_ready"), sem("empty_written")
        s_bw, s_tg = sem("bias_written"), sem("tanh_ready")

        xc = sb("xc", [N, DIM], F32)
        xcT = sb("xcT", [128, 2, N], F32)
        wsq = sb("wsq", [128, 2, 2, gate_w.shape[2]], F32)
        empty = sb("empty", [128, v["EK"], v["ROWW"]], F32)

        p_rw, v_rw, i_rw, i_sq, a_sq = (sem(n) for n in ("pe_rw", "dve_rw", "router_in", "squares_in", "act_squares"))
        a_mean, a_var, v_xc, p_xc, a_xc, p_lg, v_lg = (sem(n) for n in (
            "act_mean2", "act_variance2", "dve_xc", "pe_xcT", "act_xcT", "pe_routed", "dve_routed"))
        each = lambda name: [sem(f"{name}{u}") for u in range(NB)]
        d_ctx, d_kw, d_ks, d_qs, d_m = each("ctx_in"), each("k_out"), each("ks_in"), each("qs_in"), each("m_in")
        p_T, p_K, p_V, p_S, p_mT = (sem(n) for n in ("pe_ctxT", "pe_k", "pe_v", "pe_scores", "pe_maxT"))
        p_ST, p_PV, p_OT, p_Wo = (sem(n) for n in ("pe_scoresT", "pe_pv", "pe_oT", "pe_wo"))
        a_T, a_K, a_V, a_V1, a_V2, a_E, a_O = (sem(n) for n in ("act_ctxT", "act_k", "act_v", "act_v1", "act_v2", "act_exp", "act_oT"))
        v_T, v_K, v_L, v_max, v_nm = (sem(n) for n in ("dve_ctxT", "dve_k", "dve_plow", "dve_max", "dve_negmax"))
        v_os, v_rd, v_on, v_O, v_x1 = (sem(n) for n in ("dve_osum", "dve_rden", "dve_on", "dve_oT", "dve_x1"))
        g_r, g_V, g_L = (sem(n) for n in ("pool_rest", "pool_v", "pool_plow"))

        SB = UN // 2
        POOL = [k for k in (1, 2, 3, 5, 6, 8) if k < SB]
        vec = lambda k: sum(j not in POOL for j in range(k + 1))
        pol = lambda k: sum(j in POOL for j in range(k + 1))
        last_bank = lambda p: (JT * p + JT - 1) // 2
        pv_at = {last_bank(p) + 3: p for p in range(PAIRS)}
        SLOTS = max(pv_at) + 1
        heads_at = {0: (0, 1), 1: (2, 3), 2: (4,), 3: (5, 6), 4: (7, 8), 5: (9, 10), 6: (11, 12), 7: (13, 14), 8: (15,)}
        KP = (1, 2)
        VP = (4, 5, 6)
        ST, AG, XC, XT, LG, RT = 5, 14, 7, 11, 12, 13
        V1, VR, V2, LV = 3, 3, 6, 6
        SQ = 4
        MT, OT, OP, CT = 8, 9, 12, 10

        def at(i, c):
            return NB * i + c, i + c // NB, c % NB

        FIRST = NB + 2
        COUNT = (B - 2 - FIRST) // NB
        assert v["PARTS"] == NB * COUNT

        def steps(eng, step):
            for n in range(FIRST):
                step(0, n)
            with eng.Fori(1, 1 + COUNT) as i:
                for c in range(2, NB + 2):
                    step(i, c)
            for n in range(FIRST + NB * COUNT, B + 4):
                step(0, n)

        def squared(i, c):
            assert E == 2 * COUNT + 2
            if not isinstance(i, int):
                return 2 * i + c - 3 if c < 4 else None
            return {FIRST - 1: 0, FIRST + NB * COUNT: E - 1}.get(NB * i + c)

        def live(i, c, back):
            return not isinstance(i, int) or 0 <= NB * i + c - back < B

        def starts(i, c):
            return isinstance(i, int) and NB * i + c == 0

        def wait(eng, s, value):
            if not isinstance(value, int) or value > 0:
                eng.wait_ge(s, value)

        constants = [(f32(cTH[:, :, M:MP]), 0.0), (f32(cTL[:, :, M:MP]), 0.0), (bias_sb[:, M:MP], 0.0),
                     (VS[:, :, :, :, VW - 1:VW].rearrange("p u t h o -> p (u t) h o"), 1.0)]
        for u in range(NB):
            constants += [(f32(QS[u][0:96]), 0.0), (f32(QS[u][96:128]), 1.0), (f32(KS[u][96:128]), 1.0)]
        CLEARED = len(constants)

        with nc.Block() as block:
            @block.sync
            def _(sp):
                def load_ctx(i, c):
                    b, h, u = at(i, c)
                    wait(sp, p_T, b - NB + 1)
                    sp.dma_start(ctx_sb[:, u, :, :], ctx_768[bass.ds(b, 1), :, :].rearrange("o (p t) d -> p (o t) d", t=JT)
                                 ).then_inc(d_ctx[u], 16)

                def queries(i, c):
                    b, h, u = at(i, c)
                    wait(sp, p_ST, SB * (b - NB + 1))
                    for s, part in enumerate((0, 1, 0)):
                        for e in range(2):
                            sp.dma_start(
                                f32(QS[u][32 * s + HD * e:32 * s + HD * e + HD, :, e, 0:N]),
                                q_scr[part, bass.ds(b, 1)].rearrange("o (q e r) i -> e r (o q) i", e=2, r=HD)[e]
                            ).then_inc(d_qs[u], 16)
                    sp.dma_start(f32(KS[u][RB:RB + 1, :, :]),
                                 bias_scr[bass.ds(b, 1), :].unsqueeze(1).to_broadcast([1, PAIRS, MP])
                                 ).then_inc(d_ks[u], 16)

                def keys(i, c):
                    b, h, u = at(i, c)
                    sp.wait_ge(v_K, b + 1)
                    for part, t in ((0, kH), (1, kL)):
                        sp.dma_start(k_scr[u, part].rearrange("(m p) j -> p m j", p=128), f32(t[:, u])
                                     ).then_inc(d_kw[u], 16)
                    sp.wait_ge(d_kw[u], 32 * (h + 1))
                    for s, part in enumerate((0, 0, 1)):
                        sp.dma_start(f32(KS[u][32 * s:32 * s + 32, :, :]),
                                     k_scr[u, part].rearrange("(q r) j -> r q j", r=32)).then_inc(d_ks[u], 16)

                def step(i, c):
                    e = squared(i, c)
                    if e is not None:
                        sp.wait_ge(s_e1, 1)
                        wait(sp, a_sq, e)
                        for j, w in enumerate((gate_w, up_w)):
                            sp.dma_start(wsq[:, j], w[bass.ds(e, 1)].rearrange("o (c p) f -> p (o c) f", p=128)
                                         ).then_inc(i_sq, 16)
                    if isinstance(i, int) and NB * i + c == NB:
                        for g in range(GROUPS):
                            sp.wait_ge(s_qw[g], 64)
                    if live(i, c, -2) and not starts(i, c):
                        load_ctx(i, c + 2)
                    if not isinstance(i, int):
                        sp.wait_ge(s_e1, 1)
                        sp.dma_start(v["xs_scr"].rearrange("(t p) w -> p t w", p=128)[
                            :, bass.ds(v["EK"] * (NB * i + c - FIRST), v["EK"]), :], empty[:]).then_inc(s_ew, 16)
                    if live(i, c, 0):
                        if not starts(i, c):
                            queries(i, c)
                            keys(i, c)
                    if live(i, c, 1):
                        b, h, u = at(i, c - 1)
                        sp.wait_ge(v_nm, b + 1)
                        sp.dma_start(f32(QS[u][RM:RM + 1, :, :, 0:N]).rearrange("o q e i -> o (q e) i"),
                                     f32(nm[:])).then_inc(d_m[u], 16)

                for k in ("k", "v"):
                    w, p = shapes[k]
                    sp.dma_start(Wf[k][:], w.rearrange("(c p) n -> p c n", p=p)).then_inc(s_w[k], 16)
                load_ctx(0, 0)
                sp.dma_start(X[:], x.rearrange("b i d -> i b d")).then_inc(s_x, 16)
                for k in ("q", "o"):
                    w, p = shapes[k]
                    sp.dma_start(Wf[k][:], w.rearrange("(c p) n -> p c n", p=p)).then_inc(s_w[k], 16)
                sp.dma_start(mask_sb[:], mask).then_inc(s_m, 16)
                for j, g in enumerate((v["g_xattn"], v["g_ffn"])):
                    sp.dma_start(gates[:, j:j + 1], g.rearrange("(o a) -> o a", o=1).to_broadcast([128, 1])
                                 ).then_inc(s_g, 16)
                sp.dma_start(rw[:], router_w).then_inc(i_rw, 16)
                load_ctx(0, 1)
                load_ctx(0, 2)
                sp.wait_ge(s_bias, 1)
                sp.wait_ge(s_clear, 3)
                sp.dma_start(bias_scr, bias_sb[:]).then_inc(s_bw, 16)
                sp.wait_ge(s_clear, CLEARED)
                keys(0, 0)
                for g in range(GROUPS):
                    sp.wait_ge(s_ql, g + 1)
                    for part, t in ((0, qH), (1, qL)):
                        for c in range(2):
                            sp.dma_start(
                                q_scr[part, g * GB:(g + 1) * GB, c * 128:(c + 1) * 128, :].rearrange("b p i -> p b i"),
                                f32(t[:, g, c, :]).rearrange("p (b i) -> p b i", b=GB)).then_inc(s_qw[g], 16)
                    if g == 0:
                        sp.wait_ge(s_bw, 16)
                        sp.wait_ge(s_qw[0], 64)
                        queries(0, 0)
                steps(sp, step)

            @block.gpsimd
            def _(pool):
                def low(i, c, k):
                    b, h, u = at(i, c - 2)
                    pool.wait_ge(a_E, SB * b + k + 1)
                    pool.tensor_tensor(PL[:, 2 * k:2 * k + 2, :, 0:N], PT[:, 2 * k:2 * k + 2, :, 0:N],
                                       PH[:, 2 * k:2 * k + 2, :, 0:N], ALU.subtract).then_inc(g_L, 1)

                def values(i, c):
                    b, h, u = at(i, c - 1)
                    part = lambda k: VS[:, u, :, :, HD * k:HD * (k + 1)]
                    head = lambda t: t[:].rearrange("p t (h d) -> p t h d", d=HD)
                    pool.wait_ge(a_V1, b + 1)
                    wait(pool, g_V, b)
                    pool.tensor_tensor(head(vr), vf[:, u].rearrange("p t (h d) -> p t h d", d=HD), part(0), ALU.subtract).then_inc(g_r, 1)

                def last_values(i, c):
                    b, h, u = at(i, c - 1)
                    part = lambda k: VS[:, u, :, :, HD * k:HD * (k + 1)]
                    head = lambda t: t[:].rearrange("p t (h d) -> p t h d", d=HD)
                    pool.wait_ge(a_V2, b + 1)
                    pool.tensor_tensor(part(2), head(vr), part(1), ALU.subtract).then_inc(g_V, 1)

                pool.memset(ident[:], 0.0).then_inc(s_id0, 1)
                pool.wait_ge(s_id0, 1)
                pool.affine_select(out=ident[:], in_=ident[:], compare_op=ALU.not_equal, fill=1.0, base=0,
                                   pattern=[[-1, 128]], channel_multiplier=1).then_inc(s_id, 1)
                pool.wait_ge(s_id, 1)
                for n, (part, value) in enumerate(constants):
                    pool.memset(part, value).then_inc(s_clear, 1)
                    pool.wait_ge(s_clear, n + 1)
                for g in range(GROUPS):
                    pool.wait_ge(s_qw[g], 64)
                pool.wait_ge(s_qp, GROUPS)
                pool.wait_ge(s_bw, 16)
                for n, part in enumerate((PT[:, :, :, N:NI], PL[:, :, :, N:NI])):
                    pool.memset(part, 0.0).then_inc(s_clear, 1)
                    pool.wait_ge(s_clear, CLEARED + n + 1)
                pool.memset(empty[:], 0.0).then_inc(s_e0, 1)
                pool.wait_ge(s_e0, 1)
                pool.iota(empty[:, :, DIM:DIM + 1].rearrange("p k o -> p (k o)").bitcast(mybir.dt.int32),
                          pattern=[[128, v["EK"]]], base=2 * B * N, channel_multiplier=1).then_inc(s_e1, 1)

                def step(i, c):
                    for k in range(SLOTS):
                        if k in POOL and live(i, c, 2):
                            low(i, c, k)
                        if k == VR and live(i, c, 1):
                            values(i, c)
                        if k == LV and live(i, c, 1):
                            last_values(i, c)

                steps(pool, step)
                pool.wait_ge(s_ew, 16 * v["PARTS"])

            @block.scalar
            def _(act):
                def transposed(i, c):
                        b, h, u = at(i, c)
                        act.wait_ge(p_T, b + 1)
                        wait(act, p_V, JT * b)
                        act.activation(cTH[:, :, 0:M], misc[0:CK].rearrange("p (c n) -> p c n", c=2)[:, :, 0:M],
                                       ACT.Copy).then_inc(a_T, 1)

                def step(i, c):
                    if starts(i, c):
                        return
                    slots(i, c)

                def row_means(i, c):
                    b, h, u = at(i, c - 4)
                    act.wait_ge(v_x1, b + 1)
                    wait(act, a_var, b)
                    act.activation(xc[:], X[:, bass.ds(b, 1), :].rearrange("i o d -> i (o d)"), ACT.Copy,
                                   scale=1.0 / DIM, accum_out=mv2[:, bass.ds(b, 1), 0:1].rearrange("i o d -> i (o d)")
                                   ).then_inc(a_mean, 1)

                def variances(i, c):
                    b, h, u = at(i, c - 4)
                    act.wait_ge(p_xc, b + 1)
                    act.activation(xc[:], xc[:], ACT.Square, scale=DIM ** -0.5,
                                   accum_out=mv2[:, bass.ds(b, 1), 1:2].rearrange("i o d -> i (o d)")
                                   ).then_inc(a_var, 1)

                def slots(i, c):
                    for k in range(SLOTS):
                        if k == ST and live(i, c, 4):
                            row_means(i, c)
                        if k == XT + 1 and live(i, c, 4):
                            b, h, u = at(i, c - 4)
                            act.wait_ge(p_xc, b + 1)
                            wait(act, p_lg, b)
                            act.activation(xcT[:], psS[1][:, 0:2 * N].rearrange("p (c i) -> p c i", c=2), ACT.Copy
                                           ).then_inc(a_xc, 1)
                        if k == AG and live(i, c, 4):
                            variances(i, c)
                        if k == V2 and live(i, c, 1):
                            b, h, u = at(i, c - 1)
                            act.wait_ge(g_r, b + 1)
                            act.activation(VS[:, u, :, :, HD:2 * HD].rearrange("p t h d -> p (t h) d"),
                                           vr[:].rearrange("p t (h d) -> p (t h) d", d=HD), ACT.Copy).then_inc(a_V2, 1)
                        if k == SQ and squared(i, c) is not None:
                            e = squared(i, c)
                            act.wait_ge(i_sq, 32 * (e + 1))
                            act.activation(wsq[:].rearrange("p j c f -> p (j c f)"),
                                           wsq[:].rearrange("p j c f -> p (j c f)"), ACT.Square,
                                           accum_out=sq[:, bass.ds(e, 1)]).then_inc(a_sq, 1)
                        if k == OT + 1 and live(i, c, 3):
                            b, h, u = at(i, c - 3)
                            act.wait_ge(p_OT, b + 1)
                            wait(act, p_Wo, b)
                            act.activation(oTH[:], psS[0][:, 0:2 * N].rearrange("p (c i) -> p c i", c=2),
                                           ACT.Copy).then_inc(a_O, 1)
                        if k == CT + 1 and live(i, c, -1) and not starts(i, c):
                            transposed(i, c + 1)
                        if k < SB and live(i, c, 2):
                            b, h, u = at(i, c - 2)
                            if isinstance(b, int) and b == 0 and k == 0:
                                act.wait_ge(s_clear, CLEARED + 2)
                            act.wait_ge(p_ST, SB * b + k + 1)
                            wait(act, p_PV, PAIRS * (b - 1) + (2 * k + 1) // JT + 1)
                            act.activation(PT[:, 2 * k:2 * k + 2, :, 0:N].rearrange("p a e i -> p (a e) i"),
                                           psST[k % 2][0:JP].rearrange("p (a i) -> p a i", i=NI)[:, :, 0:N],
                                           ACT.Exp).then_inc(a_E, 1)
                        if k == V1 and live(i, c, 1):
                            b, h, u = at(i, c - 1)
                            act.wait_ge(a_V, b + 1)
                            wait(act, p_PV, PAIRS * (b - NB + 1))
                            act.activation(VS[:, u, :, :, 0:HD].rearrange("p t h d -> p (t h) d"),
                                           vf[:, u].rearrange("p t (h d) -> p (t h) d", d=HD), ACT.Copy).then_inc(a_V1, 1)
                        if k == KP[-1] and live(i, c, 0):
                            b, h, u = at(i, c)
                            act.wait_ge(p_K, 2 * b + 2)
                            wait(act, d_kw[u], 32 * h)
                            act.activation(kH[:, u], misc[:].rearrange("p (m n) -> p m n", m=2)[:, :, 0:MP],
                                           ACT.Copy).then_inc(a_K, 1)
                        if k == VP[-1] + 1 and live(i, c, 0):
                            b, h, u = at(i, c)
                            act.wait_ge(p_V, JT * b + JT)
                            wait(act, g_r, b - NB + 1)
                            act.activation(vf[:, u].rearrange("p t n -> p (t n)"), misc[0:JP, 0:JT * DIM], ACT.Copy
                                           ).then_inc(a_V, 1)

                def w_high(k):
                    act.wait_ge(s_w[k], 16)
                    act.activation(WH[k][:], Wf[k][:], ACT.Copy, scale=SCALE if k == "q" else 1.0).then_inc(s_wh, 1)

                w_high("k")
                w_high("v")
                transposed(0, 0)
                act.wait_ge(s_g, 32)
                act.activation(tg[:], gates[:], ACT.Tanh).then_inc(s_tg, 1)
                w_high("q")
                w_high("o")
                act.wait_ge(s_ve, 1)
                act.activation(rstd[:], veps[:], ACT.Sqrt).then_inc(s_sq, 1)
                slots(0, 0)

                def q_high(g):
                    act.wait_ge(s_qp, g + 1)
                    for c in range(2):
                        act.activation(qH[:, g, c, :], (psS, psST)[g % 2][c][:, 0:GB * N], ACT.Copy
                                       ).then_inc(s_qh, 1)

                for g in range(GROUPS):
                    act.wait_ge(s_xt, g + 1)
                    if g >= 2:
                        act.wait_ge(s_qp, g - 1)
                    for c in range(2):
                        act.activation(xTH[:, g % 2, c, :], psO[c][:, 0:GB * N], ACT.Copy).then_inc(s_xh, 1)
                    if g >= 1:
                        q_high(g - 1)
                    if g == 1:
                        transposed(0, 1)
                q_high(GROUPS - 1)
                steps(act, step)

            @block.tensor
            def _(pe):
                def ctx_T(i, c):
                    b, h, u = at(i, c)
                    pe.wait_ge(d_ctx[u], 16 * (h + 1))
                    wait(pe, a_V, b)
                    for k in range(2):
                        for t in range(JT):
                            mm = pe.transpose(misc[0:CK, 512 * k + JP * t:512 * k + JP * (t + 1)],
                                              ctx_sb[:, u, t, CK * k:CK * (k + 1)], ident[0:JP, 0:JP])
                    mm.then_inc(p_T, 1)

                def project_k(i, c, m):
                    b, h, u = at(i, c)
                    if m == 0:
                        pe.wait_ge(v_T, b + 1)
                    for n, (w, r) in enumerate(((WH, cTH), (WL, cTH), (WH, cTL))):
                        for k in range(2):
                            mm = pe.matmul(misc[:, 512 * m:512 * m + MP], w["k"][:, k, m * 128:(m + 1) * 128],
                                           r[:, k, :], start=(n == 0 and k == 0), stop=(n == 2 and k == 1))
                    mm.then_inc(p_K, 1)

                def project_v(i, c, t):
                    b, h, u = at(i, c)
                    if t == 0:
                        pe.wait_ge(v_K, b + 1)
                    for n, (w, r) in enumerate(((WH, cTH), (WL, cTH), (WH, cTL))):
                        for k in range(2):
                            mm = pe.matmul(misc[0:JP, DIM * t:DIM * (t + 1)], r[:, k, JP * t:JP * (t + 1)],
                                           w["v"][:, k, :], start=(n == 0 and k == 0), stop=(n == 2 and k == 1))
                    mm.then_inc(p_V, 1)

                def scores(i, c, hd):
                    b, h, u = at(i, c - 1)
                    if hd == 0:
                        pe.wait_ge(d_ks[u], 64 * (h + 1))
                        pe.wait_ge(d_qs[u], 96 * (h + 1))
                        wait(pe, v_x1, b - 2)
                    if hd == 1:
                        wait(pe, v_nm, b)
                        wait(pe, v_lg, b - 3)
                    wait(pe, v_max, HEADS * b + hd - 1)
                    pe.matmul(psS[hd % 2][0:N, 0:MP], QS[u][0:RM, hd // 2, hd % 2, 0:N], KS[u][0:RM, hd // 2, :],
                              start=True, stop=True).then_inc(p_S, 1)

                def max_T(i, c):
                    b, h, u = at(i, c - 1)
                    pe.wait_ge(v_max, HEADS * (b + 1))
                    pe.transpose(psS[1][0:HEADS, 0:N], mx[:], ident[0:N, 0:N]).then_inc(p_mT, 1)

                def scores_T(i, c, k):
                    b, h, u = at(i, c - 2)
                    if k == 0:
                        pe.wait_ge(d_m[u], 16 * (h + 1))
                    wait(pe, a_E, SB * b + k - 1)
                    for a in range(2):
                        p, t = divmod(2 * k + a, JT)
                        mm = pe.matmul(psST[k % 2][0:JP, 2 * NI * a:2 * NI * (a + 1)],
                                       KS[u][0:RM + 1, p, JP * t:JP * (t + 1)],
                                       QS[u][0:RM + 1, p, :, :].rearrange("r e i -> r (e i)"), start=True, stop=True)
                    mm.then_inc(p_ST, 1)

                def sums(i, c, p):
                    b, h, u = at(i, c - 2)
                    if p == 0:
                        pe.wait_ge(g_V, b + 1)
                    if p % 4 == 0:
                        wait(pe, v_os, 2 * (b - 1) + p // 4 + 1)
                    k = last_bank(p)
                    pe.wait_ge(v_L, vec(SB - 1) * b + vec(k))
                    pe.wait_ge(g_L, pol(SB - 1) * b + pol(k))
                    for e in range(2):
                        hd = 2 * p + e
                        for part, P in enumerate((PH, PL)):
                            for t in range(JT):
                                mm = pe.matmul(psO[hd // 8][:, VW * (hd % 8):VW * (hd % 8 + 1)], P[:, JT * p + t, e, :],
                                               VS[:, u, t, hd, :], start=(part == 0 and t == 0),
                                               stop=(part == 1 and t == JT - 1))
                    mm.then_inc(p_PV, 1)

                def out_T(i, c):
                    b, h, u = at(i, c - 3)
                    pe.wait_ge(v_on, 2 * b + 2)
                    pe.wait_ge(v_max, HEADS * min(b + 2, B) if isinstance(b, int) else HEADS * (b + 2))
                    for k in range(2):
                        mm = pe.transpose(psS[0][:, N * k:N * (k + 1)],
                                          on[:, 8 * k:8 * k + 8, :].rearrange("i h d -> i (h d)"), ident[0:N, 0:N])
                    mm.then_inc(p_OT, 1)

                def center_T(i, c):
                    b, h, u = at(i, c - 4)
                    pe.wait_ge(v_xc, b + 1)
                    wait(pe, v_lg, b)
                    if live(i, c, 1):
                        pe.wait_ge(v_nm, b + 4)
                    for k in range(2):
                        mm = pe.transpose(psS[1][:, N * k:N * (k + 1)], xc[:, 128 * k:128 * (k + 1)], ident[0:N, 0:N])
                    mm.then_inc(p_xc, 1)

                def route(i, c):
                    b, h, u = at(i, c - 4)
                    pe.wait_ge(a_xc, b + 1)
                    for k in range(2):
                        mm = pe.matmul(psS[1][0:N, 2 * N:2 * N + E], xcT[:, k, :], rwT[:, k, :],
                                       start=(k == 0), stop=(k == 1))
                    mm.then_inc(p_lg, 1)

                def project_o(i, c):
                    b, h, u = at(i, c - 3)
                    pe.wait_ge(v_O, b + 1)
                    for n, (w, r) in enumerate(((WH, oTH), (WL, oTH), (WH, oTL))):
                        for k in range(2):
                            mm = pe.matmul(psS[0][0:N, 0:DIM], r[:, k, :], w["o"][:, k, :],
                                           start=(n == 0 and k == 0), stop=(n == 2 and k == 1))
                    mm.then_inc(p_Wo, 1)

                def step(i, c):
                    if starts(i, c):
                        return
                    slots(i, c)

                def slots(i, c):
                    for s in range(SLOTS):
                        heads = heads_at.get(s, ()) if live(i, c, 1) else ()
                        if s < SB and live(i, c, 2):
                            scores_T(i, c, s)
                        if s in KP and live(i, c, 0):
                            project_k(i, c, KP.index(s))
                        for hd in heads[0:1]:
                            scores(i, c, hd)
                        if s in pv_at and live(i, c, 2):
                            sums(i, c, pv_at[s])
                        if s in VP and live(i, c, 0):
                            project_v(i, c, VP.index(s))
                        for hd in heads[1:2]:
                            scores(i, c, hd)
                        if s == MT and live(i, c, 1):
                            max_T(i, c)
                        if s == OT and live(i, c, 3):
                            out_T(i, c)
                        if s == OP and live(i, c, 3):
                            project_o(i, c)
                        if s == CT and live(i, c, -1) and not starts(i, c):
                            ctx_T(i, c + 1)
                        if s == XT and live(i, c, 4):
                            center_T(i, c)
                        if s == LG and live(i, c, 4):
                            route(i, c)

                pe.wait_ge(s_id, 1)
                ctx_T(0, 0)
                pe.wait_ge(s_wl, 2)
                pe.wait_ge(s_clear, 2)
                slots(0, 0)

                def turn(g):
                    pe.wait_ge(s_xn, g + 1)
                    if g >= 1:
                        pe.wait_ge(s_xl, g)
                    for c in range(2):
                        for b in range(GB):
                            mm = pe.transpose(psO[c][:, b * N:(b + 1) * N], xn[:, g % 2, b, c * 128:(c + 1) * 128],
                                              ident[0:N, 0:N])
                    mm.then_inc(s_xt, 1)

                pe.wait_ge(i_rw, 16)
                for k in range(2):
                    mm = pe.transpose(psST[0][:, E * k:E * (k + 1)], rw[:, 128 * k:128 * (k + 1)], ident[0:E, 0:E])
                mm.then_inc(p_rw, 1)
                pe.wait_ge(s_wl, 3)
                turn(0)
                pe.wait_ge(v_rw, 1)
                for g in range(GROUPS):
                    if g + 1 < GROUPS:
                        turn(g + 1)
                    pe.wait_ge(s_xl, g + 1)
                    if g >= 2:
                        pe.wait_ge(s_ql, g - 1)
                    for m in range(2):
                        for n, (w, r) in enumerate(((WH, xTH), (WL, xTH), (WH, xTL))):
                            for c in range(2):
                                mm = pe.matmul((psS, psST)[g % 2][m][:, 0:GB * N],
                                               w["q"][:, c, m * 128:(m + 1) * 128], r[:, g % 2, c, :],
                                               start=(n == 0 and c == 0), stop=(n == 2 and c == 1))
                    mm.then_inc(s_qp, 1)
                    if g == 1:
                        ctx_T(0, 1)
                pe.wait_ge(s_ql, GROUPS)
                pe.wait_ge(s_wl, 4)
                steps(pe, step)

            @block.vector
            def _(dve):
                def low(i, c, k):
                    b, h, u = at(i, c - 2)
                    dve.wait_ge(a_E, SB * b + k + 1)
                    dve.tensor_tensor(PL[:, 2 * k:2 * k + 2, :, 0:N].rearrange("p a e i -> p (a e) i"),
                                      PT[:, 2 * k:2 * k + 2, :, 0:N].rearrange("p a e i -> p (a e) i"),
                                      PH[:, 2 * k:2 * k + 2, :, 0:N].rearrange("p a e i -> p (a e) i"),
                                      ALU.subtract).then_inc(v_L, 1)

                def maximum(i, c, hd):
                    b, h, u = at(i, c - 1)
                    dve.wait_ge(p_S, HEADS * b + hd + 1)
                    if hd == 0:
                        wait(dve, p_mT, b)
                    dve.tensor_reduce(mx[:, hd:hd + 1], psS[hd % 2][0:N, 0:M], AX.X, ALU.max).then_inc(v_max, 1)

                def normalise(i, c, half):
                    b, h, u = at(i, c - 2)
                    dve.wait_ge(p_PV, PAIRS * b + 4 * half + 4)
                    hs = slice(8 * half, 8 * half + 8)
                    o = psO[half][0:N, 0:8 * VW].rearrange("i (h w) -> i h w", w=VW)
                    dve.reciprocal(rden[:, hs], o[:, :, VW - 1]).then_inc(v_rd, 1)
                    dve.tensor_reduce(osum[:, hs, :], o[:, :, 0:3 * HD].rearrange("i h (k d) -> i h d k", k=3),
                                      AX.X, ALU.add).then_inc(v_os, 1)
                    dve.wait_ge(v_rd, 2 * b + half + 1)
                    dve.wait_ge(v_os, 2 * b + half + 1)
                    wait(dve, p_OT, b)
                    dve.tensor_tensor(on[:, hs, :], osum[:, hs, :],
                                      rden[:, hs].unsqueeze(2).to_broadcast([N, 8, HD]),
                                      ALU.mult).then_inc(v_on, 1)

                def transposed(i, c):
                    b, h, u = at(i, c)
                    dve.wait_ge(a_T, b + 1)
                    dve.tensor_tensor(cTL[:, :, 0:M], misc[0:CK].rearrange("p (c n) -> p c n", c=2)[:, :, 0:M],
                                      f32(cTH[:, :, 0:M]), ALU.subtract).then_inc(v_T, 1)

                def step(i, c):
                    if starts(i, c):
                        return
                    slots(i, c)

                def center(i, c):
                    b, h, u = at(i, c - 4)
                    dve.wait_ge(a_mean, b + 1)
                    dve.tensor_scalar(xc[:], X[:, bass.ds(b, 1), :].rearrange("i o d -> i (o d)"),
                                      mv2[:, bass.ds(b, 1), 0:1].rearrange("i o d -> i (o d)"), None,
                                      ALU.subtract).then_inc(v_xc, 1)

                def slots(i, c):
                    for s in range(SLOTS):
                        if s == XC and live(i, c, 4):
                            center(i, c)
                        if s == OT + 1 and live(i, c, 3):
                            b, h, u = at(i, c - 3)
                            dve.wait_ge(a_O, b + 1)
                            dve.tensor_tensor(oTL[:], psS[0][:, 0:2 * N].rearrange("p (c i) -> p c i", c=2),
                                              f32(oTH[:]), ALU.subtract).then_inc(v_O, 1)
                        heads = heads_at.get(s, ()) if live(i, c, 1) else ()
                        for hd in heads[0:1]:
                            maximum(i, c, hd)
                        if 0 < s <= SB and s - 1 not in POOL and live(i, c, 2):
                            low(i, c, s - 1)
                        if s == KP[-1] + 1 and live(i, c, 0):
                            b, h, u = at(i, c)
                            dve.wait_ge(a_K, b + 1)
                            dve.tensor_tensor(kL[:, u], misc[:].rearrange("p (m n) -> p m n", m=2)[:, :, 0:MP],
                                              f32(kH[:, u]), ALU.subtract).then_inc(v_K, 1)
                        for hd in heads[1:2]:
                            maximum(i, c, hd)
                        if s == MT and live(i, c, 1):
                            b, h, u = at(i, c - 1)
                            dve.wait_ge(p_mT, b + 1)
                            if not isinstance(i, int) or b > 0:
                                b1, h1, u1 = at(i, c - 2)
                                dve.wait_ge(d_m[u1], 16 * (h1 + 1))
                            dve.tensor_scalar(nm[:], psS[1][0:HEADS, 0:N], -1.0, None, ALU.mult
                                              ).then_inc(v_nm, 1)
                        if s == OP + 1 and live(i, c, 3):
                            b, h, u = at(i, c - 3)
                            dve.wait_ge(p_Wo, b + 1)
                            dve.scalar_tensor_tensor(out=X[:, bass.ds(b, 1), :], in0=psS[0][0:N, 0:DIM].unsqueeze(1),
                                                     scalar=tg[0:N, 0:1],
                                                     in1=X[:, bass.ds(b, 1), :], op0=ALU.mult, op1=ALU.add
                                                     ).then_inc(v_x1, 1)
                        if s == pv_slot(3) + 1 and live(i, c, 2):
                            normalise(i, c, 0)
                        if s == CT + 1 and live(i, c, -1) and not starts(i, c):
                            transposed(i, c + 1)
                        if s == RT and live(i, c, 4):
                            b, h, u = at(i, c - 4)
                            dve.wait_ge(p_lg, b + 1)
                            dve.tensor_copy(routed[:, bass.ds(b, 1), :].rearrange("i o e -> i (o e)"),
                                            psS[1][0:N, 2 * N:2 * N + E]).then_inc(v_lg, 1)
                    if live(i, c, 2):
                        normalise(i, c, 1)

                pv_slot = lambda p: last_bank(p) + 3
                def w_low(k, n):
                    dve.wait_ge(s_wh, n)
                    dve.scalar_tensor_tensor(out=WL[k][:], in0=Wf[k][:], scalar=SCALE if k == "q" else 1.0,
                                             in1=f32(WH[k][:]), op0=ALU.mult, op1=ALU.subtract).then_inc(s_wl, 1)

                w_low("k", 1)
                w_low("v", 2)
                transposed(0, 0)
                dve.wait_ge(s_x, 16)
                layer_norm_stats(dve, X, stats, mv, veps, rstd, B, s_st, s_mv, s_ve, s_sq, s_rs)
                dve.wait_ge(s_m, 16)
                dve.tensor_scalar(bias_sb[:, 0:M].rearrange("b (t p) -> b t p", t=JT),
                                  mask_sb[:].rearrange("b (p t) -> b t p", t=JT),
                                  -1.0, HIDDEN, ALU.add, ALU.mult).then_inc(s_bias, 1)
                slots(0, 0)
                w_low("q", 3)
                w_low("o", 4)

                def normal(g):
                    if g >= 2:
                        dve.wait_ge(s_xt, g - 1)
                    for b in range(GB):
                        nb = g * GB + b
                        ins = dve.tensor_scalar(xn[:, g % 2, b, :], X[:, nb, :], mv[:, nb, 0:1], rstd[:, nb:nb + 1],
                                                ALU.subtract, ALU.mult)
                    ins.then_inc(s_xn, 1)

                def q_low(g):
                    dve.wait_ge(s_qh, 2 * g + 2)
                    for c in range(2):
                        ins = dve.tensor_tensor(qL[:, g, c, :], (psS, psST)[g % 2][c][:, 0:GB * N],
                                                f32(qH[:, g, c, :]), ALU.subtract)
                    ins.then_inc(s_ql, 1)

                normal(0)
                dve.wait_ge(p_rw, 1)
                dve.tensor_copy(rwT[:], psST[0][:, 0:2 * E].rearrange("p (c e) -> p c e", c=2)).then_inc(v_rw, 1)
                for g in range(GROUPS):
                    if g + 1 < GROUPS:
                        normal(g + 1)
                    dve.wait_ge(s_xh, 2 * g + 2)
                    if g >= 2:
                        dve.wait_ge(s_qp, g - 1)
                    for c in range(2):
                        ins = dve.tensor_tensor(xTL[:, g % 2, c, :], psO[c][:, 0:GB * N], f32(xTH[:, g % 2, c, :]),
                                                ALU.subtract)
                    ins.then_inc(s_xl, 1)
                    if g >= 1:
                        q_low(g - 1)
                    if g == 1:
                        transposed(0, 1)
                q_low(GROUPS - 1)
                steps(dve, step)


def experts(nc, v):
    (B, N, DIM, X, ident, tg, banks, misc, out) = (v[k] for k in "B N DIM X ident tg banks misc out".split())
    router_w, gate_w, gate_b, up_w, up_b, down_w, down_b = (
        v[k] for k in "router_w gate_w gate_b up_w up_b down_w down_b".split())
    mv2, routed, sq = v["mv2"], v["routed"], v["sq"]
    xs_scr, y_scr, NT, TS, ROWW = v["xs_scr"], v["y_scr"], v["NT"], v["TS"], v["ROWW"]
    E, FF = gate_w.shape[0], gate_w.shape[2]
    FC, DC = FF // 128, DIM // 128
    I32 = mybir.dt.int32
    XS = 2.0 ** 10
    WS = 2.0 ** 14

    with ExitStack() as stack:
        def sb(name, shape, dt):
            return stack.enter_context(nc.sbuf_tensor(name, shape, dt))

        def sem(name):
            return stack.enter_context(nc.semaphore(name))

        GH = sb("GH", [128, E, 2, DC, FF], F16)
        GL = sb("GL", [128, E, 2, DC, FF], F16)
        DH = sb("DH", [128, E, FC, DIM], F32R)
        DL = sb("DL", [128, E, FC, DIM], F32R)
        inv = sb("inv", [128, E], F32)
        gb = sb("gb", [128, E * FC], F32)
        ub = sb("ub", [128, E * FC], F32)
        tw = sb("tw", [N, 2, B], F32)
        tile_e = sb("tile_e", [1, NT], I32)
        TH = TS // 128
        xt = sb("xt", [128, 2, TH, ROWW], F32)
        l_x = [sem(f"tile_in{u}") for u in range(2)]

        with ExitStack() as inner:
            def tmp(name, shape, dt):
                return inner.enter_context(nc.sbuf_tensor(name, shape, dt))

            def isem(name):
                return inner.enter_context(nc.semaphore(name))

            WB = 3
            xn = tmp("xn2", [N, B, ROWW], F32)
            rstd, veps = tmp("rstd2", [N, B], F32), tmp("veps2", [N, B], F32)
            braw = tmp("braw", [E * FC, 2, 128], F32)
            raw = tmp("w_raw", [128, WB, 2, DC, FF], F32)
            draw = tmp("d_raw", [128, 2, FC, DIM], F32)
            half, unit, sc = tmp("half", [128, E], F32), tmp("unit", [128, E], F32), tmp("sc", [128, E], F32)
            upper, ones = tmp("upper", [N, N], F32), tmp("ones2", [128, 128], F32)
            R = {n: tmp("r_" + n, [N, B, E], F32) for n in
                 "logit low exp eq score sel1 rest sel2".split()}
            R.update(a0=R["eq"], a1=R["score"], pos=R["rest"], pick1=R["low"], pick2=R["logit"], both=R["exp"])
            r = {n: tmp("s_" + n, [N, B], F32) for n in
                 "m sum m1 t1 m2 t2 p1 p2 den rden rsum w1 w2 f1 f2".split()}
            pos = [tmp(f"pos{k}", [N, B], I32) for k in range(2)]
            c = {n: tmp("c_" + n, [N, E], F32) for n in "cnt pad e0 e1 base".split()}
            ci, ca = tmp("c_int", [N, E], I32), tmp("c_and", [N, E], I32)
            tie_i, start_i = tmp("tie_i", [N, B, E], I32), tmp("start_i", [1, NT, E], I32)
            R["tie"], start = tie_i[:].bitcast(F32), start_i[:].bitcast(F32)
            past, nexp = tmp("past", [1, NT, E], F32), tmp("nexp", [1, NT], F32)

            i_sm, i_w = isem("small_in"), [isem(f"w_in{u}") for u in range(WB)]
            i_d = [isem(f"d_in{u}") for u in range(2)]
            q_c, q_tri, q_iota, q_id = (isem(n) for n in ("pool_clear", "tri", "iota", "ids"))
            q_sc = [[isem(f"rows_out{k}{p}") for p in range(2)] for k in range(2)]
            q_l, q_dl, s_p = isem("pool_wlow"), isem("pool_dlow"), isem("act_scaled")
            t_rw, t_rank, t_n = (isem(n) for n in ("pe_biasT", "pe_rank", "pe_norm"))
            s_exp, s_h, s_d, s_sq = (isem(n) for n in ("act_exp2", "act_high", "act_down_high", "act_sqrt2"))
            e_rw, e_ve, e_rs, e_xn = (isem(n) for n in ("dve_biasT", "dve_ve2", "dve_rs2", "dve_xn2"))
            e_r, e_low, e_sel, e_pos, e_sc, e_l, e_dl = (isem(n) for n in (
                "dve_chain", "dve_low", "dve_sel", "dve_pos", "dve_scale", "dve_wlow", "dve_dlow"))
            e_ch = isem("dve_scale_chain")
            bN, bR, bC = banks[2], banks[3], banks[4]

            with nc.Block() as block:
                @block.sync
                def _(sp):
                    def split(e, first, rest):
                        sp.wait_ge(*((first, 1) if e == 0 else (rest, e)))

                    def load(e):
                        if e >= WB:
                            split(e - WB, q_l, e_l)
                        for j, w in enumerate((gate_w, up_w)):
                            sp.dma_start(raw[:, e % WB, j], w[e].rearrange("(c p) f -> p c f", p=128)
                                         ).then_inc(i_w[e % WB], 16)

                    def load_down(e):
                        if e >= 2:
                            split(e - 2, q_dl, e_dl)
                        sp.dma_start(draw[:, e % 2], down_w[e].rearrange("(f p) d -> p f d", p=128)
                                     ).then_inc(i_d[e % 2], 16)

                    load(0)
                    load_down(0)
                    for j, t in enumerate((gate_b, up_b)):
                        sp.dma_start(braw[:, j, :], t.rearrange("e (f p) -> (e f) p", p=128)).then_inc(i_sm, 16)
                    load(1)
                    load_down(1)
                    load(2)
                    for e in range(2, E):
                        if e + 1 < E:
                            load(e + 1)
                        load_down(e)
                    for k in range(2):
                        for p in range(2):
                            sp.wait_ge(q_sc[k][p], 8 * B)
                    for t in range(2):
                        sp.dma_start(xt[:, t], xs_scr[TS * t:TS * (t + 1), :].rearrange("(h p) w -> p h w", p=128)
                                     ).then_inc(l_x[t], 16)

                @block.gpsimd
                def _(pool):
                    pool.memset(upper[:], 0.0).then_inc(q_c, 1)
                    pool.wait_ge(q_c, 1)
                    pool.affine_select(out=upper[:], in_=upper[:], compare_op=ALU.is_ge, fill=1.0, base=0,
                                       pattern=[[-1, N]], channel_multiplier=1).then_inc(q_tri, 1)
                    pool.wait_ge(q_tri, 1)
                    pool.memset(ones[:], 1.0).then_inc(q_tri, 1)
                    pool.wait_ge(q_tri, 2)
                    pool.iota(tie_i[:], pattern=[[0, B], [-1, E]], base=E, channel_multiplier=0).then_inc(q_iota, 1)
                    pool.wait_ge(q_iota, 1)
                    pool.iota(start_i[:], pattern=[[TS, NT], [0, E]], base=0, channel_multiplier=0
                              ).then_inc(q_iota, 1)
                    pool.wait_ge(q_iota, 2)
                    flat = lambda t, e: t[:, e].rearrange("p f d -> p (f d)")
                    wide = lambda t, e: t[:, e].rearrange("p j c f -> p (j c f)")
                    pool.wait_ge(s_h, 1)
                    pool.tensor_tensor(wide(GL, 0), wide(raw, 0), wide(GH, 0), ALU.subtract).then_inc(q_l, 1)
                    pool.wait_ge(s_d, 1)
                    pool.tensor_tensor(flat(DL, 0), flat(draw, 0), f32(flat(DH, 0)), ALU.subtract).then_inc(q_dl, 1)
                    for k in range(2):
                        for p in range(2):
                            half_b = slice(B // 2 * p, B // 2 * (p + 1))
                            if k:
                                pool.wait_ge(q_sc[0][p], 8 * B)
                            pool.iota(xn[:, half_b, DIM:ROWW].rearrange("i b o -> i (b o)").bitcast(I32),
                                      pattern=[[2 * N, B // 2]], base=2 * N * (B // 2) * p + k, channel_multiplier=2
                                      ).then_inc(q_id, 1)
                            pool.wait_ge(q_id, 2 * k + p + 1)
                            if k == 0 and p == 0:
                                pool.wait_ge(e_pos, 2)
                            for b in range(B)[half_b]:
                                if k == 0:
                                    pool.wait_ge(e_xn, b + 1)
                                pool.indirect_dma_start(
                                    xs_scr, bass.IndirectOffsetOnAxis(ap=pos[k][:, b:b + 1].bitcast(mybir.dt.uint32), axis=0),
                                    xn[:, b, :], None).then_inc(q_sc[k][p], 16)
                    for p in range(2):
                        pool.wait_ge(q_sc[1][p], 8 * B)

                @block.scalar
                def _(act):
                    act.wait_ge(e_ve, 1)
                    act.activation(rstd[:], veps[:], ACT.Sqrt).then_inc(s_sq, 1)
                    act.wait_ge(e_low, 1)
                    act.activation(R["exp"][:], R["low"][:], ACT.Exp).then_inc(s_exp, 1)
                    act.wait_ge(e_sc, 1)
                    act.wait_ge(i_w[0], 32)
                    w = raw[:, 0].rearrange("p j c f -> p (j c f)")
                    act.activation(w, w, ACT.Copy, scale=sc[:, 0:1]).then_inc(s_p, 1)
                    act.wait_ge(s_p, 1)
                    act.activation(GH[:, 0].rearrange("p j c f -> p (j c f)"), w, ACT.Copy).then_inc(s_h, 1)

                    for e in range(1, E + 1):
                        if e < E:
                            act.wait_ge(i_w[e % WB], 32 * (e // WB + 1))
                            act.activation(GH[:, e].rearrange("p j c f -> p (j c f)"),
                                           raw[:, e % WB].rearrange("p j c f -> p (j c f)"), ACT.Copy,
                                           scale=sc[:, e:e + 1]).then_inc(s_h, 1)
                        d = e - 1
                        act.wait_ge(i_d[d % 2], 16 * (d // 2 + 1))
                        act.activation(DH[:, d].rearrange("p f d -> p (f d)"),
                                       draw[:, d % 2].rearrange("p f d -> p (f d)"), ACT.Copy).then_inc(s_d, 1)

                @block.tensor
                def _(pe):
                    pe.wait_ge(q_tri, 2)
                    pe.matmul(bN[:, 0:E], ones[:], sq[:], start=True, stop=True).then_inc(t_n, 1)
                    pe.wait_ge(i_sm, 32)
                    for j in range(2):
                        mm = pe.transpose(bC[:, 32 * j:32 * j + E * FC], braw[:, j, :], ident[0:E * FC, 0:E * FC])
                    mm.then_inc(t_rw, 1)
                    pe.wait_ge(e_sel, 1)
                    flat = R["both"][:].rearrange("i b e -> i (b e)")
                    pe.matmul(bR[0:N, 0:B * E], upper[:], flat, start=True, stop=True)
                    pe.matmul(bR[0:N, 256:256 + B * E], ones[0:N, 0:N], flat, start=True, stop=True).then_inc(t_rank, 1)

                @block.vector
                def _(dve):
                    n_chain = [0]

                    def link(ins):
                        n_chain[0] += 1
                        ins.then_inc(e_r, 1)
                        dve.wait_ge(e_r, n_chain[0])

                    dve.tensor_scalar(veps[:], mv2[:, :, 1], LN_EPS, None, ALU.add).then_inc(e_ve, 1)
                    dve.wait_ge(t_n, 1)
                    dve.tensor_scalar(half[:].bitcast(I32), bN[:, 0:E].bitcast(I32), 0x7F000000, 1,
                                      ALU.bitwise_and, ALU.logical_shift_right).then_inc(e_ch, 1)
                    dve.wait_ge(e_ch, 1)
                    dve.tensor_scalar(unit[:], half[:], 2.0 ** -124, 2.0 ** 64 / WS, ALU.max, ALU.mult
                                      ).then_inc(e_ch, 1)
                    dve.wait_ge(e_ch, 2)
                    dve.reciprocal(sc[:], unit[:]).then_inc(e_sc, 1)
                    dve.tensor_scalar(inv[:], unit[:], 1.0 / XS, None, ALU.mult).then_inc(e_ch, 1)
                    dve.wait_ge(s_sq, 1)
                    dve.reciprocal(rstd[:], rstd[:]).then_inc(e_rs, 1)
                    dve.wait_ge(q_iota, 2)
                    link(dve.tensor_copy(R["tie"], tie_i[:]))
                    link(dve.tensor_copy(start, start_i[:]))
                    dve.wait_ge(e_rs, 1)
                    wide = lambda t: t[:].unsqueeze(2).to_broadcast([N, B, E])
                    logits = R["logit"][:]
                    link(dve.tensor_tensor(logits, routed[:], wide(rstd), ALU.mult))
                    link(dve.tensor_reduce(r["m"][:], logits, AX.X, ALU.max))
                    dve.tensor_tensor(R["low"][:], logits, wide(r["m"]), ALU.subtract).then_inc(e_low, 1)
                    dve.wait_ge(s_exp, 1)
                    link(dve.tensor_reduce(r["sum"][:], R["exp"][:], AX.X, ALU.add))
                    for k, src in ((1, R["exp"]), (2, R["rest"])):
                        mk, tk, sel = r[f"m{k}"], r[f"t{k}"], R[f"sel{k}"]
                        link(dve.tensor_reduce(mk[:], src[:], AX.X, ALU.max))
                        link(dve.tensor_tensor(R["eq"][:], src[:], wide(mk), ALU.is_equal))
                        link(dve.tensor_tensor(R["score"][:], R["eq"][:], R["tie"], ALU.mult))
                        link(dve.tensor_reduce(tk[:], R["score"][:], AX.X, ALU.max))
                        link(dve.tensor_tensor(sel[:], R["score"][:], wide(tk), ALU.is_equal))
                        if k == 1:
                            link(dve.scalar_tensor_tensor(out=R["rest"][:], in0=sel[:], scalar=-4.0, in1=src[:],
                                                          op0=ALU.mult, op1=ALU.add))
                    dve.tensor_tensor(R["both"][:], R["sel1"][:], R["sel2"][:], ALU.add).then_inc(e_sel, 1)
                    dve.wait_ge(t_rank, 1)
                    rank = bR[0:N, 0:B * E].rearrange("i (b e) -> i b e", e=E)
                    total = bR[0:N, 256:256 + B * E].rearrange("i (b e) -> i b e", e=E)
                    link(dve.tensor_copy(R["a0"][:], total))
                    a, b_ = R["a0"], R["a1"]
                    sh = 1
                    while sh < B:
                        link(dve.tensor_tensor(b_[:, sh:B, :], a[:, sh:B, :], a[:, 0:B - sh, :], ALU.add))
                        link(dve.tensor_copy(b_[:, 0:sh, :], a[:, 0:sh, :]))
                        a, b_, sh = b_, a, 2 * sh
                    link(dve.tensor_scalar(ci[:], a[:, B - 1, :], TS - 1.0, None, ALU.add))
                    link(dve.tensor_scalar(ca[:], ci[:], -TS, None, ALU.bitwise_and))
                    link(dve.tensor_copy(c["pad"][:], ca[:]))
                    link(dve.tensor_copy(c["e0"][:], c["pad"][:]))
                    x0, x1, sh = c["e0"], c["e1"], 1
                    while sh < E:
                        link(dve.tensor_tensor(x1[:, sh:E], x0[:, sh:E], x0[:, 0:E - sh], ALU.add))
                        link(dve.tensor_copy(x1[:, 0:sh], x0[:, 0:sh]))
                        x0, x1, sh = x1, x0, 2 * sh
                    link(dve.tensor_tensor(c["base"][:], x0[:], c["pad"][:], ALU.subtract))
                    link(dve.tensor_tensor(b_[:], a[:], total, ALU.subtract))
                    link(dve.tensor_tensor(a[:], b_[:], rank, ALU.add))
                    link(dve.tensor_tensor(R["pos"][:], a[:], c["base"][:].unsqueeze(1).to_broadcast([N, B, E]),
                                           ALU.add))
                    for k in range(2):
                        link(dve.tensor_tensor(R[f"pick{k + 1}"][:], R["pos"][:], R[f"sel{k + 1}"][:], ALU.mult))
                        link(dve.tensor_reduce(r[f"f{k + 1}"][:], R[f"pick{k + 1}"][:], AX.X, ALU.add))
                        dve.tensor_copy(pos[k][:], r[f"f{k + 1}"][:]).then_inc(e_pos, 1)
                    for b in range(B):
                        dve.tensor_scalar(xn[:, b, 0:DIM], X[:, b, :], mv2[:, b, 0:1], rstd[:, b:b + 1],
                                          ALU.subtract, ALU.mult).then_inc(e_xn, 1)
                    link(dve.tensor_tensor(past[:], start, x0[0:1, :].unsqueeze(1).to_broadcast([1, NT, E]),
                                           ALU.is_ge))
                    link(dve.tensor_reduce(nexp[:], past[:], AX.X, ALU.add))
                    link(dve.tensor_scalar(tile_e[:], nexp[:], float(E - 1), None, ALU.min))
                    link(dve.reciprocal(r["rsum"][:], r["sum"][:]))
                    link(dve.tensor_tensor(r["p1"][:], r["m1"][:], r["rsum"][:], ALU.mult))
                    link(dve.tensor_tensor(r["p2"][:], r["m2"][:], r["rsum"][:], ALU.mult))
                    link(dve.scalar_tensor_tensor(out=r["den"][:], in0=r["p1"][:], scalar=1e-9, in1=r["p2"][:],
                                                  op0=ALU.add, op1=ALU.add))
                    link(dve.reciprocal(r["rden"][:], r["den"][:]))
                    for k in range(2):
                        link(dve.scalar_tensor_tensor(out=tw[:, k, :], in0=r[f"p{k + 1}"][:], scalar=tg[0:N, 1:2],
                                                      in1=r["rden"][:], op0=ALU.mult, op1=ALU.mult))

                    dve.wait_ge(t_rw, 1)
                    dve.tensor_copy(gb[:], bC[:, 0:E * FC]).then_inc(e_rw, 1)
                    dve.scalar_tensor_tensor(out=ub[:].rearrange("p (e f) -> p e f", e=E),
                                             in0=bC[:, 32:32 + E * FC].rearrange("p (e f) -> p e f", e=E), scalar=XS,
                                             in1=sc[:].unsqueeze(2).to_broadcast([128, E, FC]),
                                             op0=ALU.mult, op1=ALU.mult).then_inc(e_rw, 1)
                    dve.wait_ge(e_xn, B)

                    for e in range(1, E + 1):
                        if e < E:
                            dve.wait_ge(s_h, e + 1)
                            dve.scalar_tensor_tensor(
                                out=GL[:, e].rearrange("p j c f -> p (j c f)"),
                                in0=raw[:, e % WB].rearrange("p j c f -> p (j c f)"), scalar=sc[:, e:e + 1],
                                in1=GH[:, e].rearrange("p j c f -> p (j c f)"),
                                op0=ALU.mult, op1=ALU.subtract).then_inc(e_l, 1)
                        if e > 1:
                            d = e - 1
                            dve.wait_ge(s_d, d + 1)
                            dve.tensor_tensor(DL[:, d].rearrange("p f d -> p (f d)"),
                                              draw[:, d % 2].rearrange("p f d -> p (f d)"),
                                              f32(DH[:, d].rearrange("p f d -> p (f d)")),
                                              ALU.subtract).then_inc(e_dl, 1)

        tiled = stack.enter_context(ExitStack())

        def tile_sb(name, shape, dt):
            return tiled.enter_context(nc.sbuf_tensor(name, shape, dt))

        UN = 4
        dbB = tile_sb("dbB", [128, E, DIM], F32)
        i_db = sem("down_bias_in")
        xH, xL = tile_sb("xH", [128, 2, DC, TS], F16), tile_sb("xL", [128, 2, DC, TS], F16)
        sg, hf = tile_sb("sg", [128, FC, TS], F32), tile_sb("hf", [128, FC, TS], F32)
        hH, hL = tile_sb("hH", [128, 2, FC, TS], F32R), tile_sb("hL", [128, 2, FC, TS], F32R)
        where = tile_sb("where", [128, UN, TH], I32)
        v_id = sem("dve_where")
        ys = tile_sb("ys", [128, 2, TH, DIM], F32)
        y_out = [sem(f"tile_out{u}") for u in range(2)]
        k_T, k_GU, k_D = sem("pe_tileT"), sem("pe_gate_up"), sem("pe_down")
        a_x, a_s, a_h = sem("act_tile_x"), sem("act_silu"), sem("act_h")
        v_x, v_h, v_l, v_y = sem("dve_tile_x"), sem("dve_h"), sem("dve_hlow"), sem("dve_y")
        FB = 512 // TS
        FQ = FC // FB
        bT, bG, bU, bY = banks[0:2], banks[2:4], banks[4:6], [misc[:, 0:512], misc[:, 512:1024]]

        def tiles(eng, step):
            count = (NT - UN) // UN
            for n in range(UN):
                step(0, n)
            with eng.Fori(1, 1 + count) as i:
                for c in range(UN):
                    step(i, c)
            for n in range(UN * (1 + count), NT + 2):
                step(0, n)

        def has(i, c, back):
            return not isinstance(i, int) or 0 <= UN * i + c - back < NT

        def at(i, c):
            return UN * i + c, UN // 2 * i + c // 2, c % 2

        def wait(eng, s, value):
            if not isinstance(value, int) or value > 0:
                eng.wait_ge(s, value)

        def expert(eng, t):
            return eng.value_load(tile_e[0:1, bass.ds(t, 1)], min_val=0, max_val=E - 1)

        def two_experts(eng, i, c, kept):
            one = expert(eng, UN * i + c - 1) if has(i, c, 1) else None
            two = kept.get((id(i) if not isinstance(i, int) else 0, c - 2))
            if two is None and has(i, c, 2):
                two = expert(eng, UN * i + c - 2)
            kept[(id(i) if not isinstance(i, int) else 0, c - 1)] = one
            return one, two

        with nc.Block() as block:
            @block.sync
            def _(sp):
                def step(i, c):
                    if has(i, c, 0) and not (isinstance(i, int) and UN * i + c < 2):
                        t, h, u = at(i, c)
                        wait(sp, k_T, t - 1)
                        wait(sp, v_id, t - 1)
                        sp.dma_start(xt[:, u], xs_scr[bass.ds(TS * t, TS), :].rearrange("(h p) w -> p h w", p=128)
                                     ).then_inc(l_x[u], 16)

                sp.dma_start(dbB[:], down_b.unsqueeze(0).to_broadcast([128, E, DIM])).then_inc(i_db, 16)
                tiles(sp, step)

            @block.gpsimd
            def _(pool):
                for t in range(NT):
                    u = t % 2
                    pool.wait_ge(v_y, t + 1)
                    for k in range(TH):
                        pool.indirect_dma_start(
                            y_scr, bass.IndirectOffsetOnAxis(ap=where[:, t % UN, k:k + 1].bitcast(mybir.dt.uint32), axis=0),
                            ys[:, u, k, :], None).then_inc(y_out[u], 16)
                for u in range(2):
                    pool.wait_ge(y_out[u], 16 * TH * ((NT + 1 - u) // 2))

            @block.scalar
            def _(act):
                def step(i, c):
                    if has(i, c, 1):
                        e = expert(act, UN * i + c - 1)
                    if has(i, c, 0):
                        t, h, u = at(i, c)
                        act.wait_ge(k_T, t + 1)
                        wait(act, k_GU, FQ * (t - 1))
                        act.activation(xH[:, u], bT[u][:, 0:DC * TS].rearrange("p (c s) -> p c s", c=DC), ACT.Copy,
                                       scale=XS).then_inc(a_x, 1)
                    if has(i, c, 1):
                        t, h, u = at(i, c - 1)
                        for f in range(FC):
                            act.wait_ge(k_GU, FQ * t + f // FB + 1)
                            wait(act, v_h, FC * (t - 1) + f + 1)
                            act.activation(sg[:, f, :], bG[f // FB][:, TS * (f % FB):TS * (f % FB + 1)], ACT.Silu,
                                           bias=gb[:, bass.ds(e * FC + f, 1)], scale=inv[:, bass.ds(e, 1)]
                                           ).then_inc(a_s, 1)
                        act.wait_ge(v_h, FC * (t + 1))
                        wait(act, k_D, t - 1)
                        act.activation(hH[:, u], hf[:], ACT.Copy).then_inc(a_h, 1)

                tiles(act, step)

            @block.tensor
            def _(pe):
                kept = {}

                def step(i, c):
                    e1, e2 = two_experts(pe, i, c, kept)
                    if has(i, c, 0):
                        t, h, u = at(i, c)
                        pe.wait_ge(l_x[u], 16 * (h + 1))
                        wait(pe, v_x, t - 1)
                        for s in range(TH):
                            for k in range(DC):
                                mm = pe.transpose(bT[u][:, TS * k + 128 * s:TS * k + 128 * (s + 1)],
                                                  xt[:, u, s, 128 * k:128 * (k + 1)], ident[:])
                        mm.then_inc(k_T, 1)
                    if has(i, c, 1):
                        t, h, u = at(i, c - 1)
                        pe.wait_ge(v_x, t + 1)
                        for q in range(FQ):
                            wait(pe, a_s, FC * (t - 1) + FB * (q + 1))
                            wait(pe, v_h, FC * (t - 1) + FB * (q + 1))
                            for j, bank in enumerate((bG[q], bU[q])):
                                for f in range(FB * q, FB * (q + 1)):
                                    for n, (W, x) in enumerate(((GH, xH), (GH, xL), (GL, xH))):
                                        for k in range(DC):
                                            w = W[:, bass.ds(e1, 1), j, k, 128 * f:128 * (f + 1)]
                                            mm = pe.matmul(bank[:, TS * (f % FB):TS * (f % FB + 1)],
                                                           w.rearrange("p o f -> p (o f)"), x[:, u, k, :],
                                                           start=(n == 0 and k == 0), stop=(n == 2 and k == DC - 1))
                            mm.then_inc(k_GU, 1)
                    if has(i, c, 2):
                        t, h, u = at(i, c - 2)
                        pe.wait_ge(v_l, t + 1)
                        wait(pe, v_y, t - 1)
                        for s in range(TH):
                            for n, (W, x) in enumerate(((DH, hH), (DL, hH), (DH, hL))):
                                for f in range(FC):
                                    mm = pe.matmul(bY[u][:, DIM * s:DIM * (s + 1)], x[:, u, f, 128 * s:128 * (s + 1)],
                                                   W[:, bass.ds(e2, 1), f, :].rearrange("p o d -> p (o d)"),
                                                   start=(n == 0 and f == 0), stop=(n == 2 and f == FC - 1))
                        mm.then_inc(k_D, 1)

                tiles(pe, step)

            @block.vector
            def _(dve):
                kept = {}

                def step(i, c):
                    e1, e2 = two_experts(dve, i, c, kept)
                    if has(i, c, 0):
                        t, h, u = at(i, c)
                        dve.wait_ge(l_x[u], 16 * (h + 1))
                        wait(dve, y_out[u], 16 * TH * (h - 1))
                        dve.tensor_copy(where[:, c % UN].unsqueeze(2), xt[:, u, :, DIM:ROWW].bitcast(I32)
                                        ).then_inc(v_id, 1)
                    if has(i, c, 0):
                        t, h, u = at(i, c)
                        dve.wait_ge(a_x, t + 1)
                        dve.scalar_tensor_tensor(out=xL[:, u], in0=bT[u][:, 0:DC * TS].rearrange("p (c s) -> p c s", c=DC),
                                                 scalar=XS, in1=xH[:, u], op0=ALU.mult, op1=ALU.subtract
                                                 ).then_inc(v_x, 1)
                    if has(i, c, 1):
                        t, h, u = at(i, c - 1)
                        wait(dve, v_l, t)
                        for f in range(FC):
                            dve.wait_ge(a_s, FC * t + f + 1)
                            dve.scalar_tensor_tensor(out=hf[:, f, :], in0=bU[f // FB][:, TS * (f % FB):TS * (f % FB + 1)],
                                                     scalar=ub[:, bass.ds(e1 * FC + f, 1)], in1=sg[:, f, :],
                                                     op0=ALU.add, op1=ALU.mult).then_inc(v_h, 1)
                        dve.wait_ge(a_h, t + 1)
                        dve.tensor_tensor(hL[:, u], hf[:], f32(hH[:, u]), ALU.subtract).then_inc(v_l, 1)
                    if has(i, c, 2):
                        t, h, u = at(i, c - 2)
                        dve.wait_ge(k_D, t + 1)
                        wait(dve, y_out[u], 16 * TH * h)
                        dve.wait_ge(v_id, t + 1)
                        if isinstance(i, int) and UN * i + c == 2:
                            dve.wait_ge(i_db, 16)
                        dve.scalar_tensor_tensor(out=ys[:, u], in0=bY[u][:, 0:TH * DIM].rearrange("p (h d) -> p h d", h=TH),
                                                 scalar=inv[:, bass.ds(e2, 1)],
                                                 in1=dbB[:, bass.ds(e2, 1), :].to_broadcast([128, TH, DIM]),
                                                 op0=ALU.mult, op1=ALU.add).then_inc(v_y, 1)

                tiles(dve, step)

        tiled.close()
        QL, QO = 2, 4
        POOLED = [b for b in range(B) if b % QO == 1]
        yt = sb("yt", [N, B, 2, DIM], F32)
        y_in = [sem(f"y_in{g}") for g in range(B // QL)]
        v_add, a_w, g_add, s_out = sem("dve_added"), sem("act_weighted"), sem("pool_added"), sem("out_written")
        y_rows = y_scr[0:2 * B * N, :].rearrange("(b i k) d -> i b k d", i=N, k=2)
        out_rows = out.rearrange("b i d -> i b d")

        with nc.Block() as block:
            @block.sync
            def _(sp):
                for g in range(B // QL):
                    sp.dma_start(yt[:, QL * g:QL * (g + 1)], y_rows[:, QL * g:QL * (g + 1)]).then_inc(y_in[g], 16)
                for g in range(B // QO):
                    pooled = sum(b < QO * (g + 1) for b in POOLED)
                    sp.wait_ge(v_add, 2 * (QO * (g + 1) - pooled))
                    sp.wait_ge(g_add, 2 * pooled)
                    sp.dma_start(out_rows[:, QO * g:QO * (g + 1), :], X[:, QO * g:QO * (g + 1), :]).then_inc(s_out, 16)
                sp.wait_ge(s_out, 16 * (B // QO))

            @block.scalar
            def _(act):
                for b in POOLED:
                    act.wait_ge(y_in[b // QL], 16)
                    for k in range(2):
                        act.activation(yt[:, b, k, :], yt[:, b, k, :], ACT.Copy, scale=tw[:, k, b:b + 1]
                                       ).then_inc(a_w, 1)

            @block.gpsimd
            def _(pool):
                n = 0
                for b in POOLED:
                    for k in range(2):
                        pool.wait_ge(a_w, n + k + 1)
                        if k:
                            pool.wait_ge(g_add, n + k)
                        pool.tensor_tensor(X[:, b, :], X[:, b, :], yt[:, b, k, :], ALU.add).then_inc(g_add, 1)
                    n += 2

            @block.vector
            def _(dve):
                n = 0
                for g in range(B // QL):
                    mine = [b for b in range(QL * g, QL * (g + 1)) if b not in POOLED]
                    dve.wait_ge(y_in[g], 16)
                    for k in range(2):
                        for b in mine:
                            if k:
                                dve.wait_ge(v_add, n - len(mine) + 1)
                            dve.scalar_tensor_tensor(out=X[:, b, :], in0=yt[:, b, k, :], scalar=tw[:, k, b:b + 1],
                                                     in1=X[:, b, :], op0=ALU.mult, op1=ALU.add).then_inc(v_add, 1)
                            n += 1
def layer_norm_stats(dve, X, stats, mv, veps, rstd, B, s_st, s_mv, s_ve, s_sq, s_rs):
    for b in range(B):
        dve.bn_stats(stats[:, b, :], X[:, b, :]).then_inc(s_st, 1)
    dve.wait_ge(s_st, B)
    for b in range(B):
        dve.bn_aggr(mv[:, b, :], stats[:, b, :]).then_inc(s_mv, 1)
    dve.wait_ge(s_mv, B)
    dve.tensor_scalar(veps[:], mv[:, :, 1], LN_EPS, None, ALU.add).then_inc(s_ve, 1)
    dve.wait_ge(s_sq, 1)
    dve.reciprocal(rstd[:], rstd[:]).then_inc(s_rs, 1)
    dve.wait_ge(s_rs, 1)


_INS = ["x", "ctx_768", "mask_BxS2_bf1", "g_xattn", "g_ffn", "L0_xattn_Wq", "L0_xattn_Wk", "L0_xattn_Wv",
        "L0_xattn_Wo", "L0_ffn_router_w", "L0_ffn_gate_w", "L0_ffn_gate_b", "L0_ffn_up_w", "L0_ffn_up_b",
        "L0_ffn_down_w", "L0_ffn_down_b"]


def kernel(**inputs):
    import numpy as _np
    import concourse.bacc as _bacc
    from concourse.bass_utils import run_bass_kernel_spmd as _run

    nc = _bacc.Bacc("TRN2", target_bir_lowering=False, num_devices=1)
    arrays, args = {}, []
    for name in _INS:
        a = _np.ascontiguousarray(inputs[name])
        if a.dtype == _np.bool_:
            a = a.view(_np.uint8)
        arrays[f"in_{name}"] = a
        args.append(nc.dram_tensor(f"in_{name}", a.shape, mybir.dt.from_np(a.dtype), kind="ExternalInput").ap())
    out = nc.dram_tensor("out", inputs["x"].shape, F32, kind="ExternalOutput").ap()
    build(nc, *args, out)
    return _run(nc, [arrays], core_ids=[0]).results[0]["out"]
```
